# Optimizing a Trainium2 kernel written in Bass

```python
import numpy as np
import jax
import jax.numpy as jnp

def _softmax(x, axis=-1):
    return jax.nn.softmax(x, axis=axis)

def _gelu(x):
    return jax.nn.gelu(x, approximate=True)

def _silu(x):
    return jax.nn.silu(x)

def _sigmoid(x):
    return jax.nn.sigmoid(x)

def _layernorm(x, axis=-1, eps=1e-05):
    m = jnp.mean(x, axis=axis, keepdims=True)
    v = jnp.var(x, axis=axis, keepdims=True)
    return (x - m) / jnp.sqrt(v + eps)

def _scatter_add(tgt, idx, src, axis=0):
    return tgt.at[idx].add(src)

def _segment_sum(src, seg, n):
    return jax.ops.segment_sum(src, seg, n)
kernel_name = 'mk_xattn_ffn_d1_seqx_r2_30a2c4'

def setup_inputs(seed: int=0):
    np.random.seed(seed)
    _w = jnp.asarray

    def _rec_inputs():
        import jax
        import jax.numpy as jnp
        _rk = jax.random.key(seed)
        x = -0.0002928 + 1 * jax.random.normal(jax.random.fold_in(_rk, 1), (4, 1024, 512), jnp.float32)
        _lenS = 1024 - jax.random.randint(jax.random.fold_in(_rk, 7), (4,), 0, max(1, 1024 // 4) + 1, jnp.int32)
        _lenS2 = 64 - jax.random.randint(jax.random.fold_in(_rk, 8), (4,), 0, max(1, 64 // 4) + 1, jnp.int32)
        _ctx_1024P = jax.random.normal(jax.random.fold_in(_rk, 11), (4, 16, 512), jnp.float32)
        _ctx_1024c = jax.random.dirichlet(jax.random.fold_in(_rk, 511), 0.3 * jnp.ones((16,), jnp.float32), (4, 64))
        _ctx_1024t = jnp.einsum('bsk,bkd->bsd', _ctx_1024c, _ctx_1024P)
        _ctx_1024t = _ctx_1024t * jax.lax.rsqrt(jnp.mean(jnp.square(_ctx_1024t)) + 1e-12) * 0.953939
        ctx_1024 = -1.39393e-06 + 0.999914 * (_ctx_1024t + 0.3 * jax.random.normal(jax.random.fold_in(_rk, 611), (4, 64, 512), jnp.float32))
        _validS = jnp.arange(1024)[None, :] < _lenS[:, None]
        _validS2 = jnp.arange(64)[None, :] < _lenS2[:, None]
        _causal = jnp.tril(jnp.ones((1024, 1024), dtype=bool))
        mask_Bx1xSxS2_ik0 = jnp.where(jnp.broadcast_to(_validS2[:, None, None, :], (4, 1, 1024, 64)), 0, 1).astype(jnp.int32)
        mask_Bx1xS2_bk0 = jnp.logical_not(jnp.broadcast_to(_validS2[:, None, :], (4, 1, 64)))
        return (x, ctx_1024, mask_Bx1xSxS2_ik0, mask_Bx1xS2_bk0)
    x, ctx_1024, mask_Bx1xSxS2_ik0, mask_Bx1xS2_bk0 = _rec_inputs()

    def _L0_xattn_setup():
        import jax, jax.numpy as jnp
        import numpy as np
        B, NQ, NKV = (2, 1024, 1024)
        QUERY_DIM = 512
        CONTEXT_DIM = 512
        HEADS = 16
        DIM_HEAD = 64
        INNER = HEADS * DIM_HEAD
        SCALE = DIM_HEAD ** (-0.5)
        key = jax.random.key(seed)
        ks = jax.random.split(key, 9)
        x = jax.random.normal(ks[0], (B, NQ, QUERY_DIM), dtype=jnp.float32)
        context = jax.random.normal(ks[1], (B, NKV, CONTEXT_DIM), dtype=jnp.float32)
        tgt_mask = jax.random.randint(ks[2], (B, 1, NQ, NKV), 0, 2, dtype=jnp.int32)
        src_mask = jax.random.randint(ks[3], (B, 1, NKV), 0, 2) > 0
        w = 0.02
        Wq = jax.random.normal(ks[4], (INNER, QUERY_DIM), dtype=jnp.float32) * w
        Wk = jax.random.normal(ks[5], (INNER, CONTEXT_DIM), dtype=jnp.float32) * w
        Wv = jax.random.normal(ks[6], (INNER, CONTEXT_DIM), dtype=jnp.float32) * w
        Wo = jax.random.normal(ks[7], (QUERY_DIM, INNER), dtype=jnp.float32) * w
        bo = jax.random.normal(ks[8], (QUERY_DIM,), dtype=jnp.float32) * w
        return {'x': x, 'context': context, 'tgt_mask': tgt_mask, 'src_mask': src_mask, 'Wq': Wq, 'Wk': Wk, 'Wv': Wv, 'Wo': Wo, 'bo': bo}
    _L0_xattn_all = _L0_xattn_setup()
    _L0_xattn_in = {k: v for k, v in _L0_xattn_all.items() if k in ('Wq', 'Wk', 'Wv', 'Wo', 'bo')}
    del _L0_xattn_all

    def _L0_ffn_setup():
        import jax, jax.numpy as jnp
        import numpy as np
        D_MODEL = 512
        HIDDEN = 2048
        N_ROUTING = 2
        key = jax.random.key(seed)
        ks = jax.random.split(key, 10)
        s = 0.02
        x = jax.random.normal(ks[0], (4, 2048, D_MODEL), dtype=jnp.float32)
        gate_w = jax.random.normal(ks[1], (N_ROUTING, D_MODEL), dtype=jnp.float32) * s
        w1 = jax.random.normal(ks[2], (N_ROUTING, D_MODEL, HIDDEN), dtype=jnp.float32) * s
        b1 = jax.random.normal(ks[3], (N_ROUTING, HIDDEN), dtype=jnp.float32) * s
        w2 = jax.random.normal(ks[4], (N_ROUTING, HIDDEN, D_MODEL), dtype=jnp.float32) * s
        b2 = jax.random.normal(ks[5], (N_ROUTING, D_MODEL), dtype=jnp.float32) * s
        sw1 = jax.random.normal(ks[6], (D_MODEL, HIDDEN), dtype=jnp.float32) * s
        sb1 = jax.random.normal(ks[7], (HIDDEN,), dtype=jnp.float32) * s
        sw2 = jax.random.normal(ks[8], (HIDDEN, D_MODEL), dtype=jnp.float32) * s
        sb2 = jax.random.normal(ks[9], (D_MODEL,), dtype=jnp.float32) * s
        return {'x': x, 'gate_w': gate_w, 'w1': w1, 'b1': b1, 'w2': w2, 'b2': b2, 'sw1': sw1, 'sb1': sb1, 'sw2': sw2, 'sb2': sb2}
    _L0_ffn_all = _L0_ffn_setup()
    _L0_ffn_in = {k: v for k, v in _L0_ffn_all.items() if k in ('gate_w', 'w1', 'b1', 'w2', 'b2', 'sw1', 'sb1', 'sw2', 'sb2')}
    del _L0_ffn_all
    return {'x': x, 'ctx_1024': ctx_1024, 'mask_Bx1xSxS2_ik0': mask_Bx1xSxS2_ik0, 'mask_Bx1xS2_bk0': mask_Bx1xS2_bk0, 'L0_xattn_Wq': _L0_xattn_in['Wq'], 'L0_xattn_Wk': _L0_xattn_in['Wk'], 'L0_xattn_Wv': _L0_xattn_in['Wv'], 'L0_xattn_Wo': _L0_xattn_in['Wo'], 'L0_xattn_bo': _L0_xattn_in['bo'], 'L0_ffn_gate_w': _L0_ffn_in['gate_w'], 'L0_ffn_w1': _L0_ffn_in['w1'], 'L0_ffn_b1': _L0_ffn_in['b1'], 'L0_ffn_w2': _L0_ffn_in['w2'], 'L0_ffn_b2': _L0_ffn_in['b2'], 'L0_ffn_sw1': _L0_ffn_in['sw1'], 'L0_ffn_sb1': _L0_ffn_in['sb1'], 'L0_ffn_sw2': _L0_ffn_in['sw2'], 'L0_ffn_sb2': _L0_ffn_in['sb2']}

def reference(x, ctx_1024, mask_Bx1xSxS2_ik0, mask_Bx1xS2_bk0, L0_xattn_Wq, L0_xattn_Wk, L0_xattn_Wv, L0_xattn_Wo, L0_xattn_bo, L0_ffn_gate_w, L0_ffn_w1, L0_ffn_b1, L0_ffn_w2, L0_ffn_b2, L0_ffn_sw1, L0_ffn_sb1, L0_ffn_sw2, L0_ffn_sb2):
    import jax
    import jax.numpy as jnp

    def _L0_xattn_ref(x, context, tgt_mask, src_mask, Wq, Wk, Wv, Wo, bo):
        import jax, jax.numpy as jnp
        import numpy as np
        B, NQ, NKV = (2, 1024, 1024)
        QUERY_DIM = 512
        CONTEXT_DIM = 512
        HEADS = 16
        DIM_HEAD = 64
        INNER = HEADS * DIM_HEAD
        SCALE = DIM_HEAD ** (-0.5)
        b, nq, _ = x.shape
        nkv = context.shape[1]
        q = jnp.einsum('bnc,ec->bne', x, Wq).reshape(b, nq, HEADS, DIM_HEAD).transpose(0, 2, 1, 3)
        k = jnp.einsum('bmc,ec->bme', context, Wk).reshape(b, nkv, HEADS, DIM_HEAD).transpose(0, 2, 1, 3)
        v = jnp.einsum('bmc,ec->bme', context, Wv).reshape(b, nkv, HEADS, DIM_HEAD).transpose(0, 2, 1, 3)
        sim = jnp.einsum('bhid,bhjd->bhij', q, k) * SCALE
        neg = -jnp.finfo(sim.dtype).max
        sim = jnp.where(tgt_mask == 0, neg, sim)
        sim = jnp.where(src_mask[:, None, :], sim, neg)
        attn = jax.nn.softmax(sim, axis=-1)
        out = jnp.einsum('bhij,bhjd->bhid', attn, v)
        out = out.transpose(0, 2, 1, 3).reshape(b, nq, INNER)
        return jnp.einsum('bne,oe->bno', out, Wo) + bo

    def _L0_ffn_ref(x, gate_w, w1, b1, w2, b2, sw1, sb1, sw2, sb2):
        import jax, jax.numpy as jnp
        import numpy as np
        D_MODEL = 512
        HIDDEN = 2048
        N_ROUTING = 2
        B, S, D = x.shape
        xf = x.reshape(-1, D)
        gate_scores = xf @ gate_w.T
        gate_probs = jax.nn.softmax(gate_scores, axis=-1)
        top1 = jnp.argmax(gate_probs, axis=-1)
        one_hot = jax.nn.one_hot(top1, N_ROUTING, dtype=xf.dtype)
        masked = xf[None, :, :] * one_hot.T[:, :, None]
        h = jax.nn.relu(jnp.einsum('end,edh->enh', masked, w1) + b1[:, None, :])
        expert_out = jnp.einsum('enh,ehd->end', h, w2) + b2[:, None, :]
        routing_output = expert_out.sum(axis=0)
        shared = jax.nn.relu(xf @ sw1 + sb1) @ sw2 + sb2
        return (routing_output + shared).reshape(B, S, D)
    x = x + _L0_xattn_ref(_layernorm(x, axis=-1), ctx_1024, mask_Bx1xSxS2_ik0, mask_Bx1xS2_bk0, L0_xattn_Wq, L0_xattn_Wk, L0_xattn_Wv, L0_xattn_Wo, L0_xattn_bo)
    x = x + _L0_ffn_ref(_layernorm(x, axis=-1), L0_ffn_gate_w, L0_ffn_w1, L0_ffn_b1, L0_ffn_w2, L0_ffn_b2, L0_ffn_sw1, L0_ffn_sb1, L0_ffn_sw2, L0_ffn_sb2)
    return x

_drawn_inputs = setup_inputs


def setup_inputs(seed=0):
    import zlib

    import numpy as np

    out = dict(_drawn_inputs(seed))
    spreads = {}
    factors = {'L0_xattn_bo': 2.938, 'L0_ffn_b1': 3.663, 'L0_ffn_sb1': 4.927, 'L0_ffn_sb2': 3.143}
    for name, (base, spread) in spreads.items():
        noise = np.random.default_rng([zlib.crc32(name.encode()), seed]).standard_normal(out[name].shape)
        drawn = base * np.exp(spread * noise) if base else spread * noise
        out[name] = jnp.asarray(drawn.astype(out[name].dtype))
    for name, factor in factors.items():
        out[name] = (out[name] * factor).astype(out[name].dtype)
    return out
```

```python
from contextlib import ExitStack

import concourse.bass as bass
from concourse import mybir

F32 = mybir.dt.float32
F16 = mybir.dt.float16
I32 = mybir.dt.int32
U8 = mybir.dt.uint8
ALU = mybir.AluOpType
ACT = mybir.ActivationFunctionType
AX = mybir.AxisListType
RADD = bass.bass_isa.ReduceOp.max

P = 128
BATCH, SEQ, DM = 4, 1024, 512
KEYS, HEADS, DH = 64, 16, 64
INNER = HEADS * DH
HID = 2048
ROWS = BATCH * SEQ
KC = DM // P
PAIRS = HEADS // 2
HC = HID // P
HK = HEADS * KEYS
SUB = ROWS // P
TOK = 256
TILES = ROWS // TOK
SCALE = DH ** -0.5
NEG = float(3.4028234663852886e38)
EPS = 1e-5
LN_SCALE = 2.0 ** 11
P_SCALE = 2.0 ** 15
TIE = 2.0 ** -25
EXP_FIELD = 0x7F800000
MANT = 1 << 23


def shift(g, u, d, n):
    return g + (u + d) // n, (u + d) % n


def live(g, u, n, count):
    return not isinstance(g, int) or 0 <= n * g + u < count


def at_least(eng, sem, value):
    if not isinstance(value, int) or value > 0:
        eng.wait_ge(sem, value)


def groups(eng, n, body, peel_last=1):
    for g in (-1, 0, 1):
        body(g)
    with eng.Fori(2, n - peel_last) as g:
        body(g)
    for g in range(n - peel_last, n + 1):
        body(g)


def xattn_ffn(nc, x, ctxT, tgt, src, wq, wkT, wvT, woT, bo, gate_w, w1, b1, w2, b2, sw1, sb1, sw2, sb2, out):
    x1_d = nc.dram_tensor("x1_scratch", (ROWS, DM), F32, kind="Internal").ap()
    z_d = nc.dram_tensor("z_scratch", (ROWS, DM), F32, kind="Internal").ap()

    with ExitStack() as ctx:
        def sem(name):
            return ctx.enter_context(nc.semaphore(name))

        def sb(name, shape, dt=F32, where=ctx):
            return where.enter_context(nc.sbuf_tensor(name, shape, dt))

        def ps(name, shape, where):
            return where.enter_context(nc.psum_tensor(name, shape, F32))

        ident = sb("ident", [P, P])
        sc = sb("sc", [P, 48])
        expert1 = sb("expert1", [P, SUB])
        expert0 = sb("expert0", [P, SUB])
        AWQ, AWO, AK, AV, BND, EBITS, SM, IM, SV, IV, INV_SIM, INV_OUT = range(12)

        def scale_of(link, eng, bound, s, inv):
            n = bound.shape[1]
            e = sc[:, EBITS + 24:EBITS + 24 + n].bitcast(I32)
            link(eng.tensor_scalar(bound, bound, 2.0 ** -90, 2.0 ** 90, ALU.max, ALU.min))
            link(eng.tensor_scalar(e, bound.bitcast(I32), EXP_FIELD, None, ALU.bitwise_and))
            link(eng.tensor_scalar(s.bitcast(I32), e, -1.0, float(268 * MANT), ALU.mult, ALU.add))
            link(eng.tensor_scalar(inv.bitcast(I32), e, float(-14 * MANT), None, ALU.add))

        with ExitStack() as at:
            fmh = sb("fmh", [P, KC, BATCH, HK], F16, at)
            fml = sb("fml", [P, KC, BATCH, HK], F16, at)
            fvh = sb("fvh", [P, BATCH, PAIRS, DM], F16, at)
            fvl = sb("fvl", [P, BATCH, PAIRS, DM], F16, at)
            with ExitStack() as pro:
                slot0 = sb("slot0", [P, 4096], F32, pro)
                slot1 = sb("slot1", [P, 4096], F32, pro)
                kd = sb("kd", [P, PAIRS, BATCH, 2, KEYS], F32, pro)
                vd = sb("vd", [P, PAIRS, BATCH, 2, KEYS], F32, pro)
                ctxt = sb("ctxt", [P, KC, BATCH * KEYS], F32, pro)
                am = sb("am", [P, 4], F32, pro)
                amr = sb("amr", [P, 4], F32, pro)
                pk = [ps(f"pk{n}", [P, 512], pro) for n in range(4)]
                in_ctx, in_wk, in_wv, in_wq, in_wo = (pro.enter_context(nc.semaphore(n)) for n in ("in_ctx", "in_wk", "in_wv", "in_wq", "in_wo"))
                zeroed = pro.enter_context(nc.semaphore("zeroed"))
                kv_done = pro.enter_context(nc.semaphore("kv_done"))
                kv_out = pro.enter_context(nc.semaphore("kv_out"))
                amaxed = pro.enter_context(nc.semaphore("amaxed"))
                reduced = pro.enter_context(nc.semaphore("reduced"))
                f_done = pro.enter_context(nc.semaphore("f_done"))
                f_hi = pro.enter_context(nc.semaphore("f_hi"))
                f_lo = pro.enter_context(nc.semaphore("f_lo"))
                dstep = pro.enter_context(nc.semaphore("dstep_p"))
                idst = pro.enter_context(nc.semaphore("idst"))
                wk_v = slot0[:, :].rearrange("p (k e) -> p k e", k=KC)
                wv_v = slot1[:, :].rearrange("p (k e) -> p k e", k=KC)
                wq_v = slot0[:, :].rearrange("p (q c) -> p q c", q=PAIRS)
                wo_v = slot1[:, :].rearrange("p (q c) -> p q c", q=PAIRS)
                NF = KC * PAIRS + BATCH * PAIRS

                with nc.Block() as block:
                    @block.sync
                    def _(sp):
                        sp.dma_start(ctxt[:, :, :], ctxT.rearrange("(k p) n -> p k n", p=P)).then_inc(in_ctx, 16)
                        sp.dma_start(wk_v, wkT.rearrange("(k p) n -> p k n", p=P)).then_inc(in_wk, 16)
                        sp.dma_start(wv_v, wvT.rearrange("(k p) n -> p k n", p=P)).then_inc(in_wv, 16)
                        sp.wait_ge(kv_done, PAIRS)
                        sp.dma_start(wq_v, wq.rearrange("(q p) n -> p q n", p=P)).then_inc(in_wq, 16)
                        sp.wait_ge(kv_done, 2 * PAIRS)
                        sp.dma_start(wo_v, woT.rearrange("(q p) n -> p q n", p=P)).then_inc(in_wo, 16)

                    @block.gpsimd
                    def _(pool):
                        pool.memset(ident[:, :], 0.0).then_inc(idst, 1)
                        pool.wait_ge(idst, 1)
                        pool.affine_select(out=ident[:, :], in_=ident[:, :], compare_op=ALU.not_equal, fill=1.0,
                                           base=0, pattern=[[-1, P]], channel_multiplier=1).then_inc(idst, 1)
                        pool.memset(kd[:, :, :, :, :], 0.0).then_inc(zeroed, 1)
                        pool.memset(vd[:, :, :, :, :], 0.0).then_inc(zeroed, 1)
                        pool.wait_ge(amaxed, 4)
                        pool.partition_all_reduce(amr[:, :], am[:, :], P, RADD).then_inc(reduced, 1)

                    @block.tensor
                    def _(pe):
                        pe.wait_ge(in_ctx, 16)
                        n = 0
                        for w, s in ((wk_v, in_wk), (wv_v, in_wv)):
                            pe.wait_ge(s, 16)
                            for q in range(PAIRS):
                                if n >= 4:
                                    pe.wait_ge(kv_out, n - 3)
                                for k in range(KC):
                                    mm = pe.matmul(pk[n % 4][:, 0:BATCH * KEYS], w[:, k, q * P:(q + 1) * P], ctxt[:, k, :],
                                                   start=(k == 0), stop=(k == KC - 1))
                                mm.then_inc(kv_done, 1)
                                n += 1
                        pe.wait_ge(kv_out, 2 * PAIRS)
                        pe.wait_ge(in_wq, 16)
                        for n in range(NF):
                            if n == KC * PAIRS:
                                pe.wait_ge(in_wo, 16)
                            if n >= 4:
                                pe.wait_ge(f_lo, n - 3)
                            if n < KC * PAIRS:
                                k, q = n // PAIRS, n % PAIRS
                                mm = pe.matmul(pk[n % 4][:, :], wq_v[:, q, k * P:(k + 1) * P],
                                               kd[:, q, :, :, :].rearrange("p b h k -> p (b h k)"), start=True, stop=True)
                            else:
                                b, q = (n - KC * PAIRS) // PAIRS, n % PAIRS
                                mm = pe.matmul(pk[n % 4][:, :], vd[:, q, b, :, :].rearrange("p h k -> p (h k)"),
                                               wo_v[:, q, :], start=True, stop=True)
                            mm.then_inc(f_done, 1)

                    def f_dst(n, m, v):
                        if n < KC * PAIRS:
                            k, q = n // PAIRS, n % PAIRS
                            return m[:, k, :, q * P:(q + 1) * P]
                        b, q = (n - KC * PAIRS) // PAIRS, n % PAIRS
                        return v[:, b, q, :]

                    def f_src(n):
                        s = pk[n % 4][:, :]
                        return s.rearrange("p (b n) -> p b n", b=BATCH) if n < KC * PAIRS else s

                    @block.scalar
                    def _(act):
                        act.wait_ge(dstep, 14)
                        for n in range(NF):
                            act.wait_ge(f_done, n + 1)
                            s = SM if n < KC * PAIRS else SV
                            act.activation(f_dst(n, fmh, fvh), f_src(n), ACT.Copy, scale=sc[:, s:s + 1]).then_inc(f_hi, 1)

                    @block.vector
                    def _(dve):
                        dve.wait_ge(zeroed, 2)
                        for n in range(2 * PAIRS):
                            q, t = n % PAIRS, (kd if n < PAIRS else vd)
                            dve.wait_ge(kv_done, n + 1)
                            v = pk[n % 4][:, 0:BATCH * KEYS].rearrange("p (b k) -> p b k", b=BATCH)
                            dve.tensor_copy(t[0:64, q, :, 0, :], v[0:64])
                            dve.tensor_copy(t[64:128, q, :, 1, :], v[64:128]).then_inc(kv_out, 1)
                        dve.wait_ge(kv_out, 2 * PAIRS)
                        for c, (t, s) in enumerate(((slot0[:, :], in_wq), (slot1[:, :], in_wo),
                                                    (kd[:, :, :, :, :], None), (vd[:, :, :, :, :], None))):
                            if s is not None:
                                dve.wait_ge(s, 16)
                            dve.tensor_reduce(am[:, c:c + 1], t, AX.XYZW if len(t.shape) > 2 else AX.X, ALU.max, apply_absolute_value=True).then_inc(amaxed, 1)
                        dve.wait_ge(reduced, 1)
                        steps = [0]

                        def link(ins):
                            steps[0] += 1
                            ins.then_inc(dstep, 1)
                            dve.wait_ge(dstep, steps[0])

                        link(dve.tensor_scalar(sc[:, SM:SM + 1], amr[:, 2:3], amr[:, 0:1], float(DH), ALU.mult, ALU.mult))
                        scale_of(link, dve, sc[:, SM:SM + 1], sc[:, SM:SM + 1], sc[:, IM:IM + 1])
                        link(dve.tensor_scalar(sc[:, SV:SV + 1], amr[:, 3:4], amr[:, 1:2], float(DH), ALU.mult, ALU.mult))
                        scale_of(link, dve, sc[:, SV:SV + 1], sc[:, SV:SV + 1], sc[:, IV:IV + 1])
                        link(dve.tensor_scalar(sc[:, INV_SIM:INV_SIM + 1], sc[:, IM:IM + 1], SCALE / LN_SCALE, None, ALU.mult))
                        link(dve.tensor_scalar(sc[:, INV_OUT:INV_OUT + 1], sc[:, IV:IV + 1], 1.0 / P_SCALE, None, ALU.mult))
                        link(dve.tensor_copy(sc[:, 40:41], sc[:, INV_OUT:INV_OUT + 1]))
                        link(dve.tensor_copy(sc[:, 41:42], sc[:, INV_OUT:INV_OUT + 1]))
                        for n in range(NF):
                            dve.wait_ge(f_hi, n + 1)
                            s = SM if n < KC * PAIRS else SV
                            dve.scalar_tensor_tensor(out=f_dst(n, fml, fvl), in0=f_src(n), scalar=sc[:, s:s + 1],
                                                     in1=f_dst(n, fmh, fvh), op0=ALU.mult, op1=ALU.subtract).then_inc(f_lo, 1)

            with ExitStack() as a:
                N = 4
                S = {}

                def sems(*names):
                    for n in names:
                        S[n] = a.enter_context(nc.semaphore("a_" + n))

                sems("const_in", "src_neg", "stats", "rs", "xn", "xT", "xTh", "xTl", "sim", "keep", "neg", "smask", "mx", "sub", "exp",
                     "sum", "sum2", "rcp", "half_set", "prob", "pT", "pTh", "pTl", "att", "xr_bo", "x1", "stats2", "rs2", "z", "g0", "g1", "pick1", "pick0",
                     "ve", "ve2", "agg", "agg2")
                for n in ("x_in", "m_in", "r_in", "x1_out", "z_out"):
                    for u in range(N):
                        S[n, u] = a.enter_context(nc.semaphore(f"a_{n}{u}"))
                xb = sb("xb", [P, 4, DM], F32, a)
                xn = sb("xn", [P, 2, DM], F32, a)
                xTh = sb("xTh", [P, 2, KC, P], F16, a)
                xTl = sb("xTl", [P, 2, KC, P], F16, a)
                tg = sb("tg", [P, 4, KEYS], I32, a)
                keep = sb("keep", [P, KEYS], F32, a)
                neg = sb("neg", [P, 2, KEYS], F32, a)
                srcb = sb("srcb", [P, BATCH * KEYS], U8, a)
                srcf = sb("srcf", [P, BATCH * KEYS], F32, a)
                s = sb("s", [P, 2, HEADS, KEYS], F32, a)
                mx = sb("mx", [P, 2, HEADS], F32, a)
                sm = sb("sm", [P, 2, HEADS], F32, a)
                ri = sb("ri", [P, 2, HEADS], F32, a)
                pTh = sb("pTh", [P, PAIRS, P], F16, a)
                pTl = sb("pTl", [P, PAIRS, P], F16, a)
                xr = sb("xr", [P, 4, DM], F32, a)
                x1 = sb("x1", [P, 4, DM], F32, a)
                z = sb("z", [P, 4, DM], F32, a)
                bob = sb("bob", [P, DM], F32, a)
                gw = sb("gw", [P, 2, DM], F32, a)
                junk = sb("junk", [P, 2, DM], F32, a)
                half = sb("half", [P, 1], F32, a)
                eps = sb("eps", [P, 1], F32, a)
                st = sb("st", [P, 2, 6], F32, a)
                mv = sb("mv", [P, 2, 2], F32, a)
                ve = sb("ve", [P, 2, 1], F32, a)
                rs = sb("rs", [P, 2, 1], F32, a)
                st2 = sb("st2", [P, 2, 6], F32, a)
                mv2 = sb("mv2", [P, 2, 2], F32, a)
                ve2 = sb("ve2", [P, 2, 1], F32, a)
                rs2 = sb("rs2", [P, 2, 1], F32, a)
                gg = sb("gg", [P, 2, 2], F32, a)
                pS = [ps(f"pS{n}", [P, HK], a) for n in range(2)]
                pX = ps("pX", [P, DM], a)
                pP = ps("pP", [P, HK], a)
                pO = ps("pO", [P, DM], a)

                def count(g, u):
                    return N * g + u + 1

                def dma_count(g):
                    return 16 * g + 16

                def step(eng, g, u, d, fn):
                    g2, u2 = shift(g, u, d, N)
                    if live(g2, u2, N, SUB):
                        fn(eng, g2, u2)

                def rows(t, g, u):
                    return t[bass.ds((N * g + u) * P, P), :]

                with nc.Block() as block:
                    @block.sync
                    def _(sp):
                        sp.dma_start(srcb[:, :], src.partition_broadcast(P)).then_inc(S["const_in"], 16)
                        sp.dma_start(bob[:, :], bo.partition_broadcast(P)).then_inc(S["const_in"], 16)
                        sp.dma_start(gw[:, :, :].rearrange("p e n -> p (e n)"),
                                     gate_w.rearrange("e n -> (e n)").partition_broadcast(P)).then_inc(S["const_in"], 16)

                        def load_x(e, g, u):
                            at_least(e, S["xn"], count(g, u) - 4)
                            e.dma_start(xb[:, u, :], rows(x, g, u)).then_inc(S["x_in", u], 16)

                        def load_m(e, g, u):
                            at_least(e, S["keep"], count(g, u) - 4)
                            e.dma_start(tg[:, u, :], rows(tgt, g, u)).then_inc(S["m_in", u], 16)

                        def load_r(e, g, u):
                            at_least(e, S["x1"], count(g, u) - 4)
                            e.dma_start(xr[:, u, :], rows(x, g, u)).then_inc(S["r_in", u], 16)

                        def store(e, g, u):
                            e.wait_ge(S["x1"], count(g, u))
                            e.dma_start(rows(x1_d, g, u), x1[:, u, :]).then_inc(S["x1_out", u], 16)
                            e.wait_ge(S["z"], count(g, u))
                            e.dma_start(rows(z_d, g, u), z[:, u, :]).then_inc(S["z_out", u], 16)

                        def body(g):
                            for u in range(N):
                                step(sp, g, u, 6, load_x)
                                step(sp, g, u, 4, load_m)
                                step(sp, g, u, 2, load_r)
                                step(sp, g, u, -2, store)
                        for g in (-2,):
                            for u in (2, 3):
                                step(sp, g, u, 6, load_x)
                        groups(sp, SUB // N, body, peel_last=2)
                        for u in range(N):
                            sp.wait_ge(S["x1_out", u], 16 * SUB // N)
                            sp.wait_ge(S["z_out", u], 16 * SUB // N)

                    @block.tensor
                    def _(pe):
                        def t_x(e, g, u):
                            e.wait_ge(S["xn"], count(g, u))
                            at_least(e, S["xTl"], count(g, u) - 1)
                            for k in range(KC):
                                mm = e.transpose(pX[:, k * P:(k + 1) * P], xn[:, u % 2, k * P:(k + 1) * P], ident[:, :])
                            mm.then_inc(S["xT"], 1)

                        def sim(e, g, u):
                            e.wait_ge(S["xTl"], count(g, u))
                            at_least(e, S["smask"], count(g, u) - 2)
                            b = (N * g + u) // (SUB // BATCH)
                            for h in range(2):
                                n = 0
                                for k in range(KC):
                                    for xt, f in ((xTh, fmh), (xTh, fml), (xTl, fmh)):
                                        mm = e.matmul(pS[u % 2][:, h * 512:(h + 1) * 512], xt[:, u % 2, k, :],
                                                      f[:, k, bass.ds(b, 1), h * 512:(h + 1) * 512],
                                                      start=(n == 0), stop=(n == 3 * KC - 1))
                                        n += 1
                            mm.then_inc(S["sim"], 1)

                        def t_p(e, g, u):
                            e.wait_ge(S["prob"], count(g, u))
                            at_least(e, S["pTl"], count(g, u) - 1)
                            for q in range(PAIRS):
                                mm = e.transpose(pP[:, q * P:(q + 1) * P],
                                                 s[:, u % 2, 2 * q:2 * q + 2, :].rearrange("p h k -> p (h k)"), ident[:, :])
                            mm.then_inc(S["pT"], 1)

                        def attend(e, g, u):
                            e.wait_ge(S["pTl"], count(g, u))
                            at_least(e, S["x1"], count(g, u) - 1)
                            b = (N * g + u) // (SUB // BATCH)
                            n = 0
                            for q in range(PAIRS):
                                for pt, f in ((pTh, fvh), (pTh, fvl), (pTl, fvh)):
                                    mm = e.matmul(pO[:, :], pt[:, q, :], f[:, bass.ds(b, 1), q, :],
                                                  start=(n == 0), stop=(n == 3 * PAIRS - 1))
                                    n += 1
                            mm.then_inc(S["att"], 1)

                        def body(g):
                            for u in range(N):
                                step(pe, g, u, 0, t_p)
                                step(pe, g, u, 2, sim)
                                step(pe, g, u, 3, t_x)
                                step(pe, g, u, 0, attend)
                        groups(pe, SUB // N, body, peel_last=1)

                    @block.scalar
                    def _(act):
                        def hi_x(e, g, u):
                            e.wait_ge(S["xT"], count(g, u))
                            at_least(e, S["sim"], count(g, u) - 2)
                            e.activation(xTh[:, u % 2, :, :], pX[:, :].rearrange("p (k n) -> p k n", k=KC), ACT.Copy, scale=LN_SCALE).then_inc(S["xTh"], 1)

                        def hi_p(e, g, u):
                            e.wait_ge(S["pT"], count(g, u))
                            at_least(e, S["att"], count(g, u) - 1)
                            e.activation(pTh[:, :, :], pP[:, :].rearrange("p (k n) -> p k n", k=PAIRS), ACT.Copy).then_inc(S["pTh"], 1)

                        def exp(e, g, u):
                            e.wait_ge(S["sub"], count(g, u))
                            e.activation(s[:, u % 2, :, :], s[:, u % 2, :, :], ACT.Exp).then_inc(S["exp"], 1)

                        def body(g):
                            for u in range(N):
                                step(act, g, u, 0, hi_p)
                                step(act, g, u, 3, hi_x)
                                step(act, g, u, 2, exp)
                        groups(act, SUB // N, body, peel_last=1)

                    @block.gpsimd
                    def _(pool):
                        pool.memset(half[:, :], -0.5).then_inc(S["half_set"], 1)
                        pool.memset(eps[:, :], EPS).then_inc(S["half_set"], 1)
                        pool.wait_ge(S["const_in"], 48)
                        pool.wait_ge(S["half_set"], 2)

                        def rstd(src_sem, mv, ve, rs, ves, done):
                            def fn(e, g, u):
                                e.wait_ge(src_sem, count(g, u))
                                e.tensor_tensor(ve[:, u % 2, :], mv[:, u % 2, 1:2], eps[:, :], ALU.add).then_inc(ves, 1)
                                e.wait_ge(ves, count(g, u))
                                e.tensor_tensor(rs[:, u % 2, :], ve[:, u % 2, :], half[:, :], ALU.pow).then_inc(done, 1)
                            return fn

                        def sub(e, g, u):
                            e.wait_ge(S["mx"], count(g, u))
                            v = s[:, u % 2, :, :]
                            e.tensor_tensor(v, v, mx[:, u % 2, :].unsqueeze(2).broadcast_to([P, HEADS, KEYS]), ALU.subtract).then_inc(S["sub"], 1)

                        def norm(e, g, u):
                            e.wait_ge(S["rcp"], count(g, u))
                            v = s[:, u % 2, :, :]
                            e.tensor_tensor(v, v, ri[:, u % 2, :].unsqueeze(2).broadcast_to([P, HEADS, KEYS]), ALU.mult).then_inc(S["prob"], 1)

                        def add_bo(e, g, u):
                            e.wait_ge(S["r_in", u], dma_count(g))
                            e.tensor_tensor(xr[:, u, :], xr[:, u, :], bob[:, :], ALU.add).then_inc(S["xr_bo"], 1)

                        rs_1 = rstd(S["agg"], mv, ve, rs, S["ve"], S["rs"])
                        rs_2 = rstd(S["agg2"], mv2, ve2, rs2, S["ve2"], S["rs2"])

                        def body(g):
                            for u in range(N):
                                step(pool, g, u, 4, rs_1)
                                step(pool, g, u, 1, norm)
                                step(pool, g, u, -1, rs_2)
                                step(pool, g, u, 0, add_bo)
                                step(pool, g, u, 2, sub)
                        groups(pool, SUB // N, body, peel_last=1)

                    @block.vector
                    def _(dve):
                        dve.wait_ge(S["const_in"], 48)
                        dve.tensor_scalar(srcf[:, :], srcb[:, :], 0.0, None, ALU.not_equal).then_inc(S["src_neg"], 1)
                        dve.wait_ge(S["src_neg"], 1)

                        def lo_p(e, g, u):
                            e.wait_ge(S["pTh"], count(g, u))
                            e.tensor_tensor(pTl[:, :, :], pP[:, :].rearrange("p (k n) -> p k n", k=PAIRS), pTh[:, :, :], ALU.subtract).then_inc(S["pTl"], 1)

                        def stats(e, g, u):
                            e.wait_ge(S["x_in", u], dma_count(g))
                            e.bn_stats(st[:, u % 2, :], xb[:, u, :]).then_inc(S["stats"], 1)

                        def stats_done(e, g, u):
                            e.wait_ge(S["stats"], count(g, u))

                        def aggregate(e, g, u):
                            e.bn_aggr(mv[:, u % 2, :], st[:, u % 2, :]).then_inc(S["agg"], 1)

                        def stats2_done(e, g, u):
                            e.wait_ge(S["stats2"], count(g, u))

                        def aggregate2(e, g, u):
                            e.bn_aggr(mv2[:, u % 2, :], st2[:, u % 2, :]).then_inc(S["agg2"], 1)

                        def sums(e, g, u):
                            e.wait_ge(S["exp"], count(g, u))
                            e.tensor_reduce(sm[:, u % 2, :], s[:, u % 2, :, :], AX.X, ALU.add).then_inc(S["sum"], 1)
                            e.wait_ge(S["sum"], count(g, u))
                            e.reciprocal(mx[:, u % 2, :], sm[:, u % 2, :]).then_inc(S["sum2"], 1)
                            e.wait_ge(S["sum2"], count(g, u))
                            e.tensor_scalar(ri[:, u % 2, :], mx[:, u % 2, :], P_SCALE, None, ALU.mult).then_inc(S["rcp"], 1)

                        def residual(e, g, u):
                            e.wait_ge(S["att"], count(g, u))
                            e.wait_ge(S["xr_bo"], count(g, u))
                            if not isinstance(g, int) or g > 0:
                                e.wait_ge(S["x1_out", u], dma_count(g) - 16)
                                e.wait_ge(S["z_out", u], dma_count(g) - 16)
                            e.scalar_tensor_tensor(out=x1[:, u, :], in0=pO[:, :], scalar=sc[:, INV_OUT:INV_OUT + 1], in1=xr[:, u, :],
                                                   op0=ALU.mult, op1=ALU.add).then_inc(S["x1"], 1)
                            e.wait_ge(S["x1"], count(g, u))
                            e.bn_stats(st2[:, u % 2, :], x1[:, u, :]).then_inc(S["stats2"], 1)

                        def normal(e, g, u):
                            e.wait_ge(S["rs"], count(g, u))
                            at_least(e, S["xT"], count(g, u) - 2)
                            e.tensor_scalar(xn[:, u % 2, :], xb[:, u, :], mv[:, u % 2, 0:1], rs[:, u % 2, :], ALU.subtract, ALU.mult).then_inc(S["xn"], 1)

                        def masked(e, g, u):
                            e.wait_ge(S["m_in", u], dma_count(g))
                            b = (N * g + u) // (SUB // BATCH)
                            e.scalar_tensor_tensor(out=keep[:, :], in0=tg[:, u, :], scalar=0.0, in1=srcf[:, bass.ds(b * KEYS, KEYS)],
                                                   op0=ALU.not_equal, op1=ALU.mult).then_inc(S["keep"], 1)
                            e.wait_ge(S["keep"], count(g, u))
                            e.tensor_scalar(neg[:, u % 2, :], keep[:, :], 1.0, NEG, ALU.subtract, ALU.mult).then_inc(S["neg"], 1)
                            e.wait_ge(S["neg"], count(g, u))
                            e.wait_ge(S["sim"], count(g, u))
                            e.scalar_tensor_tensor(out=s[:, u % 2, :, :], in0=pS[u % 2][:, :].rearrange("p (h k) -> p h k", k=KEYS),
                                                   scalar=sc[:, INV_SIM:INV_SIM + 1],
                                                   in1=neg[:, u % 2, :].unsqueeze(1).broadcast_to([P, HEADS, KEYS]),
                                                   op0=ALU.mult, op1=ALU.add).then_inc(S["smask"], 1)
                            e.wait_ge(S["smask"], count(g, u))
                            e.tensor_reduce(mx[:, u % 2, :], s[:, u % 2, :, :], AX.X, ALU.max).then_inc(S["mx"], 1)

                        def lo_x(e, g, u):
                            e.wait_ge(S["xTh"], count(g, u))
                            e.scalar_tensor_tensor(out=xTl[:, u % 2, :, :], in0=pX[:, :].rearrange("p (k n) -> p k n", k=KC), scalar=LN_SCALE,
                                                   in1=xTh[:, u % 2, :, :], op0=ALU.mult, op1=ALU.subtract).then_inc(S["xTl"], 1)

                        def gate(e, g, u):
                            e.wait_ge(S["rs2"], count(g, u))
                            e.tensor_scalar(z[:, u, :], x1[:, u, :], mv2[:, u % 2, 0:1], rs2[:, u % 2, :], ALU.subtract, ALU.mult).then_inc(S["z"], 1)
                            e.wait_ge(S["z"], count(g, u))
                            for k in range(2):
                                e.tensor_tensor_reduce(junk[:, k, :], z[:, u, :], gw[:, k, :], 1.0, 0.0, ALU.mult, ALU.add, gg[:, u % 2, k:k + 1]).then_inc(S[f"g{k}"], 1)
                            e.wait_ge(S["g0"], count(g, u))
                            e.wait_ge(S["g1"], count(g, u))
                            e.tensor_scalar(expert1[:, bass.ds(N * g + u, 1)], gg[:, u % 2, 1:2], gg[:, u % 2, 0:1], TIE,
                                            ALU.subtract, ALU.is_gt).then_inc(S["pick1"], 1)

                        def body(g):
                            for u in range(N):
                                step(dve, g, u, 0, lo_p)
                                step(dve, g, u, 4, stats)
                                step(dve, g, u, 4, stats_done)
                                step(dve, g, u, 1, sums)
                                step(dve, g, u, 4, aggregate)
                                step(dve, g, u, -1, residual)
                                step(dve, g, u, -1, stats2_done)
                                step(dve, g, u, 4, normal)
                                step(dve, g, u, -1, aggregate2)
                                step(dve, g, u, 2, masked)
                                step(dve, g, u, 3, lo_x)
                                step(dve, g, u, -1, gate)
                        groups(dve, SUB // N, body, peel_last=1)
                        dve.wait_ge(S["pick1"], SUB)
                        dve.tensor_scalar(expert0[:, :], expert1[:, :], -1.0, 1.0, ALU.mult, ALU.add)

        A1, A2, AM, AR, SW1, IW1, SW2, IW2, SH, IH = 12, 13, 14, 18, 22, 23, 24, 25, 26, 27
        with ExitStack() as f:
            w1h = sb("w1h", [P, KC, HID], F16, f)
            w1l = sb("w1l", [P, KC, HID], F16, f)
            w2h = sb("w2h", [P, HC, DM], F16, f)
            w2l = sb("w2l", [P, HC, DM], F16, f)
            b1s = sb("b1s", [P, HC], F32, f)
            brow = sb("brow", [P, DM], F32, f)
            for e in range(3):
                first, last = e == 0, e == 2
                net = ((sw1, sb1, sw2, sb2), (w1[0], b1[0], w2[0], b2[0]), (w1[1], b1[1], w2[1], b2[1]))[e]
                gate_col = (None, expert0, expert1)[e]
                prepare(nc, e, sb, scale_of, sc, net, (w1h, w1l, w2h, w2l, b1s, brow), (A1, A2, AM, AR, SW1, IW1, SW2, IW2, SH, IH))
                ffn(nc, e, sb, ps, sc, ident, gate_col, z_d, x1_d if first else out, out, (w1h, w1l, w2h, w2l, b1s, brow), (A1, A2))


def prepare(nc, e, sb, scale_of, sc, net, dst, cols):
    w1, b1, w2, b2 = net
    w1h, w1l, w2h, w2l, b1s, brow = dst
    A1, A2, AM, AR, SW1, IW1, SW2, IW2, SH, IH = cols
    with ExitStack() as p:
        raw1 = sb(f"raw1_{e}", [P, KC, HID], F32, p)
        raw2 = sb(f"raw2_{e}", [P, HC, DM], F32, p)
        b1r = sb(f"b1r_{e}", [P, HC], F32, p)
        in1, in2, inb, amaxed, reduced, hi, dstep = (p.enter_context(nc.semaphore(f"w{e}_{n}")) for n in
                                                   ("in1", "in2", "inb", "amaxed", "reduced", "hi", "dstep"))
        am, ar = sc[:, AM:AM + 3], sc[:, AR:AR + 3]
        pieces = [(raw1[:, k, :], w1h[:, k, :], w1l[:, k, :], SW1) for k in range(KC)]
        pieces += [(raw2[:, j:j + 4, :], w2h[:, j:j + 4, :], w2l[:, j:j + 4, :], SW2) for j in range(0, HC, 4)]
        with nc.Block() as block:
            @block.sync
            def _(sp):
                sp.dma_start(raw1[:, :, :], w1.rearrange("(k p) n -> p k n", p=P)).then_inc(in1, 16)
                sp.dma_start(raw2[:, :, :], w2.rearrange("(j p) n -> p j n", p=P)).then_inc(in2, 16)
                with nc.allow_non_contiguous_dma("a bias in columns"):
                    sp.dma_start(b1r[:, :], b1.rearrange("(j p) -> p j", p=P)).then_inc(inb, 16)
                sp.dma_start(brow[:, :], b2.partition_broadcast(P)).then_inc(inb, 16)

            @block.gpsimd
            def _(pool):
                pool.wait_ge(amaxed, 3)
                pool.partition_all_reduce(ar, am, P, RADD).then_inc(reduced, 1)

            @block.vector
            def _(dve):
                steps = [0]

                def link(ins):
                    steps[0] += 1
                    ins.then_inc(dstep, 1)
                    dve.wait_ge(dstep, steps[0])

                for c, (t, s, n) in enumerate(((raw1[:, :, :], in1, 16), (raw2[:, :, :], in2, 16), (b1r[:, :], inb, 32))):
                    dve.wait_ge(s, n)
                    dve.tensor_reduce(sc[:, AM + c:AM + c + 1], t, AX.XY if c < 2 else AX.X, ALU.max,
                                      apply_absolute_value=True).then_inc(amaxed, 1)
                dve.wait_ge(reduced, 1)

                def col(c, n=1):
                    return sc[:, c:c + n]

                link(dve.tensor_copy(col(SW1), col(AR)))
                scale_of(link, dve, col(SW1), col(SW1), col(IW1))
                link(dve.tensor_copy(col(SW2), col(AR + 1)))
                scale_of(link, dve, col(SW2), col(SW2), col(IW2))
                link(dve.scalar_tensor_tensor(out=col(SH), in0=col(AR), scalar=float(DM), in1=col(AR + 2), op0=ALU.mult, op1=ALU.add))
                scale_of(link, dve, col(SH), col(SH), col(IH))
                link(dve.tensor_scalar(col(A1), col(IW1), col(SH), 1.0 / LN_SCALE, ALU.mult, ALU.mult))
                link(dve.tensor_scalar(col(A2), col(IH), col(IW2), None, ALU.mult))
                link(dve.tensor_scalar(b1s[:, :], b1r[:, :], col(SH), None, ALU.mult))
                for n, (r, h, l, s) in enumerate(pieces):
                    dve.wait_ge(hi, n + 1)
                    dve.scalar_tensor_tensor(out=l, in0=r, scalar=col(s), in1=h, op0=ALU.mult, op1=ALU.subtract)

            @block.scalar
            def _(act):
                act.wait_ge(dstep, 18)
                for n, (r, h, l, s) in enumerate(pieces):
                    act.activation(h, r, ACT.Copy, scale=sc[:, s:s + 1]).then_inc(hi, 1)


def ffn(nc, e, sb, ps, sc, ident, gate_col, z_d, res_d, out_d, weights, cols):
    w1h, w1l, w2h, w2l, b1s, brow = weights
    A1, A2 = cols
    with ExitStack() as f:
        N = 2
        R = TOK // P
        S = {n: f.enter_context(nc.semaphore(f"f{e}_{n}")) for n in
             ("gated", "zT", "zTh", "zTl", "h", "hf", "hh", "hl", "y", "o", "ob")}
        for n in ("z_in", "r_in", "out"):
            for u in range(N):
                S[n, u] = f.enter_context(nc.semaphore(f"f{e}_{n}{u}"))
        zb = sb(f"zb{e}", [P, N, R, DM], F32, f)
        rb = sb(f"rb{e}", [P, N, R, DM], F32, f)
        ob = sb(f"ob{e}", [P, N, R, DM], F32, f)
        zTh = sb(f"zTh{e}", [P, N, KC, TOK], F16, f)
        zTl = sb(f"zTl{e}", [P, N, KC, TOK], F16, f)
        HR = 4
        hf = sb(f"hf{e}", [P, HR, TOK], F32, f)
        hh = sb(f"hh{e}", [P, HR, TOK], F16, f)
        hl = sb(f"hl{e}", [P, HR, TOK], F16, f)
        pZ = ps(f"pZ{e}", [P, R, DM], f)
        pH = [ps(f"pH{e}{n}", [P, 512], f) for n in range(2)]
        pY = [[ps(f"pY{e}{u}{r}", [P, DM], f) for r in range(R)] for u in range(N)]

        def count(g, u):
            return N * g + u + 1

        def step(eng, g, u, d, fn, *more):
            g2, u2 = shift(g, u, d, N)
            if live(g2, u2, N, TILES):
                fn(eng, g2, u2, *more)

        def rows(t, g, u):
            return t[bass.ds((N * g + u) * TOK, TOK), :].rearrange("(r p) n -> p r n", p=P)

        LAG = 2
        z_ready = S["gated"] if gate_col is not None else None

        with nc.Block() as block:
            @block.sync
            def _(sp):
                def load_z(q, g, u):
                    at_least(q, S["zT"], count(g, u) - 2)
                    q.dma_start(zb[:, u, :, :], rows(z_d, g, u)).then_inc(S["z_in", u], 16)

                def load_r(q, g, u):
                    at_least(q, S["o"], count(g, u) - 2)
                    q.dma_start(rb[:, u, :, :], rows(res_d, g, u)).then_inc(S["r_in", u], 16)

                def store(q, g, u):
                    q.wait_ge(S["ob"], count(g, u))
                    q.dma_start(rows(out_d, g, u), ob[:, u, :, :]).then_inc(S["out", u], 16)

                def body(g):
                    for u in range(N):
                        step(sp, g, u, 2, load_z)
                        step(sp, g, u, 1, load_r)
                        step(sp, g, u, -1, store)
                groups(sp, TILES // N, body)
                for u in range(N):
                    sp.wait_ge(S["out", u], 16 * TILES // N)

            @block.gpsimd
            def _(pool):
                def bias(q, g, u):
                    q.wait_ge(S["o"], count(g, u))
                    for r in range(R):
                        v = q.tensor_tensor(ob[:, u, r, :], ob[:, u, r, :], brow[:, :], ALU.add)
                    v.then_inc(S["ob"], 1)

                def body(g):
                    for u in range(N):
                        step(pool, g, u, -1, bias)
                groups(pool, TILES // N, body)

            @block.tensor
            def _(pe):
                def t_z(q, g, u):
                    if gate_col is not None:
                        q.wait_ge(S["gated"], count(g, u))
                    else:
                        q.wait_ge(S["z_in", u], 16 * g + 16)
                    at_least(q, S["zTl"], count(g, u) - 1)
                    for r in range(R):
                        for k in range(KC):
                            mm = q.transpose(pZ[:, r, k * P:(k + 1) * P], zb[:, u, r, k * P:(k + 1) * P], ident[:, :])
                    mm.then_inc(S["zT"], 1)

                def first(q, g, u, j):
                    if j == 0:
                        q.wait_ge(S["zTl"], count(g, u))
                    done = HC * (N * g + u) + j
                    at_least(q, S["hh"], done - 1)
                    n = 0
                    for k in range(KC):
                        for w, zt in ((w1h, zTh), (w1h, zTl), (w1l, zTh)):
                            mm = q.matmul(pH[j % 2][:, 0:TOK], w[:, k, j * P:(j + 1) * P], zt[:, u, k, :],
                                          start=(n == 0), stop=(n == 3 * KC - 1))
                            n += 1
                    mm.then_inc(S["h"], 1)

                def second(q, g, u, j):
                    if j == 0:
                        at_least(q, S["o"], count(g, u) - 2)
                    q.wait_ge(S["hl"], HC * (N * g + u) + j + 1)
                    for r in range(R):
                        for n, (h, w) in enumerate(((hh, w2h), (hh, w2l), (hl, w2h))):
                            mm = q.matmul(pY[u][r][:, :], h[:, j % HR, r * P:(r + 1) * P], w[:, j, :],
                                          start=(j == 0 and n == 0), stop=(j == HC - 1 and n == 2))
                    mm.then_inc(S["y"], 1)

                def body(g):
                    for u in range(N):
                        for j in range(HC):
                            step(pe, g, u, 0, first, j)
                            if j >= LAG:
                                step(pe, g, u, 0, second, j - LAG)
                            else:
                                step(pe, g, u, -1, second, j - LAG + HC)
                            if j == 9:
                                step(pe, g, u, 1, t_z)
                groups(pe, TILES // N, body)

            @block.scalar
            def _(act):
                def hi_z(q, g, u):
                    q.wait_ge(S["zT"], count(g, u))
                    at_least(q, S["h"], HC * (count(g, u) - 2))
                    for r in range(R):
                        v = q.activation(zTh[:, u, :, r * P:(r + 1) * P], pZ[:, r, :].rearrange("p (k n) -> p k n", k=KC), ACT.Copy,
                                         scale=LN_SCALE)
                    v.then_inc(S["zTh"], 1)

                def relu(q, g, u, j):
                    done = HC * (N * g + u) + j
                    q.wait_ge(S["h"], done + 1)
                    at_least(q, S["hl"], done + 1 - HR)
                    q.activation(hf[:, j % HR, :], pH[j % 2][:, 0:TOK], ACT.Relu, bias=b1s[:, j:j + 1], scale=sc[:, A1:A1 + 1]).then_inc(S["hf"], 1)
                    at_least(q, S["y"], done + 1 - HR)
                    q.activation(hh[:, j % HR, :], pH[j % 2][:, 0:TOK], ACT.Relu, bias=b1s[:, j:j + 1], scale=sc[:, A1:A1 + 1]).then_inc(S["hh"], 1)

                def body(g):
                    for u in range(N):
                        for j in range(HC):
                            step(act, g, u, 0, relu, j)
                            if j == 9:
                                step(act, g, u, 1, hi_z)
                groups(act, TILES // N, body)

            @block.vector
            def _(dve):
                def gated(q, g, u):
                    q.wait_ge(S["z_in", u], 16 * g + 16)
                    for r in range(R):
                        v = q.tensor_scalar(zb[:, u, r, :], zb[:, u, r, :], gate_col[:, bass.ds((N * g + u) * R + r, 1)], None, ALU.mult)
                    v.then_inc(S["gated"], 1)

                def lo_z(q, g, u):
                    q.wait_ge(S["zTh"], count(g, u))
                    for r in range(R):
                        v = q.scalar_tensor_tensor(out=zTl[:, u, :, r * P:(r + 1) * P], in0=pZ[:, r, :].rearrange("p (k n) -> p k n", k=KC),
                                                   scalar=LN_SCALE, in1=zTh[:, u, :, r * P:(r + 1) * P], op0=ALU.mult, op1=ALU.subtract)
                    v.then_inc(S["zTl"], 1)

                def lo_h(q, g, u, j):
                    q.wait_ge(S["hh"], HC * (N * g + u) + j + 1)
                    q.tensor_tensor(hl[:, j % HR, :], hf[:, j % HR, :], hh[:, j % HR, :], ALU.subtract).then_inc(S["hl"], 1)

                def result(q, g, u):
                    q.wait_ge(S["y"], HC * count(g, u))
                    q.wait_ge(S["r_in", u], 16 * g + 16)
                    if not isinstance(g, int) or g > 0:
                        q.wait_ge(S["out", u], 16 * g)
                    for r in range(R):
                        v = q.scalar_tensor_tensor(out=ob[:, u, r, :], in0=pY[u][r][:, :], scalar=sc[:, A2:A2 + 1], in1=rb[:, u, r, :],
                                                   op0=ALU.mult, op1=ALU.add)
                    v.then_inc(S["o"], 1)

                def body(g):
                    for u in range(N):
                        for j in range(HC):
                            step(dve, g, u, 0, lo_h, j)
                            if j == 3:
                                step(dve, g, u, -1, result)
                            if j == 5 and gate_col is not None:
                                step(dve, g, u, 1, gated)
                            if j == 9:
                                step(dve, g, u, 1, lo_z)
                groups(dve, TILES // N, body)


def kernel(**inputs):
    import numpy as np
    import concourse.bacc as bacc
    from concourse.bass_utils import run_bass_kernel_spmd

    nc = bacc.Bacc("TRN2", target_bir_lowering=False, num_devices=1)
    a = {k: np.asarray(v) for k, v in inputs.items()}
    laid = {
        "x": a["x"].reshape(ROWS, DM),
        "ctxT": a["ctx_1024"].reshape(BATCH * KEYS, DM).T,
        "tgt": a["mask_Bx1xSxS2_ik0"].reshape(ROWS, KEYS),
        "src": a["mask_Bx1xS2_bk0"].reshape(BATCH * KEYS),
        "wq": a["L0_xattn_Wq"], "wkT": a["L0_xattn_Wk"].T, "wvT": a["L0_xattn_Wv"].T, "woT": a["L0_xattn_Wo"].T,
        "bo": a["L0_xattn_bo"], "gate_w": a["L0_ffn_gate_w"], "w1": a["L0_ffn_w1"], "b1": a["L0_ffn_b1"],
        "w2": a["L0_ffn_w2"], "b2": a["L0_ffn_b2"], "sw1": a["L0_ffn_sw1"], "sb1": a["L0_ffn_sb1"],
        "sw2": a["L0_ffn_sw2"], "sb2": a["L0_ffn_sb2"],
    }
    arrays, args = {}, {}
    for name, v in laid.items():
        v = np.ascontiguousarray(v)
        arrays[f"in_{name}"] = v
        args[name] = nc.dram_tensor(f"in_{name}", v.shape, mybir.dt.from_np(v.dtype), kind="ExternalInput").ap()
    out = nc.dram_tensor("out_0", (ROWS, DM), F32, kind="ExternalOutput").ap()
    xattn_ffn(nc, out=out, **args)
    r = run_bass_kernel_spmd(nc, [arrays], core_ids=[0])
    return r.results[0]["out_0"].reshape(BATCH, SEQ, DM)
```

```python
from contextlib import ExitStack

import concourse.bass as bass
from concourse import mybir

F32 = mybir.dt.float32
F16 = mybir.dt.float16
I32 = mybir.dt.int32
U8 = mybir.dt.uint8
ALU = mybir.AluOpType
ACT = mybir.ActivationFunctionType
AX = mybir.AxisListType
RMAX = bass.bass_isa.ReduceOp.max

P = 128
BATCH, SEQ, DM = 4, 1024, 512
KEYS, HEADS, DH = 64, 16, 64
INNER = HEADS * DH
HID = 2048
ROWS = BATCH * SEQ
KC = DM // P
PAIRS = HEADS // 2
HC = HID // P
HK = HEADS * KEYS
SUB = ROWS // P
TOK = 256
TILES = ROWS // TOK
SLOT_TILES = TILES + 1
SLOTS = SLOT_TILES * TOK
SLOT_SUBS = SLOTS // P
SCALE = DH ** -0.5
NEG = float(3.4028234663852886e38)
EPS = 1e-5
LN_SCALE = 2.0 ** 11
P_SCALE = 2.0 ** 15
TIE = 2.0 ** -25
EXP_FIELD = 0x7F800000
MANT = 1 << 23


def shift(g, u, d, n):
    return g + (u + d) // n, (u + d) % n


def live(g, u, n, count):
    return not isinstance(g, int) or 0 <= n * g + u < count


def at_least(eng, sem, value):
    if not isinstance(value, int) or value > 0:
        eng.wait_ge(sem, value)


def wait_apart(eng, sem, count):
    if isinstance(count, int):
        at_least(eng, sem, count)
    else:
        count = eng.to_reg(count)
        eng.wait_ge(sem, 1)
        eng.wait_ge(sem, count)


def groups(eng, n, body, peel_last=1):
    for g in (-1, 0, 1):
        body(g)
    with eng.Fori(2, n - peel_last) as g:
        body(g)
    for g in range(n - peel_last, n + 1):
        body(g)


def xattn_ffn(nc, x, ctxT, tgt, src, wq, wkT, wvT, woT, bo, gate_w, w1, b1, w2, b2, sw1, sb1, sw2, sb2, out):
    x1_d = nc.dram_tensor("x1_scratch", (ROWS, DM), F32, kind="Internal").ap()
    z_d = nc.dram_tensor("z_scratch", (ROWS, DM), F32, kind="Internal").ap()
    res_d = nc.dram_tensor("res_scratch", (ROWS, DM), F32, kind="Internal").ap()
    s1_d = nc.dram_tensor("s1_split", (2, DM, HID), F16, kind="Internal").ap()
    s2_d = nc.dram_tensor("s2_split", (2, HID, DM), F16, kind="Internal").ap()
    e1_d = nc.dram_tensor("e1_split", (2, 2, DM, HID), F16, kind="Internal").ap()
    e2_d = nc.dram_tensor("e2_split", (2, 2, HID, DM), F16, kind="Internal").ap()

    def units(t):
        if len(t.shape) == 3:
            t = t.rearrange("e k n -> (e k) n")
        return t if t.shape[1] == DM else t.rearrange("k (a n) -> (k a) n", n=DM)

    with ExitStack() as ctx:
        def sem(name):
            return ctx.enter_context(nc.semaphore(name))

        def sb(name, shape, dt=F32, where=ctx):
            return where.enter_context(nc.sbuf_tensor(name, shape, dt))

        def ps(name, shape, where):
            return where.enter_context(nc.psum_tensor(name, shape, F32))

        ident = sb("ident", [P, P])
        sc = sb("sc", [P, 48])
        expert1 = sb("expert1", [P, SUB])
        ones = sb("ones", [P, P])
        upper = sb("upper", [P, P])
        lane = sb("lane", [P, P])
        row_id = sb("row_id", [P, SUB])
        starts = sb("starts", [P, SLOT_TILES])
        amw = sb("amw", [P, 4])
        b1e = sb("b1e", [P, 2 * HC])
        b1e_s = sb("b1e_s", [P, 2, HC])
        b1s = sb("b1s", [P, HC])
        (EBITS, SM, IM, SV, IV, INV_SIM, INV_OUT, SW1, IW1, SW2, IW2, SH, IH, A1, A2,
         EW1, IEW1, EW2, IEW2, EH, IEH, EA1, EA2, C0, AME, ARE) = [*range(24), 24, 28]

        def scale_of(link, eng, bound, s, inv):
            n = bound.shape[1]
            e = sc[:, EBITS:EBITS + n].bitcast(I32)
            link(eng.tensor_scalar(bound, bound, 2.0 ** -90, 2.0 ** 90, ALU.max, ALU.min))
            link(eng.tensor_scalar(e, bound.bitcast(I32), EXP_FIELD, None, ALU.bitwise_and))
            link(eng.tensor_scalar(s.bitcast(I32), e, -1.0, float(268 * MANT), ALU.mult, ALU.add))
            link(eng.tensor_scalar(inv.bitcast(I32), e, float(-14 * MANT), None, ALU.add))

        def net_scales(link, eng, largest, b1_in, b1_out, cols):
            S1, I1, S2, I2, H, IHH, O1, O2 = cols

            def col(c):
                return sc[:, c:c + 1]

            link(eng.tensor_copy(col(S1), largest[:, 0:1]))
            scale_of(link, eng, col(S1), col(S1), col(I1))
            link(eng.tensor_copy(col(S2), largest[:, 1:2]))
            scale_of(link, eng, col(S2), col(S2), col(I2))
            link(eng.scalar_tensor_tensor(out=col(H), in0=largest[:, 0:1], scalar=float(DM), in1=largest[:, 2:3], op0=ALU.mult, op1=ALU.add))
            scale_of(link, eng, col(H), col(H), col(IHH))
            link(eng.tensor_scalar(col(O1), col(I1), col(H), 1.0 / LN_SCALE, ALU.mult, ALU.mult))
            link(eng.tensor_scalar(col(O2), col(IHH), col(I2), None, ALU.mult))
            link(eng.tensor_scalar(b1_out, b1_in, col(H), None, ALU.mult))

        with ExitStack() as at:
            fmh = sb("fmh", [P, KC, BATCH, HK], F16, at)
            fml = sb("fml", [P, KC, BATCH, HK], F16, at)
            fvh = sb("fvh", [P, BATCH, PAIRS, DM], F16, at)
            fvl = sb("fvl", [P, BATCH, PAIRS, DM], F16, at)
            with ExitStack() as pro:
                slot0 = sb("slot0", [P, 4096], F32, pro)
                slot1 = sb("slot1", [P, 4096], F32, pro)
                kd = sb("kd", [P, PAIRS, BATCH, 2, KEYS], F32, pro)
                vd = sb("vd", [P, PAIRS, BATCH, 2, KEYS], F32, pro)
                ctxt = sb("ctxt", [P, KC, BATCH * KEYS], F32, pro)
                am = sb("am", [P, 4], F32, pro)
                amr = sb("amr", [P, 4], F32, pro)
                ams = sb("ams", [P, 18], F32, pro)
                ams3 = sb("ams3", [P, 3], F32, pro)
                amsr = sb("amsr", [P, 3], F32, pro)
                b1r = sb("b1r", [P, HC], F32, pro)
                raw1 = fvh[:, :, :, :].rearrange("p b q n -> p (b q n)").bitcast(F32)
                raw2 = fvl[:, :, :, :].rearrange("p b q n -> p (b q n)").bitcast(F32)
                in_s1, in_s2, in_b1, s_seen, s_red, s_max = (pro.enter_context(nc.semaphore(n)) for n in ("in_s1", "in_s2", "in_b1", "s_seen", "s_red", "s_max"))
                reduced_v = pro.enter_context(nc.semaphore("reduced_v"))
                sstep = pro.enter_context(nc.semaphore("sstep"))
                pk = [ps(f"pk{n}", [P, 512], pro) for n in range(4)]
                in_ctx, in_wk, in_wv, in_wq, in_wo = (pro.enter_context(nc.semaphore(n)) for n in ("in_ctx", "in_wk", "in_wv", "in_wq", "in_wo"))
                zeroed = pro.enter_context(nc.semaphore("zeroed"))
                kv_done = pro.enter_context(nc.semaphore("kv_done"))
                kv_out = pro.enter_context(nc.semaphore("kv_out"))
                amaxed = pro.enter_context(nc.semaphore("amaxed"))
                reduced = pro.enter_context(nc.semaphore("reduced"))
                f_done = pro.enter_context(nc.semaphore("f_done"))
                f_hi = pro.enter_context(nc.semaphore("f_hi"))
                f_lo = pro.enter_context(nc.semaphore("f_lo"))
                dstep = pro.enter_context(nc.semaphore("dstep_p"))
                vstep = pro.enter_context(nc.semaphore("vstep"))
                idst = pro.enter_context(nc.semaphore("idst"))
                wk_v = slot0[:, :].rearrange("p (k e) -> p k e", k=KC)
                wv_v = slot1[:, :].rearrange("p (k e) -> p k e", k=KC)
                wq_v = slot0[:, :].rearrange("p (q c) -> p q c", q=PAIRS)
                wo_v = slot1[:, :].rearrange("p (q c) -> p q c", q=PAIRS)
                NF = KC * PAIRS + BATCH * PAIRS

                with nc.Block() as block:
                    @block.sync
                    def _(sp):
                        sp.dma_start(ctxt[:, :, :], ctxT.rearrange("(k p) n -> p k n", p=P)).then_inc(in_ctx, 16)
                        sp.dma_start(wk_v, wkT.rearrange("(k p) n -> p k n", p=P)).then_inc(in_wk, 16)
                        sp.dma_start(wv_v, wvT.rearrange("(k p) n -> p k n", p=P)).then_inc(in_wv, 16)
                        sp.dma_start(raw1, sw1.rearrange("(p k) n -> p (k n)", p=P)).then_inc(in_s1, 16)
                        sp.wait_ge(kv_done, PAIRS)
                        sp.dma_start(wq_v, wq.rearrange("(q p) n -> p q n", p=P)).then_inc(in_wq, 16)
                        sp.dma_start(raw2, sw2.rearrange("(p k) n -> p (k n)", p=P)).then_inc(in_s2, 16)
                        with nc.allow_non_contiguous_dma("biases in columns"):
                            sp.dma_start(b1r[:, :], sb1.rearrange("(j p) -> p j", p=P)).then_inc(in_b1, 16)
                            sp.dma_start(b1e[:, :], b1.rearrange("e (j p) -> p (e j)", p=P)).then_inc(in_b1, 16)
                        sp.wait_ge(kv_done, 2 * PAIRS)
                        sp.dma_start(wo_v, woT.rearrange("(q p) n -> p q n", p=P)).then_inc(in_wo, 16)

                    @block.gpsimd
                    def _(pool):
                        pool.memset(ident[:, :], 0.0).then_inc(idst, 1)
                        pool.wait_ge(idst, 1)
                        pool.affine_select(out=ident[:, :], in_=ident[:, :], compare_op=ALU.not_equal, fill=1.0,
                                           base=0, pattern=[[-1, P]], channel_multiplier=1).then_inc(idst, 1)
                        pool.memset(kd[:, :, :, :, :], 0.0).then_inc(zeroed, 1)
                        pool.memset(vd[:, :, :, :, :], 0.0).then_inc(zeroed, 1)
                        pool.memset(ones[:, :], 1.0).then_inc(idst, 1)
                        pool.wait_ge(idst, 3)
                        pool.affine_select(out=upper[:, :], in_=ones[:, :], compare_op=ALU.is_gt, fill=0.0,
                                           base=0, pattern=[[1, P]], channel_multiplier=-1)
                        pool.iota(lane[:, :], pattern=[[1, P]], base=0, channel_multiplier=0, allow_small_or_imprecise_dtypes=True)
                        pool.iota(row_id[:, :], pattern=[[P, SUB]], base=-ROWS, channel_multiplier=1, allow_small_or_imprecise_dtypes=True)
                        pool.iota(starts[:, :], pattern=[[TOK, SLOT_TILES]], base=0, channel_multiplier=0, allow_small_or_imprecise_dtypes=True)
                        pool.wait_ge(amaxed, 2)
                        pool.partition_all_reduce(amr[:, 0:2], am[:, 0:2], P, RMAX).then_inc(reduced, 1)
                        pool.wait_ge(amaxed, 4)
                        pool.partition_all_reduce(amr[:, 2:4], am[:, 2:4], P, RMAX).then_inc(reduced_v, 1)
                        pool.wait_ge(s_max, 3)
                        pool.partition_all_reduce(amsr[:, :], ams3[:, :], P, RMAX).then_inc(s_red, 1)

                    @block.tensor
                    def _(pe):
                        pe.wait_ge(in_ctx, 16)
                        n = 0
                        for w, s in ((wk_v, in_wk), (wv_v, in_wv)):
                            pe.wait_ge(s, 16)
                            for q in range(PAIRS):
                                if n >= 4:
                                    pe.wait_ge(kv_out, n - 3)
                                for k in range(KC):
                                    mm = pe.matmul(pk[n % 4][:, 0:BATCH * KEYS], w[:, k, q * P:(q + 1) * P], ctxt[:, k, :],
                                                   start=(k == 0), stop=(k == KC - 1))
                                mm.then_inc(kv_done, 1)
                                n += 1
                        pe.wait_ge(kv_out, 2 * PAIRS)
                        pe.wait_ge(in_wq, 16)
                        for n in range(NF):
                            if n == KC * PAIRS:
                                pe.wait_ge(in_wo, 16)
                            if n >= 4:
                                pe.wait_ge(f_lo, n - 3)
                            if n < KC * PAIRS:
                                k, q = n // PAIRS, n % PAIRS
                                mm = pe.matmul(pk[n % 4][:, :], wq_v[:, q, k * P:(k + 1) * P],
                                               kd[:, q, :, :, :].rearrange("p b h k -> p (b h k)"), start=True, stop=True)
                            else:
                                b, q = (n - KC * PAIRS) // PAIRS, n % PAIRS
                                mm = pe.matmul(pk[n % 4][:, :], vd[:, q, b, :, :].rearrange("p h k -> p (h k)"),
                                               wo_v[:, q, :], start=True, stop=True)
                            mm.then_inc(f_done, 1)

                    def f_dst(n, m, v):
                        if n < KC * PAIRS:
                            k, q = n // PAIRS, n % PAIRS
                            return m[:, k, :, q * P:(q + 1) * P]
                        b, q = (n - KC * PAIRS) // PAIRS, n % PAIRS
                        return v[:, b, q, :]

                    def f_src(n):
                        s = pk[n % 4][:, :]
                        return s.rearrange("p (b n) -> p b n", b=BATCH) if n < KC * PAIRS else s

                    @block.scalar
                    def _(act):
                        act.wait_ge(dstep, 5)
                        for n in range(NF):
                            if n == KC * PAIRS:
                                act.wait_ge(vstep, 5)
                                act.wait_ge(s_seen, 17)
                            act.wait_ge(f_done, n + 1)
                            s = SM if n < KC * PAIRS else SV
                            act.activation(f_dst(n, fmh, fvh), f_src(n), ACT.Copy, scale=sc[:, s:s + 1]).then_inc(f_hi, 1)

                    @block.vector
                    def _(dve):
                        dve.wait_ge(zeroed, 2)
                        for n in range(2 * PAIRS):
                            q, t = n % PAIRS, (kd if n < PAIRS else vd)
                            dve.wait_ge(kv_done, n + 1)
                            v = pk[n % 4][:, 0:BATCH * KEYS].rearrange("p (b k) -> p b k", b=BATCH)
                            dve.tensor_copy(t[0:64, q, :, 0, :], v[0:64])
                            dve.tensor_copy(t[64:128, q, :, 1, :], v[64:128]).then_inc(kv_out, 1)
                        dve.wait_ge(kv_out, 2 * PAIRS)

                        def largest(c, t, arrived):
                            if arrived is not None:
                                dve.wait_ge(arrived, 16)
                            dve.tensor_reduce(am[:, c:c + 1], t, AX.XYZW if len(t.shape) > 2 else AX.X, ALU.max,
                                              apply_absolute_value=True).then_inc(amaxed, 1)

                        def linker(sem):
                            steps = [0]

                            def link(ins):
                                steps[0] += 1
                                ins.then_inc(sem, 1)
                                dve.wait_ge(sem, steps[0])
                            return link

                        def col(c):
                            return sc[:, c:c + 1]

                        largest(0, kd[:, :, :, :, :], None)
                        largest(1, slot0[:, :], in_wq)
                        dve.wait_ge(reduced, 1)
                        link = linker(dstep)
                        link(dve.tensor_scalar(col(SM), amr[:, 0:1], amr[:, 1:2], float(DH), ALU.mult, ALU.mult))
                        scale_of(link, dve, col(SM), col(SM), col(IM))

                        def split(n):
                            dve.wait_ge(f_hi, n + 1)
                            s = SM if n < KC * PAIRS else SV
                            dve.scalar_tensor_tensor(out=f_dst(n, fml, fvl), in0=f_src(n), scalar=col(s),
                                                     in1=f_dst(n, fmh, fvh), op0=ALU.mult, op1=ALU.subtract).then_inc(f_lo, 1)

                        for n in range(KC * PAIRS):
                            split(n)
                            if n % 2 == 1:
                                c = n // 2
                                dve.wait_ge(in_s1 if c < 8 else in_s2, 16)
                                t = (raw1 if c < 8 else raw2)[:, (c % 8) * 1024:(c % 8 + 1) * 1024]
                                dve.tensor_reduce(ams[:, c:c + 1], t, AX.X, ALU.max, apply_absolute_value=True).then_inc(s_seen, 1)
                        largest(2, vd[:, :, :, :, :], None)
                        largest(3, slot1[:, :], in_wo)
                        dve.wait_ge(in_b1, 32)
                        dve.tensor_reduce(ams[:, 16:17], b1r[:, :], AX.X, ALU.max, apply_absolute_value=True).then_inc(s_seen, 1)
                        dve.wait_ge(s_seen, 17)
                        for c, (a0, a1) in enumerate(((0, 8), (8, 16), (16, 17))):
                            dve.tensor_reduce(ams3[:, c:c + 1], ams[:, a0:a1], AX.X, ALU.max).then_inc(s_max, 1)
                        dve.wait_ge(reduced_v, 1)
                        link = linker(vstep)
                        link(dve.tensor_scalar(col(SV), amr[:, 2:3], amr[:, 3:4], float(DH), ALU.mult, ALU.mult))
                        scale_of(link, dve, col(SV), col(SV), col(IV))
                        for n in range(KC * PAIRS, NF):
                            split(n)
                        dve.wait_ge(s_red, 1)
                        link = linker(sstep)
                        link(dve.tensor_scalar(col(INV_SIM), col(IM), SCALE / LN_SCALE, None, ALU.mult))
                        link(dve.tensor_scalar(col(INV_OUT), col(IV), 1.0 / P_SCALE, None, ALU.mult))
                        net_scales(link, dve, amsr, b1r[:, :], b1s[:, :], (SW1, IW1, SW2, IW2, SH, IH, A1, A2))
                        link(dve.memset(amw[:, :], 0.0))

            with ExitStack() as a:
                N = 4
                S = {}

                def sems(*names):
                    for n in names:
                        S[n] = a.enter_context(nc.semaphore("a_" + n))

                sems("const_in", "src_neg", "stats", "rs", "xn", "xT", "xTh", "xTl", "sim", "keep", "neg", "smask", "mx", "sub", "exp",
                     "sum", "sum2", "rcp", "half_set", "prob", "pT", "pTh", "pTl", "att", "xr_bo", "x1", "stats2", "rs2", "z", "g0", "g1", "pick1", "pick0",
                     "ve", "ve2", "agg", "agg2")
                for n in ("x_in", "m_in"):
                    for u in range(N):
                        S[n, u] = a.enter_context(nc.semaphore(f"a_{n}{u}"))
                for n in ("r_in", "x1_out", "z_out", "ew_in", "sw_in", "sw_out"):
                    for u in range(2):
                        S[n, u] = a.enter_context(nc.semaphore(f"a_{n}{u}"))
                sems("ew_max", "amw", "sws", "swh", "swl")
                xb = sb("xb", [P, 4, DM], F32, a)
                xn = sb("xn", [P, 2, DM], F32, a)
                xTh = sb("xTh", [P, 2, KC, P], F16, a)
                xTl = sb("xTl", [P, 2, KC, P], F16, a)
                tg = sb("tg", [P, 4, KEYS], I32, a)
                keep = sb("keep", [P, KEYS], F32, a)
                neg = sb("neg", [P, 2, KEYS], F32, a)
                srcb = sb("srcb", [P, BATCH * KEYS], U8, a)
                srcf = sb("srcf", [P, BATCH * KEYS], F32, a)
                s = sb("s", [P, 2, HEADS, KEYS], F32, a)
                mx = sb("mx", [P, 2, HEADS], F32, a)
                sm = sb("sm", [P, 2, HEADS], F32, a)
                ri = sb("ri", [P, 2, HEADS], F32, a)
                pTh = sb("pTh", [P, PAIRS, P], F16, a)
                pTl = sb("pTl", [P, PAIRS, P], F16, a)
                xr = sb("xr", [P, 2, DM], F32, a)
                x1 = sb("x1", [P, 2, DM], F32, a)
                z = sb("z", [P, 2, DM], F32, a)
                ew = sb("ew", [P, 2, 2, DM], F32, a)
                ewm = sb("ewm", [P, 2, 2], F32, a)
                sw = sb("sw", [P, 2, DM], F32, a)
                swh = sb("swh", [P, 2, DM], F16, a)
                swl = sb("swl", [P, 2, DM], F16, a)
                bob = sb("bob", [P, DM], F32, a)
                gw = sb("gw", [P, 2, DM], F32, a)
                junk = sb("junk", [P, DM], F32, a)
                half = sb("half", [P, 1], F32, a)
                eps = sb("eps", [P, 1], F32, a)
                st = sb("st", [P, 2, 6], F32, a)
                mv = sb("mv", [P, 2, 2], F32, a)
                ve = sb("ve", [P, 2, 1], F32, a)
                rs = sb("rs", [P, 2, 1], F32, a)
                st2 = sb("st2", [P, 2, 6], F32, a)
                mv2 = sb("mv2", [P, 2, 2], F32, a)
                ve2 = sb("ve2", [P, 2, 1], F32, a)
                rs2 = sb("rs2", [P, 2, 1], F32, a)
                gg = sb("gg", [P, 2, 2], F32, a)
                pS = [ps(f"pS{n}", [P, HK], a) for n in range(2)]
                pX = ps("pX", [P, DM], a)
                pP = ps("pP", [P, HK], a)
                pO = ps("pO", [P, DM], a)

                def count(g, u):
                    return N * g + u + 1

                def dma_count(g):
                    return 16 * g + 16

                def dma_count2(g, u):
                    return 16 * (2 * g + u // 2 + 1)

                def step(eng, g, u, d, fn):
                    g2, u2 = shift(g, u, d, N)
                    if live(g2, u2, N, SUB):
                        fn(eng, g2, u2)

                def rows(t, g, u):
                    return t[bass.ds((N * g + u) * P, P), :]

                with nc.Block() as block:
                    @block.sync
                    def _(sp):
                        sp.dma_start(srcb[:, :], src.partition_broadcast(P)).then_inc(S["const_in"], 16)
                        sp.dma_start(bob[:, :], bo.partition_broadcast(P)).then_inc(S["const_in"], 16)
                        sp.dma_start(gw[:, :, :].rearrange("p e n -> p (e n)"),
                                     gate_w.rearrange("e n -> (e n)").partition_broadcast(P)).then_inc(S["const_in"], 16)

                        def load_x(e, g, u):
                            at_least(e, S["xn"], count(g, u) - 4)
                            e.dma_start(xb[:, u, :], rows(x, g, u)).then_inc(S["x_in", u], 16)

                        def load_m(e, g, u):
                            at_least(e, S["keep"], count(g, u) - 4)
                            e.dma_start(tg[:, u, :], rows(tgt, g, u)).then_inc(S["m_in", u], 16)

                        def load_r(e, g, u):
                            at_least(e, S["x1"], count(g, u) - 2)
                            e.dma_start(xr[:, u % 2, :], rows(x, g, u)).then_inc(S["r_in", u % 2], 16)

                        def load_w(e, g, u):
                            at_least(e, S["ew_max"], 2 * count(g, u) - 4)
                            e.dma_start(ew[:, u % 2, 0, :], rows(units(w1), g, u)).then_inc(S["ew_in", u % 2], 16)
                            e.dma_start(ew[:, u % 2, 1, :], rows(units(w2), g, u)).then_inc(S["ew_in", u % 2], 16)
                            wait_apart(e, S["swl"], count(g, u) - 2)
                            e.dma_start(sw[:, u % 2, :], sw_rows((sw1, sw2)[u % 2], g, u)).then_inc(S["sw_in", u % 2], 16)

                        def sw_rows(t, g, u):
                            return units(t)[bass.ds((2 * g + u // 2) * P, P), :]

                        def store_w(e, g, u):
                            wait_apart(e, S["swl"], count(g, u))
                            t = (s1_d, s2_d)[u % 2]
                            e.dma_start(sw_rows(t[0], g, u), swh[:, u % 2, :]).then_inc(S["sw_out", u % 2], 16)
                            e.dma_start(sw_rows(t[1], g, u), swl[:, u % 2, :]).then_inc(S["sw_out", u % 2], 16)

                        def store(e, g, u):
                            e.wait_ge(S["x1"], count(g, u))
                            e.dma_start(rows(x1_d, g, u), x1[:, u % 2, :]).then_inc(S["x1_out", u % 2], 16)
                            e.wait_ge(S["z"], count(g, u))
                            e.dma_start(rows(z_d, g, u), z[:, u % 2, :]).then_inc(S["z_out", u % 2], 16)

                        def body(g):
                            for u in range(N):
                                step(sp, g, u, 6, load_x)
                                step(sp, g, u, 4, load_m)
                                step(sp, g, u, 1, load_r)
                                step(sp, g, u, -2, store)
                                step(sp, g, u, 1, load_w)
                                step(sp, g, u, -1, store_w)
                        for g in (-2,):
                            for u in (2, 3):
                                step(sp, g, u, 6, load_x)
                        groups(sp, SUB // N, body, peel_last=2)
                        for u in range(2):
                            sp.wait_ge(S["x1_out", u], 16 * SUB // 2)
                            sp.wait_ge(S["z_out", u], 16 * SUB // 2)
                            sp.wait_ge(S["sw_out", u], 16 * SUB)

                    @block.tensor
                    def _(pe):
                        def t_x(e, g, u):
                            e.wait_ge(S["xn"], count(g, u))
                            at_least(e, S["xTl"], count(g, u) - 1)
                            for k in range(KC):
                                mm = e.transpose(pX[:, k * P:(k + 1) * P], xn[:, u % 2, k * P:(k + 1) * P], ident[:, :])
                            mm.then_inc(S["xT"], 1)

                        def sim(e, g, u):
                            e.wait_ge(S["xTl"], count(g, u))
                            at_least(e, S["smask"], count(g, u) - 2)
                            b = (N * g + u) // (SUB // BATCH)
                            for h in range(2):
                                n = 0
                                for k in range(KC):
                                    for xt, f in ((xTh, fmh), (xTh, fml), (xTl, fmh)):
                                        mm = e.matmul(pS[u % 2][:, h * 512:(h + 1) * 512], xt[:, u % 2, k, :],
                                                      f[:, k, bass.ds(b, 1), h * 512:(h + 1) * 512],
                                                      start=(n == 0), stop=(n == 3 * KC - 1))
                                        n += 1
                            mm.then_inc(S["sim"], 1)

                        def t_p(e, g, u):
                            e.wait_ge(S["prob"], count(g, u))
                            at_least(e, S["pTl"], count(g, u) - 1)
                            for q in range(PAIRS):
                                mm = e.transpose(pP[:, q * P:(q + 1) * P],
                                                 s[:, u % 2, 2 * q:2 * q + 2, :].rearrange("p h k -> p (h k)"), ident[:, :])
                            mm.then_inc(S["pT"], 1)

                        def attend(e, g, u):
                            e.wait_ge(S["pTl"], count(g, u))
                            at_least(e, S["x1"], count(g, u) - 1)
                            b = (N * g + u) // (SUB // BATCH)
                            n = 0
                            for q in range(PAIRS):
                                for pt, f in ((pTh, fvh), (pTh, fvl), (pTl, fvh)):
                                    mm = e.matmul(pO[:, :], pt[:, q, :], f[:, bass.ds(b, 1), q, :],
                                                  start=(n == 0), stop=(n == 3 * PAIRS - 1))
                                    n += 1
                            mm.then_inc(S["att"], 1)

                        def body(g):
                            for u in range(N):
                                step(pe, g, u, 0, t_p)
                                step(pe, g, u, 2, sim)
                                step(pe, g, u, 3, t_x)
                                step(pe, g, u, 0, attend)
                        groups(pe, SUB // N, body, peel_last=1)

                    @block.scalar
                    def _(act):
                        def hi_x(e, g, u):
                            e.wait_ge(S["xT"], count(g, u))
                            at_least(e, S["sim"], count(g, u) - 2)
                            e.activation(xTh[:, u % 2, :, :], pX[:, :].rearrange("p (k n) -> p k n", k=KC), ACT.Copy, scale=LN_SCALE).then_inc(S["xTh"], 1)

                        def hi_p(e, g, u):
                            e.wait_ge(S["pT"], count(g, u))
                            at_least(e, S["att"], count(g, u) - 1)
                            e.activation(pTh[:, :, :], pP[:, :].rearrange("p (k n) -> p k n", k=PAIRS), ACT.Copy).then_inc(S["pTh"], 1)

                        def scale_w(e, g, u):
                            s_col = (SW1, SW2)[u % 2]
                            e.wait_ge(S["sw_in", u % 2], dma_count2(g, u))
                            at_least(e, S["swl"], count(g, u) - 2)
                            if not isinstance(g, int) or N * g + u >= 2:
                                e.wait_ge(S["sw_out", u % 2], 2 * dma_count2(g, u) - 32)
                            e.activation(swh[:, u % 2, :], sw[:, u % 2, :], ACT.Copy, scale=sc[:, s_col:s_col + 1]).then_inc(S["swh"], 1)
                            e.wait_ge(S["swh"], count(g, u))
                            e.activation(sw[:, u % 2, :], sw[:, u % 2, :], ACT.Copy, scale=sc[:, s_col:s_col + 1]).then_inc(S["sws"], 1)

                        def exp(e, g, u):
                            e.wait_ge(S["sub"], count(g, u))
                            e.activation(s[:, u % 2, :, :], s[:, u % 2, :, :], ACT.Exp).then_inc(S["exp"], 1)

                        def body(g):
                            for u in range(N):
                                step(act, g, u, 0, hi_p)
                                step(act, g, u, 3, hi_x)
                                step(act, g, u, 2, exp)
                                step(act, g, u, 0, scale_w)
                        groups(act, SUB // N, body, peel_last=1)

                    @block.gpsimd
                    def _(pool):
                        pool.memset(half[:, :], -0.5).then_inc(S["half_set"], 1)
                        pool.memset(eps[:, :], EPS).then_inc(S["half_set"], 1)
                        pool.wait_ge(S["const_in"], 48)
                        pool.wait_ge(S["half_set"], 2)

                        def rstd(src_sem, mv, ve, rs, ves, done):
                            def fn(e, g, u):
                                e.wait_ge(src_sem, count(g, u))
                                e.tensor_tensor(ve[:, u % 2, :], mv[:, u % 2, 1:2], eps[:, :], ALU.add).then_inc(ves, 1)
                                e.wait_ge(ves, count(g, u))
                                e.tensor_tensor(rs[:, u % 2, :], ve[:, u % 2, :], half[:, :], ALU.pow).then_inc(done, 1)
                            return fn

                        def sub(e, g, u):
                            e.wait_ge(S["mx"], count(g, u))
                            v = s[:, u % 2, :, :]
                            e.tensor_tensor(v, v, mx[:, u % 2, :].unsqueeze(2).broadcast_to([P, HEADS, KEYS]), ALU.subtract).then_inc(S["sub"], 1)

                        def norm(e, g, u):
                            e.wait_ge(S["rcp"], count(g, u))
                            v = s[:, u % 2, :, :]
                            e.tensor_tensor(v, v, ri[:, u % 2, :].unsqueeze(2).broadcast_to([P, HEADS, KEYS]), ALU.mult).then_inc(S["prob"], 1)

                        def add_bo(e, g, u):
                            e.wait_ge(S["r_in", u % 2], dma_count2(g, u))
                            e.tensor_tensor(xr[:, u % 2, :], xr[:, u % 2, :], bob[:, :], ALU.add).then_inc(S["xr_bo"], 1)

                        def low_w(e, g, u):
                            e.wait_ge(S["sws"], count(g, u))
                            e.tensor_tensor(swl[:, u % 2, :], sw[:, u % 2, :], swh[:, u % 2, :], ALU.subtract).then_inc(S["swl"], 1)

                        rs_1 = rstd(S["agg"], mv, ve, rs, S["ve"], S["rs"])
                        rs_2 = rstd(S["agg2"], mv2, ve2, rs2, S["ve2"], S["rs2"])

                        def body(g):
                            for u in range(N):
                                step(pool, g, u, 4, rs_1)
                                step(pool, g, u, 1, norm)
                                step(pool, g, u, -1, rs_2)
                                step(pool, g, u, 0, add_bo)
                                step(pool, g, u, 2, sub)
                                step(pool, g, u, 0, low_w)
                        groups(pool, SUB // N, body, peel_last=1)

                    @block.vector
                    def _(dve):
                        dve.wait_ge(S["const_in"], 48)
                        dve.tensor_scalar(srcf[:, :], srcb[:, :], 0.0, None, ALU.not_equal).then_inc(S["src_neg"], 1)
                        dve.wait_ge(S["src_neg"], 1)

                        def lo_p(e, g, u):
                            e.wait_ge(S["pTh"], count(g, u))
                            e.tensor_tensor(pTl[:, :, :], pP[:, :].rearrange("p (k n) -> p k n", k=PAIRS), pTh[:, :, :], ALU.subtract).then_inc(S["pTl"], 1)

                        def stats(e, g, u):
                            e.wait_ge(S["x_in", u], dma_count(g))
                            e.bn_stats(st[:, u % 2, :], xb[:, u, :]).then_inc(S["stats"], 1)

                        def stats_done(e, g, u):
                            e.wait_ge(S["stats"], count(g, u))

                        def aggregate(e, g, u):
                            e.bn_aggr(mv[:, u % 2, :], st[:, u % 2, :]).then_inc(S["agg"], 1)

                        def stats2_done(e, g, u):
                            e.wait_ge(S["stats2"], count(g, u))

                        def aggregate2(e, g, u):
                            e.bn_aggr(mv2[:, u % 2, :], st2[:, u % 2, :]).then_inc(S["agg2"], 1)

                        def sums(e, g, u):
                            e.wait_ge(S["exp"], count(g, u))
                            e.tensor_reduce(sm[:, u % 2, :], s[:, u % 2, :, :], AX.X, ALU.add).then_inc(S["sum"], 1)
                            e.wait_ge(S["sum"], count(g, u))
                            e.reciprocal(mx[:, u % 2, :], sm[:, u % 2, :]).then_inc(S["sum2"], 1)
                            e.wait_ge(S["sum2"], count(g, u))
                            e.tensor_scalar(ri[:, u % 2, :], mx[:, u % 2, :], P_SCALE, None, ALU.mult).then_inc(S["rcp"], 1)

                        def residual(e, g, u):
                            e.wait_ge(S["att"], count(g, u))
                            e.wait_ge(S["xr_bo"], count(g, u))
                            if not isinstance(g, int) or N * g + u >= 2:
                                e.wait_ge(S["x1_out", u % 2], dma_count2(g, u) - 16)
                                e.wait_ge(S["z_out", u % 2], dma_count2(g, u) - 16)
                            e.scalar_tensor_tensor(out=x1[:, u % 2, :], in0=pO[:, :], scalar=sc[:, INV_OUT:INV_OUT + 1], in1=xr[:, u % 2, :],
                                                   op0=ALU.mult, op1=ALU.add).then_inc(S["x1"], 1)
                            e.wait_ge(S["x1"], count(g, u))
                            e.bn_stats(st2[:, u % 2, :], x1[:, u % 2, :]).then_inc(S["stats2"], 1)

                        def normal(e, g, u):
                            e.wait_ge(S["rs"], count(g, u))
                            at_least(e, S["xT"], count(g, u) - 2)
                            e.tensor_scalar(xn[:, u % 2, :], xb[:, u, :], mv[:, u % 2, 0:1], rs[:, u % 2, :], ALU.subtract, ALU.mult).then_inc(S["xn"], 1)

                        def masked(e, g, u):
                            e.wait_ge(S["m_in", u], dma_count(g))
                            b = (N * g + u) // (SUB // BATCH)
                            e.scalar_tensor_tensor(out=keep[:, :], in0=tg[:, u, :], scalar=0.0, in1=srcf[:, bass.ds(b * KEYS, KEYS)],
                                                   op0=ALU.not_equal, op1=ALU.mult).then_inc(S["keep"], 1)
                            e.wait_ge(S["keep"], count(g, u))
                            e.tensor_scalar(neg[:, u % 2, :], keep[:, :], 1.0, NEG, ALU.subtract, ALU.mult).then_inc(S["neg"], 1)
                            e.wait_ge(S["neg"], count(g, u))
                            e.wait_ge(S["sim"], count(g, u))
                            e.scalar_tensor_tensor(out=s[:, u % 2, :, :], in0=pS[u % 2][:, :].rearrange("p (h k) -> p h k", k=KEYS),
                                                   scalar=sc[:, INV_SIM:INV_SIM + 1],
                                                   in1=neg[:, u % 2, :].unsqueeze(1).broadcast_to([P, HEADS, KEYS]),
                                                   op0=ALU.mult, op1=ALU.add).then_inc(S["smask"], 1)
                            e.wait_ge(S["smask"], count(g, u))
                            e.tensor_reduce(mx[:, u % 2, :], s[:, u % 2, :, :], AX.X, ALU.max).then_inc(S["mx"], 1)

                        def lo_x(e, g, u):
                            e.wait_ge(S["xTh"], count(g, u))
                            e.scalar_tensor_tensor(out=xTl[:, u % 2, :, :], in0=pX[:, :].rearrange("p (k n) -> p k n", k=KC), scalar=LN_SCALE,
                                                   in1=xTh[:, u % 2, :, :], op0=ALU.mult, op1=ALU.subtract).then_inc(S["xTl"], 1)

                        def largest_w(e, g, u):
                            e.wait_ge(S["ew_in", u % 2], 2 * dma_count2(g, u))
                            for c in range(2):
                                e.tensor_reduce(ewm[:, u % 2, c:c + 1], ew[:, u % 2, c, :], AX.X, ALU.max,
                                                apply_absolute_value=True).then_inc(S["ew_max"], 1)
                            e.wait_ge(S["ew_max"], 2 * count(g, u))
                            at_least(e, S["amw"], count(g, u) - 1)
                            e.tensor_tensor(amw[:, 0:2], amw[:, 0:2], ewm[:, u % 2, :], ALU.max).then_inc(S["amw"], 1)

                        def gate(e, g, u):
                            e.wait_ge(S["rs2"], count(g, u))
                            e.tensor_scalar(z[:, u % 2, :], x1[:, u % 2, :], mv2[:, u % 2, 0:1], rs2[:, u % 2, :], ALU.subtract, ALU.mult).then_inc(S["z"], 1)
                            e.wait_ge(S["z"], count(g, u))
                            for k in range(2):
                                if k == 1:
                                    e.wait_ge(S["g0"], count(g, u))
                                e.tensor_tensor_reduce(junk[:, :], z[:, u % 2, :], gw[:, k, :], 1.0, 0.0, ALU.mult, ALU.add, gg[:, u % 2, k:k + 1]).then_inc(S[f"g{k}"], 1)
                            e.wait_ge(S["g1"], count(g, u))
                            e.tensor_scalar(expert1[:, bass.ds(N * g + u, 1)], gg[:, u % 2, 1:2], gg[:, u % 2, 0:1], TIE,
                                            ALU.subtract, ALU.is_gt).then_inc(S["pick1"], 1)

                        def body(g):
                            for u in range(N):
                                step(dve, g, u, 0, lo_p)
                                step(dve, g, u, 4, stats)
                                step(dve, g, u, 4, stats_done)
                                step(dve, g, u, 1, sums)
                                step(dve, g, u, 4, aggregate)
                                step(dve, g, u, -1, residual)
                                step(dve, g, u, -1, stats2_done)
                                step(dve, g, u, 4, normal)
                                step(dve, g, u, -1, aggregate2)
                                step(dve, g, u, 2, masked)
                                step(dve, g, u, 3, lo_x)
                                step(dve, g, u, -1, gate)
                                step(dve, g, u, 0, largest_w)
                        groups(dve, SUB // N, body, peel_last=1)

        with ExitStack() as f:
            wA = weight_set(sb, "A", f)
            wB = weight_set(sb, "B", f)
            cacc = sb("cacc", [P, 2, DM], F32, f)
            inv = sb("inv", [P, SLOT_SUBS], F32, f)
            is1 = sb("is1", [P, SLOT_TILES], F32, f)
            w0_in = f.enter_context(nc.semaphore("w0_in"))
            room = (sb, ps, sc, wA, wB, cacc, inv, is1, w0_in)
            shared_net(nc, room, x1_d, z_d, res_d, (s1_d, s2_d), (e1_d, e2_d), units, w1, w2, sb2, net_scales,
                       (ones, upper, lane, row_id, starts, amw, b1e, b1e_s, b1s, expert1, ident),
                       (A1, A2, (EW1, IEW1, EW2, IEW2, EH, IEH, EA1, EA2), C0, AME, ARE))
            experts(nc, room, z_d, res_d, out, (e1_d, e2_d), b2, (ones, b1e_s, ident), (EA1, EA2))


class Net:

    N = 2
    R = TOK // P
    HR = 4
    LAG = 2

    def __init__(self, nc, tag, count, sb, ps, sc, ident, a1, a2, own):
        self.nc, self.tiles, self.ident = nc, count, ident
        self.a1, self.a2 = sc[:, a1:a1 + 1], sc[:, a2:a2 + 1]
        N, R, HR = self.N, self.R, self.HR
        S = self.S = {n: own.enter_context(nc.semaphore(f"{tag}_{n}")) for n in
                      ("zT", "zTh", "zTl", "h", "hh", "hl", "y", "o", "ob")}
        for n in ("z_in", "r_in", "out"):
            for u in range(N):
                S[n, u] = own.enter_context(nc.semaphore(f"{tag}_{n}{u}"))
        self.zb = sb(f"{tag}_zb", [P, N, R, DM], F32, own)
        self.rb = sb(f"{tag}_rb", [P, N, R, DM], F32, own)
        self.ob = sb(f"{tag}_ob", [P, N, R, DM], F32, own)
        self.zTh = sb(f"{tag}_zTh", [P, N, KC, TOK], F16, own)
        self.zTl = sb(f"{tag}_zTl", [P, N, KC, TOK], F16, own)
        self.hf = sb(f"{tag}_hf", [P, HR, TOK], F32, own)
        self.hh = sb(f"{tag}_hh", [P, HR, TOK], F16, own)
        self.hl = sb(f"{tag}_hl", [P, HR, TOK], F16, own)
        self.pZ = ps(f"{tag}_pZ", [P, R, DM], own)
        self.pH = [ps(f"{tag}_pH{n}", [P, 512], own) for n in range(2)]
        self.pY = [[ps(f"{tag}_pY{u}{r}", [P, DM], own) for r in range(R)] for u in range(N)]

    def tile(self, g, u):
        return self.N * g + u

    def step(self, eng, g, u, d, fn, *more):
        g2, u2 = shift(g, u, d, self.N)
        if live(g2, u2, self.N, self.tiles):
            fn(eng, g2, u2, *more)

    def t_z(self, q, g, u, z_count):
        t = self.tile(g, u)
        q.wait_ge(self.S["z_in", u], z_count * (g + 1))
        at_least(q, self.S["zTl"], t)
        for r in range(self.R):
            for k in range(KC):
                mm = q.transpose(self.pZ[:, r, k * P:(k + 1) * P], self.zb[:, u, r, k * P:(k + 1) * P], self.ident[:, :])
        mm.then_inc(self.S["zT"], 1)

    def first(self, q, g, u, j, weights):
        w1h, w1l = weights[0:2]
        if j == 0:
            q.wait_ge(self.S["zTl"], self.tile(g, u) + 1)
        at_least(q, self.S["hh"], HC * self.tile(g, u) + j - 1)
        n = 0
        for k in range(KC):
            for w, zt in ((w1h, self.zTh), (w1h, self.zTl), (w1l, self.zTh)):
                mm = q.matmul(self.pH[j % 2][:, 0:TOK], w[:, k, j * P:(j + 1) * P], zt[:, u, k, :],
                              start=(n == 0), stop=(n == 3 * KC - 1))
                n += 1
        mm.then_inc(self.S["h"], 1)

    def second(self, q, g, u, j, weights):
        w2h, w2l = weights[2:4]
        if j == 0:
            at_least(q, self.S["o"], self.tile(g, u) - 1)
        q.wait_ge(self.S["hl"], HC * self.tile(g, u) + j + 1)
        for r in range(self.R):
            for n, (h, w) in enumerate(((self.hh, w2h), (self.hh, w2l), (self.hl, w2h))):
                mm = q.matmul(self.pY[u][r][:, :], h[:, j % self.HR, r * P:(r + 1) * P], w[:, j, :],
                              start=(j == 0 and n == 0), stop=(j == HC - 1 and n == 2))
        mm.then_inc(self.S["y"], 1)

    def hi_z(self, q, g, u):
        q.wait_ge(self.S["zT"], self.tile(g, u) + 1)
        at_least(q, self.S["h"], HC * (self.tile(g, u) - 1))
        for r in range(self.R):
            v = q.activation(self.zTh[:, u, :, r * P:(r + 1) * P], self.pZ[:, r, :].rearrange("p (k n) -> p k n", k=KC), ACT.Copy,
                             scale=LN_SCALE)
        v.then_inc(self.S["zTh"], 1)

    def relu(self, q, g, u, j, bias):
        done = HC * self.tile(g, u) + j
        b = bias(u, j)
        q.wait_ge(self.S["h"], done + 1)
        at_least(q, self.S["hl"], done + 1 - self.HR)
        q.activation(self.hf[:, j % self.HR, :], self.pH[j % 2][:, 0:TOK], ACT.Relu, bias=b, scale=self.a1)
        at_least(q, self.S["y"], done + 1 - self.HR)
        q.activation(self.hh[:, j % self.HR, :], self.pH[j % 2][:, 0:TOK], ACT.Relu, bias=b, scale=self.a1).then_inc(self.S["hh"], 1)

    def lo_z(self, q, g, u):
        q.wait_ge(self.S["zTh"], self.tile(g, u) + 1)
        for r in range(self.R):
            v = q.scalar_tensor_tensor(out=self.zTl[:, u, :, r * P:(r + 1) * P], in0=self.pZ[:, r, :].rearrange("p (k n) -> p k n", k=KC),
                                       scalar=LN_SCALE, in1=self.zTh[:, u, :, r * P:(r + 1) * P], op0=ALU.mult, op1=ALU.subtract)
        v.then_inc(self.S["zTl"], 1)

    def lo_h(self, q, g, u, j):
        q.wait_ge(self.S["hh"], HC * self.tile(g, u) + j + 1)
        q.tensor_tensor(self.hl[:, j % self.HR, :], self.hf[:, j % self.HR, :], self.hh[:, j % self.HR, :], ALU.subtract).then_inc(self.S["hl"], 1)

    def result(self, q, g, u, r_count, out_count):
        q.wait_ge(self.S["y"], HC * (self.tile(g, u) + 1))
        q.wait_ge(self.S["r_in", u], r_count * (g + 1))
        if not isinstance(g, int) or g > 0:
            q.wait_ge(self.S["out", u], out_count * g)
        for r in range(self.R):
            v = q.scalar_tensor_tensor(out=self.ob[:, u, r, :], in0=self.pY[u][r][:, :], scalar=self.a2, in1=self.rb[:, u, r, :],
                                       op0=ALU.mult, op1=ALU.add)
        v.then_inc(self.S["o"], 1)


def weight_set(sb, tag, own):
    return (sb(f"w1h{tag}", [P, KC, HID], F16, own), sb(f"w1l{tag}", [P, KC, HID], F16, own),
            sb(f"w2h{tag}", [P, HC, DM], F16, own), sb(f"w2l{tag}", [P, HC, DM], F16, own))


def shared_net(nc, room, x1_d, z_d, res_d, split_s, split_e, units, w1, w2, sb2, net_scales, consts, cols):
    sb, ps, sc, wA, wB, cacc, inv, is1, w0_in = room
    ones, upper, lane, row_id, starts, amw, b1e, b1e_s, b1s, expert1, ident = consts
    A1, A2, ECOLS, C0, AME, ARE = cols
    EW1, EW2 = ECOLS[0], ECOLS[2]
    s1_d, s2_d = split_s
    e1_d, e2_d = split_e
    Q = 4
    with ExitStack() as f:
        net = Net(nc, "s", TILES, sb, ps, sc, ident, A1, A2, f)
        N, S, step = net.N, net.S, net.step

        def sem(n):
            S[n] = f.enter_context(nc.semaphore("s_" + n))

        for n in ("brow_in", "e_am", "e_red", "e_step", "ranks", "sort", "onehot", "placed", "invadd", "eh", "el", "cacc", "rb1"):
            sem(n)
        for q in range(Q):
            sem(f"w1_in{q}")
            sem(f"w2_in{q}")
        for u in range(N):
            sem(f"e_in{u}")
        sem("e_out")
        brow = sb("s_brow", [P, DM], F32, f)
        rb1 = sb("s_rb1", [P, 2 * HC], F32, f)
        er = sb("s_er", [P, N, 2, 2, DM], F32, f)
        eh = sb("s_eh", [P, 2, 2, DM], F16, f)
        el = sb("s_el", [P, 2, 2, DM], F16, f)
        place = sb("s_place", [P, 2, SUB], F32, f)
        work = sb("s_work", [P, 6, SUB], F32, f)
        worki = sb("s_worki", [P, 3, SUB], I32, f)
        hot = sb("s_hot", [P, 2, P], F32, f)
        hota = sb("s_hota", [P, 2, SLOT_SUBS], F32, f)
        pI = net.pZ
        pR = pI[:, 1, 0:2 * SUB]
        pV = pI[:, 1, 0:SLOT_SUBS]
        EXP_STEPS = 18
        BF = 12

        def rows(t, g, u):
            return t[bass.ds((N * g + u) * TOK, TOK), :].rearrange("(r p) n -> p r n", p=P)

        with nc.Block() as block:
            @block.sync
            def _(sp):
                for q in range(Q):
                    n = HID // Q
                    for i in range(2):
                        sp.dma_start(wA[i][:, :, q * n:(q + 1) * n], s1_d[i].rearrange("(k p) n -> p k n", p=P)[:, :, q * n:(q + 1) * n]).then_inc(S[f"w1_in{q}"], 16)
                    if q == 0:
                        sp.dma_start(net.zb[:, 0, :, :], rows(z_d, 0, 0)).then_inc(S["z_in", 0], 16)
                        sp.dma_start(net.zb[:, 1, :, :], rows(z_d, 0, 1)).then_inc(S["z_in", 1], 16)
                    n = HC // Q
                    for i in range(2):
                        sp.dma_start(wA[2 + i][:, q * n:(q + 1) * n, :], s2_d[i].rearrange("(j p) n -> p j n", p=P)[:, q * n:(q + 1) * n, :]).then_inc(S[f"w2_in{q}"], 16)
                    if q == 0:
                        sp.dma_start(brow[:, :], sb2.partition_broadcast(P)).then_inc(S["brow_in"], 16)

                def load_z(q, g, u):
                    q.wait_ge(S["zT"], net.tile(g, u) - 1)
                    q.dma_start(net.zb[:, u, :, :], rows(z_d, g, u)).then_inc(S["z_in", u], 16)

                def load_r(q, g, u):
                    at_least(q, S["o"], net.tile(g, u) - 1)
                    q.dma_start(net.rb[:, u, :, :], rows(x1_d, g, u)).then_inc(S["r_in", u], 16)

                def store(q, g, u):
                    wait_apart(q, S["ob"], net.tile(g, u) + 1)
                    q.dma_start(rows(res_d, g, u), net.ob[:, u, :, :]).then_inc(S["out", u], 16)

                def load_e(q, g, u):
                    wait_apart(q, S["el"], 2 * (net.tile(g, u) - 1))
                    for i, w in enumerate((w1, w2)):
                        q.dma_start(er[:, u, i, :, :], rows(units(w), g, u)).then_inc(S[f"e_in{u}"], 16)

                def store_e(q, g, u):
                    wait_apart(q, S["el"], 2 * net.tile(g, u) + 2)
                    for i, d in enumerate((e1_d, e2_d)):
                        q.dma_start(rows(units(d[0]), g, u), eh[:, i, :, :]).then_inc(S["e_out"], 16)
                        q.dma_start(rows(units(d[1]), g, u), el[:, i, :, :]).then_inc(S["e_out"], 16)

                def body(g):
                    if isinstance(g, int) and g == TILES // N - 1:
                        load_set(nc, sp, wB, e1_d, e2_d, 0, w0_in)
                    for u in range(N):
                        if not isinstance(g, int) or g >= 0:
                            step(sp, g, u, 2, load_z)
                        step(sp, g, u, 1, load_r)
                        step(sp, g, u, 1, load_e)
                        step(sp, g, u, -1, store)
                        step(sp, g, u, 0, store_e)
                groups(sp, TILES // N, body)
                for u in range(N):
                    sp.wait_ge(S["out", u], 16 * TILES // N)
                sp.wait_ge(S["e_out"], 64 * TILES)

            @block.gpsimd
            def _(pool):
                pool.memset(cacc[:, :, :], 0.0).then_inc(S["cacc"], 1)
                pool.memset(inv[:, :], 0.0).then_inc(S["invadd"], 1)
                pool.wait_ge(S["e_am"], 1)
                pool.partition_all_reduce(sc[:, ARE:ARE + 3], sc[:, AME:AME + 3], P, RMAX).then_inc(S["e_red"], 1)
                pool.wait_ge(S["brow_in"], 16)

                def bias(q, g, u):
                    q.wait_ge(S["o"], net.tile(g, u) + 1)
                    for r in range(net.R):
                        v = q.tensor_tensor(net.ob[:, u, r, :], net.ob[:, u, r, :], brow[:, :], ALU.add)
                    v.then_inc(S["ob"], 1)

                def body(g):
                    for u in range(N):
                        step(pool, g, u, -1, bias)
                groups(pool, TILES // N, body)

            @block.tensor
            def _(pe):
                def place_rows(q, g, u):
                    t = net.tile(g, u)
                    q.wait_ge(S["onehot"], t + 1)
                    q.wait_ge(S["invadd"], t + 1)
                    if not isinstance(g, int) or t + 3 <= TILES:
                        q.wait_ge(S["zTl"], t + 3)
                    for r in range(2):
                        mm = q.matmul(pV, hot[:, r, :], hota[:, r, :], start=(r == 0), stop=(r == 1))
                    mm.then_inc(S["placed"], 1)

                def first(q, g, u, j):
                    if isinstance(g, int) and g == 0 and u == 0 and j % (HC // Q) == 0:
                        q.wait_ge(S[f"w1_in{j * Q // HC}"], 32)
                    net.first(q, g, u, j, wA)

                def second(q, g, u, j):
                    if isinstance(g, int) and g == 0 and u == 0 and j % (HC // Q) == 0:
                        q.wait_ge(S[f"w2_in{j * Q // HC}"], 32)
                    net.second(q, g, u, j, wA)

                def t_z(q, g, u):
                    if isinstance(g, int) and g == 1 and u == 0:
                        q.wait_ge(S["sort"], 2)
                    at_least(q, S["invadd"], net.tile(g, u) - 1)
                    net.t_z(q, g, u, 16)

                def body(g):
                    for u in range(N):
                        for j in range(HC):
                            step(pe, g, u, 0, first, j)
                            if j >= net.LAG:
                                step(pe, g, u, 0, second, j - net.LAG)
                            else:
                                step(pe, g, u, -1, second, j - net.LAG + HC)
                            if j == 9:
                                step(pe, g, u, 1, t_z)
                            if j == 12 and isinstance(g, int) and g == 0 and u == 0:
                                pe.wait_ge(S["zTl"], 2)
                                pe.matmul(pR[:, 0:SUB], upper[:, :], expert1[:, :], start=True, stop=True)
                                pe.matmul(pR[:, SUB:2 * SUB], ones[:, :], expert1[:, :], start=True, stop=True).then_inc(S["ranks"], 1)
                            if j == 14:
                                step(pe, g, u, -1, place_rows)
                groups(pe, TILES // N, body)

            @block.scalar
            def _(act):
                def split_hi(q, g, u, i):
                    t = net.tile(g, u)
                    q.wait_ge(S[f"e_in{u}"], 32 * (g + 1))
                    if not isinstance(g, int) or t > 0:
                        q.wait_ge(S["e_out"], 64 * t)
                    q.activation(eh[:, i, :, :], er[:, u, i, :, :], ACT.Copy, scale=sc[:, (EW1, EW2)[i]:(EW1, EW2)[i] + 1]).then_inc(S["eh"], 1)

                def body(g):
                    for u in range(N):
                        for j in range(HC):
                            step(act, g, u, 0, net.relu, j, lambda u, j: b1s[:, j:j + 1])
                            if j == 9:
                                step(act, g, u, 1, net.hi_z)
                            if j in (BF, BF + 2):
                                if isinstance(g, int) and g == 0 and u == 0 and j == BF:
                                    act.wait_ge(S["e_step"], EXP_STEPS)
                                step(act, g, u, 0, split_hi, (j - BF) // 2)
                groups(act, TILES // N, body)

            def linker(dve, sem):
                steps = [0]

                def link(ins):
                    steps[0] += 1
                    ins.then_inc(sem, 1)
                    dve.wait_ge(sem, steps[0])
                return link, steps

            @block.vector
            def _(dve):
                def expert_scales():
                    dve.wait_ge(S["e_red"], 1)
                    link, steps = linker(dve, S["e_step"])
                    net_scales(link, dve, sc[:, ARE:ARE + 3], b1e[:, :], b1e_s[:, :, :].rearrange("p e j -> p (e j)"), ECOLS)
                    assert steps[0] == EXP_STEPS, steps[0]

                def slots():
                    link, _ = linker(dve, S["sort"])
                    dve.wait_ge(S["ranks"], 1)
                    before, total, run, other, slot = (work[:, n, :] for n in range(5))
                    link(dve.tensor_copy(before, pR[:, 0:SUB]))
                    link(dve.tensor_copy(total, pR[:, SUB:2 * SUB]))
                    link(dve.tensor_copy(run, total))
                    d = 1
                    while d < SUB:
                        link(dve.tensor_copy(other[:, 0:d], run[:, 0:d]))
                        link(dve.tensor_tensor(other[:, d:SUB], run[:, d:SUB], run[:, 0:SUB - d], ALU.add))
                        run, other = other, run
                        d *= 2
                    count1 = run[:, SUB - 1:SUB]
                    link(dve.tensor_scalar(is1[:, :], starts[:, :], count1, float(ROWS), ALU.add, ALU.is_ge))
                    link(dve.tensor_tensor(other, run, total, ALU.subtract))
                    link(dve.tensor_tensor(before, before, other, ALU.add))
                    link(dve.tensor_scalar(slot, before, -1.0, float(SLOTS - 1), ALU.mult, ALU.add))
                    link(dve.tensor_tensor(other, row_id[:, :], before, ALU.subtract))
                    link(dve.tensor_scalar(other, other, float(ROWS), None, ALU.add))
                    link(dve.tensor_tensor(slot, slot, other, ALU.subtract))
                    link(dve.tensor_tensor(slot, slot, expert1[:, :], ALU.mult))
                    link(dve.tensor_tensor(slot, slot, other, ALU.add))
                    link(dve.tensor_copy(worki[:, 0, :], slot))
                    link(dve.tensor_scalar(worki[:, 1, :], worki[:, 0, :], P - 1, None, ALU.bitwise_and))
                    link(dve.tensor_scalar(worki[:, 2, :], worki[:, 0, :], 7, None, ALU.logical_shift_right))
                    link(dve.tensor_copy(place[:, 0, :], worki[:, 1, :]))
                    link(dve.tensor_copy(place[:, 1, :], worki[:, 2, :]))

                def one_hot(q, g, u):
                    t = net.tile(g, u)
                    at_least(q, S["placed"], t)
                    for r in range(2):
                        c = bass.ds(t * 2 + r, 1)
                        q.tensor_scalar(hot[:, r, :], lane[:, :], place[:, 0, c], None, ALU.is_equal)
                        v = q.tensor_scalar(hota[:, r, :], lane[:, 0:SLOT_SUBS], place[:, 1, c], row_id[:, c], ALU.is_equal, ALU.mult)
                    v.then_inc(S["onehot"], 1)

                def add_placed(q, g, u):
                    q.wait_ge(S["placed"], net.tile(g, u) + 1)
                    q.tensor_tensor(inv[:, :], pV, inv[:, :], ALU.add).then_inc(S["invadd"], 1)

                def split_lo(q, g, u, i):
                    t = net.tile(g, u)
                    q.wait_ge(S["eh"], 2 * t + i + 1)
                    q.scalar_tensor_tensor(out=el[:, i, :, :], in0=er[:, u, i, :, :], scalar=sc[:, (EW1, EW2)[i]:(EW1, EW2)[i] + 1],
                                           in1=eh[:, i, :, :], op0=ALU.mult, op1=ALU.subtract).then_inc(S["el"], 1)

                def idle_expert(q, g, u):
                    t = net.tile(g, u)
                    for c in range(2):
                        q.wait_ge(S["cacc"], 2 * t + c + 1)
                        e = bass.ds(t // (TILES // 2), 1)
                        v = cacc[:, e, :].rearrange("p e n -> p (e n)")
                        q.scalar_tensor_tensor(out=v, in0=er[:, u, 1, c, :], scalar=rb1[:, bass.ds(2 * t + c, 1)], in1=v,
                                               op0=ALU.mult, op1=ALU.add).then_inc(S["cacc"], 1)

                def body(g):
                    for u in range(N):
                        for j in range(HC):
                            step(dve, g, u, 0, net.lo_h, j)
                            if j == 1:
                                step(dve, g, u, -2, add_placed)
                            if j == 3:
                                step(dve, g, u, -1, net.result, 16, 16)
                            if j == 4 and isinstance(g, int) and g == 0 and u == 0:
                                expert_scales()
                            if j == 3 and isinstance(g, int) and g == 0 and u == 1:
                                slots()
                            if j == 6:
                                step(dve, g, u, -1, one_hot)
                            if j == 9:
                                step(dve, g, u, 1, net.lo_z)
                            if j in (BF, BF + 2):
                                step(dve, g, u, 0, split_lo, (j - BF) // 2)
                            if j == BF + 1:
                                step(dve, g, u, 0, idle_expert)
                dve.tensor_copy(sc[:, AME:AME + 2], amw[:, 0:2])
                dve.tensor_scalar(rb1[:, :], b1e[:, :], 0.0, None, ALU.max).then_inc(S["rb1"], 1)
                dve.tensor_reduce(sc[:, AME + 2:AME + 3], b1e[:, :], AX.X, ALU.max, apply_absolute_value=True).then_inc(S["e_am"], 1)
                dve.wait_ge(S["rb1"], 1)
                groups(dve, TILES // N, body)


def load_set(nc, q, dst, e1_d, e2_d, e, done):
    for i in range(2):
        q.dma_start(dst[i][:, :, :], e1_d[i, e].rearrange("(k p) n -> p k n", p=P)).then_inc(done, 16)
        q.dma_start(dst[2 + i][:, :, :], e2_d[i, e].rearrange("(j p) n -> p j n", p=P)).then_inc(done, 16)


def experts(nc, room, z_d, res_d, out, split_e, b2, consts, cols):
    sb, ps, sc, wA, wB, cacc, inv, is1, w0_in = room
    ones, b1e_s, ident = consts
    e1_d, e2_d = split_e
    with ExitStack() as f:
        net = Net(nc, "e", SLOT_TILES, sb, ps, sc, ident, *cols, f)
        N, S, step, R = net.N, net.S, net.step, net.R
        for n in ("w1_in", "b2_in", "cleared", "is0", "flags", "idle", "idle_row", "pick_z", "pick_r", "pick_o", "bias", "sel0", "sel", "b2s", "bias0"):
            S[n] = f.enter_context(nc.semaphore("e_" + n))
        b2r = sb("e_b2r", [P, 2, DM], F32, f)
        is0 = sb("e_is0", [P, SLOT_TILES], F32, f)
        flags = sb("e_flags", [P, SLOT_TILES], I32, f)
        iz = sb("e_iz", [P, N, R], I32, f)
        ir = sb("e_ir", [P, N, R], I32, f)
        io = sb("e_io", [P, N, R], I32, f)
        idle = sb("e_idle", [P, 2, DM], F32, f)
        sel = sb("e_sel", [P, N, DM], F32, f)
        bsel = sb("e_bsel", [P, N, HC], F32, f)

        with nc.Block() as block:
            @block.sync
            def _(sp):
                sp.dma_start(b2r[:, :, :].rearrange("p e n -> p (e n)"), b2.rearrange("e n -> (e n)").partition_broadcast(P)).then_inc(S["b2_in"], 16)
                load_set(nc, sp, wA, e1_d, e2_d, 1, S["w1_in"])

            @block.gpsimd
            def _(pool):
                pool.memset(net.zb[:, :, :, :], 0.0)
                pool.memset(net.rb[:, :, :, :], 0.0).then_inc(S["cleared"], 1)

                def gather_z(q, g, u):
                    wait_apart(q, S["pick_z"], net.tile(g, u) + 1)
                    for r in range(R):
                        q.indirect_dma_start(net.zb[:, u, r, :], None, z_d, bass.IndirectOffsetOnAxis(ap=iz[:, u, r:r + 1], axis=0),
                                             bounds_check=ROWS - 1, oob_is_err=False).then_inc(S["z_in", u], 16)

                def gather_r(q, g, u):
                    wait_apart(q, S["pick_r"], net.tile(g, u) + 1)
                    for r in range(R):
                        q.indirect_dma_start(net.rb[:, u, r, :], None, res_d, bass.IndirectOffsetOnAxis(ap=ir[:, u, r:r + 1], axis=0),
                                             bounds_check=ROWS - 1, oob_is_err=False).then_inc(S["r_in", u], 16)

                def add_idle(q, g, u):
                    q.wait_ge(S["sel"], net.tile(g, u) + 1)
                    q.wait_ge(S["o"], net.tile(g, u) + 1)
                    for r in range(R):
                        v = q.tensor_tensor(net.ob[:, u, r, :], net.ob[:, u, r, :], sel[:, u, :], ALU.add)
                    v.then_inc(S["ob"], 1)

                def scatter(q, g, u):
                    wait_apart(q, S["ob"], net.tile(g, u) + 1)
                    for r in range(R):
                        q.indirect_dma_start(out, bass.IndirectOffsetOnAxis(ap=io[:, u, r:r + 1], axis=0), net.ob[:, u, r, :], None,
                                             bounds_check=ROWS - 1, oob_is_err=False).then_inc(S["out", u], 16)

                def body(g):
                    for u in range(N):
                        step(pool, g, u, 1, gather_z)
                        step(pool, g, u, -1, add_idle)
                        step(pool, g, u, -1, scatter)
                        step(pool, g, u, 1, gather_r)
                pool.wait_ge(S["cleared"], 1)
                groups(pool, TILES // N + 1, body)
                pool.wait_ge(S["out", 0], 32 * (TILES // N + 1))
                pool.wait_ge(S["out", 1], 32 * (TILES // N))

            @block.tensor
            def _(pe):
                def tile(q, g, u, weights, loaded):
                    q.wait_ge(loaded, 64)
                    for j in range(HC + net.LAG):
                        if j < HC:
                            net.first(q, g, u, j, weights)
                        else:
                            if j == HC:
                                step(q, g, u, 1, net.t_z, 32)
                        if j >= net.LAG:
                            net.second(q, g, u, j - net.LAG, weights)

                def by_expert(q, g, u):
                    e = q.value_load(flags[0:1, bass.ds(net.tile(g, u), 1)], min_val=0, max_val=1)
                    with q.If(e == 0):
                        tile(q, g, u, wB, w0_in)
                    with q.Else():
                        tile(q, g, u, wA, S["w1_in"])

                def body(g):
                    for u in range(N):
                        if isinstance(g, int) and g == 0 and u == 1:
                            pe.wait_ge(S["idle_row"], 2)
                        step(pe, g, u, 0, by_expert)

                for e in range(2):
                    pe.matmul(net.pY[1][e][:, :], ones[:, :], cacc[:, 1 - e, :], start=True, stop=True).then_inc(S["idle"], 1)
                net.t_z(pe, 0, 0, 32)
                pe.wait_ge(S["flags"], 1)
                groups(pe, TILES // N + 1, body)

            @block.scalar
            def _(act):
                def body(g):
                    for u in range(N):
                        for j in range(HC):
                            if j == 0:
                                step(act, g, u, 0, lambda q, g, u: q.wait_ge(S["bias"], net.tile(g, u) + 1))
                            step(act, g, u, 0, net.relu, j, lambda u, j: bsel[:, u, j:j + 1])
                        step(act, g, u, 1, net.hi_z)
                groups(act, TILES // N + 1, body)

            @block.vector
            def _(dve):
                def pick(dst, done, free):
                    def fn(q, g, u):
                        free(q, g, u)
                        q.tensor_scalar(dst[:, u, :], inv[:, bass.ds(net.tile(g, u) * R, R)], float(ROWS), None, ALU.add).then_inc(done, 1)
                    return fn

                def out_before(q, g, u):
                    if not isinstance(g, int) or g > 0:
                        q.wait_ge(S["out", u], 32 * g)

                pick_z = pick(iz, S["pick_z"], lambda q, g, u: at_least(q, S["zT"], net.tile(g, u) - 1))
                pick_r = pick(ir, S["pick_r"], lambda q, g, u: at_least(q, S["o"], net.tile(g, u) - 1))
                pick_o = pick(io, S["pick_o"], out_before)

                def pick_bias(q, g, u):
                    at_least(q, S["hh"], HC * (net.tile(g, u) - 1))
                    t = bass.ds(net.tile(g, u), 1)
                    q.tensor_scalar(bsel[:, u, :], b1e_s[:, 0, :], is0[:, t], None, ALU.mult).then_inc(S["bias0"], 1)
                    q.wait_ge(S["bias0"], net.tile(g, u) + 1)
                    q.scalar_tensor_tensor(out=bsel[:, u, :], in0=b1e_s[:, 1, :], scalar=is1[:, t], in1=bsel[:, u, :],
                                           op0=ALU.mult, op1=ALU.add).then_inc(S["bias"], 1)

                def pick_idle(q, g, u):
                    at_least(q, S["ob"], net.tile(g, u) - 1)
                    t = bass.ds(net.tile(g, u), 1)
                    q.tensor_scalar(sel[:, u, :], idle[:, 0, :], is0[:, t], None, ALU.mult).then_inc(S["sel0"], 1)
                    q.wait_ge(S["sel0"], net.tile(g, u) + 1)
                    q.scalar_tensor_tensor(out=sel[:, u, :], in0=idle[:, 1, :], scalar=is1[:, t], in1=sel[:, u, :],
                                           op0=ALU.mult, op1=ALU.add).then_inc(S["sel"], 1)

                def idle_rows():
                    dve.wait_ge(S["b2_in"], 16)
                    dve.tensor_tensor(b2r[:, 0, :], b2r[:, 0, :], b2r[:, 1, :], ALU.add).then_inc(S["b2s"], 1)
                    dve.wait_ge(S["b2s"], 1)
                    dve.wait_ge(S["idle"], 2)
                    for e in range(2):
                        dve.tensor_tensor(idle[:, e, :], net.pY[1][e][:, :], b2r[:, 0, :], ALU.add).then_inc(S["idle_row"], 1)
                    dve.wait_ge(S["idle_row"], 2)

                def body(g):
                    for u in range(N):
                        step(dve, g, u, 1, pick_z)
                        step(dve, g, u, 0, pick_o)
                        for j in range(HC):
                            step(dve, g, u, 0, net.lo_h, j)
                            if j == 3:
                                step(dve, g, u, -1, net.result, 32, 32)
                                step(dve, g, u, 1, pick_r)
                            if j == 5 and isinstance(g, int) and g == 0 and u == 0:
                                idle_rows()
                            if j == 6:
                                step(dve, g, u, 1, pick_bias)
                            if j == 8:
                                step(dve, g, u, 0, pick_idle)
                        step(dve, g, u, 1, net.lo_z)

                dve.tensor_copy(flags[:, :], is1[:, :]).then_inc(S["flags"], 1)
                dve.tensor_scalar(is0[:, :], is1[:, :], -1.0, 1.0, ALU.mult, ALU.add).then_inc(S["is0"], 1)
                dve.wait_ge(S["is0"], 1)
                groups(dve, TILES // N + 1, body)


def kernel(**inputs):
    import numpy as np
    import concourse.bacc as bacc
    from concourse.bass_utils import run_bass_kernel_spmd

    nc = bacc.Bacc("TRN2", target_bir_lowering=False, num_devices=1)
    a = {k: np.asarray(v) for k, v in inputs.items()}
    laid = {
        "x": a["x"].reshape(ROWS, DM),
        "ctxT": a["ctx_1024"].reshape(BATCH * KEYS, DM).T,
        "tgt": a["mask_Bx1xSxS2_ik0"].reshape(ROWS, KEYS),
        "src": a["mask_Bx1xS2_bk0"].reshape(BATCH * KEYS),
        "wq": a["L0_xattn_Wq"], "wkT": a["L0_xattn_Wk"].T, "wvT": a["L0_xattn_Wv"].T, "woT": a["L0_xattn_Wo"].T,
        "bo": a["L0_xattn_bo"], "gate_w": a["L0_ffn_gate_w"], "w1": a["L0_ffn_w1"], "b1": a["L0_ffn_b1"],
        "w2": a["L0_ffn_w2"], "b2": a["L0_ffn_b2"], "sw1": a["L0_ffn_sw1"], "sb1": a["L0_ffn_sb1"],
        "sw2": a["L0_ffn_sw2"], "sb2": a["L0_ffn_sb2"],
    }
    arrays, args = {}, {}
    for name, v in laid.items():
        v = np.ascontiguousarray(v)
        arrays[f"in_{name}"] = v
        args[name] = nc.dram_tensor(f"in_{name}", v.shape, mybir.dt.from_np(v.dtype), kind="ExternalInput").ap()
    out = nc.dram_tensor("out_0", (ROWS, DM), F32, kind="ExternalOutput").ap()
    xattn_ffn(nc, out=out, **args)
    r = run_bass_kernel_spmd(nc, [arrays], core_ids=[0])
    return r.results[0]["out_0"].reshape(BATCH, SEQ, DM)
```

```python
from contextlib import ExitStack

import numpy as np
import concourse.bass as bass
from concourse import mybir

F32 = mybir.dt.float32
F16 = mybir.dt.float16
I32 = mybir.dt.int32
U8 = mybir.dt.uint8
ALU = mybir.AluOpType
ACT = mybir.ActivationFunctionType
AX = mybir.AxisListType
RMAX = bass.bass_isa.ReduceOp.max

P = 128
BATCH, SEQ, DM = 4, 1024, 512
KEYS, HEADS, DH = 64, 16, 64
INNER = HEADS * DH
HID = 2048
ROWS = BATCH * SEQ
KC = DM // P
PAIRS = HEADS // 2
HC = HID // P
HK = HEADS * KEYS
SUB = ROWS // P
TOK = 256
TILES = ROWS // TOK
SLOTS = ROWS + P
SLOT_SUBS = SLOTS // P
SLOT_TILES = TILES + 1
HALF = TILES
SCALE = DH ** -0.5
NEG = float(3.4028234663852886e38)
EPS = 1e-5
LN_SCALE = 2.0 ** 11
P_SCALE = 2.0 ** 15
TIE = 2.0 ** -25
EXP_FIELD = 0x7F800000
MANT = 1 << 23


def shift(g, u, d, n):
    return g + (u + d) // n, (u + d) % n


def live(g, u, n, count):
    return not isinstance(g, int) or 0 <= n * g + u < count


def at_least(eng, sem, value):
    if not isinstance(value, int) or value > 0:
        eng.wait_ge(sem, value)


def wait_apart(eng, sem, count):
    if isinstance(count, int):
        at_least(eng, sem, count)
    else:
        count = eng.to_reg(count)
        eng.wait_ge(sem, 1)
        eng.wait_ge(sem, count)


def groups(eng, n, body, peel_last=1):
    for g in (-1, 0, 1):
        body(g)
    with eng.Fori(2, n - peel_last) as g:
        body(g)
    for g in range(n - peel_last, n + 1):
        body(g)


def carve(room):
    word = [0]

    def take(shape, dt=F32):
        words = int(np.prod(shape)) * mybir.dt.size(dt) // 4
        v = room[:, word[0]:word[0] + words]
        word[0] += words
        assert word[0] <= room.shape[1]
        if dt != F32:
            v = v.bitcast(dt)
        if len(shape) == 1:
            return v
        d = "abcd"[:len(shape)]
        return v.rearrange(f"p ({' '.join(d)}) -> p {' '.join(d)}", **dict(zip(d, shape)))
    return take


def xattn_ffn(nc, x, ctxT, tgt, src, wq, wkT, wvT, woT, bo, gate_w, w1, b1, w2, b2, sw1, sb1, sw2, sb2, out):
    x1_d = nc.dram_tensor("x1_scratch", (ROWS, DM), F32, kind="Internal").ap()
    z_d = nc.dram_tensor("z_scratch", (ROWS, DM), F32, kind="Internal").ap()
    res_d = nc.dram_tensor("res_scratch", (ROWS, DM), F32, kind="Internal").ap()
    s1_d = nc.dram_tensor("s1_split", (2, DM, HID), F16, kind="Internal").ap()
    s2_d = nc.dram_tensor("s2_split", (2, HID, DM), F16, kind="Internal").ap()
    e1_d = nc.dram_tensor("e1_split", (2, 2, DM, HID), F16, kind="Internal").ap()
    e2_d = nc.dram_tensor("e2_split", (2, 2, HID, DM), F16, kind="Internal").ap()

    def units(t):
        if len(t.shape) == 3:
            t = t.rearrange("e k n -> (e k) n")
        return t if t.shape[1] == DM else t.rearrange("k (a n) -> (k a) n", n=DM)

    with ExitStack() as ctx:
        def sem(name):
            return ctx.enter_context(nc.semaphore(name))

        def sb(name, shape, dt=F32, where=ctx):
            return where.enter_context(nc.sbuf_tensor(name, shape, dt))

        def ps(name, shape, where):
            return where.enter_context(nc.psum_tensor(name, shape, F32))

        ident = sb("ident", [P, P])
        sc = sb("sc", [P, 48])
        expert1 = sb("expert1", [P, SUB])
        ones = sb("ones", [P, P])
        upper = sb("upper", [P, P])
        lane = sb("lane", [P, P])
        row_id = sb("row_id", [P, SUB])
        starts = sb("starts", [P, SLOT_TILES])
        amw = sb("amw", [P, 4])
        b1e = sb("b1e", [P, 2 * HC])
        b1e_s = sb("b1e_s", [P, 2, HC])
        b1s = sb("b1s", [P, HC])
        (EBITS, SM, IM, SV, IV, INV_SIM, INV_OUT, SW1, IW1, SW2, IW2, SH, IH, A1, A2,
         EW1, IEW1, EW2, IEW2, EH, IEH, EA1, EA2, AME, ARE) = [*range(23), 24, 28]

        def scale_of(link, eng, bound, s, inv):
            n = bound.shape[1]
            e = sc[:, EBITS:EBITS + n].bitcast(I32)
            link(eng.tensor_scalar(bound, bound, 2.0 ** -90, 2.0 ** 90, ALU.max, ALU.min))
            link(eng.tensor_scalar(e, bound.bitcast(I32), EXP_FIELD, None, ALU.bitwise_and))
            link(eng.tensor_scalar(s.bitcast(I32), e, -1.0, float(268 * MANT), ALU.mult, ALU.add))
            link(eng.tensor_scalar(inv.bitcast(I32), e, float(-14 * MANT), None, ALU.add))

        def net_scales(link, eng, largest, b1_in, b1_out, cols):
            S1, I1, S2, I2, H, IHH, O1, O2 = cols

            def col(c):
                return sc[:, c:c + 1]

            link(eng.tensor_copy(col(S1), largest[:, 0:1]))
            scale_of(link, eng, col(S1), col(S1), col(I1))
            link(eng.tensor_copy(col(S2), largest[:, 1:2]))
            scale_of(link, eng, col(S2), col(S2), col(I2))
            link(eng.scalar_tensor_tensor(out=col(H), in0=largest[:, 0:1], scalar=float(DM), in1=largest[:, 2:3], op0=ALU.mult, op1=ALU.add))
            scale_of(link, eng, col(H), col(H), col(IHH))
            link(eng.tensor_scalar(col(O1), col(I1), col(H), 1.0 / LN_SCALE, ALU.mult, ALU.mult))
            link(eng.tensor_scalar(col(O2), col(IHH), col(I2), None, ALU.mult))
            link(eng.tensor_scalar(b1_out, b1_in, col(H), None, ALU.mult))

        room_f = sb("room_f", [P, 4, 8192], F16)
        room_v = sb("room_v", [P, 4, 8192], F16)
        rows_room = sb("rows_room", [P, 4, DM])
        room_a = sb("room_a", [P, 8192])
        banks_a = ctx.enter_context(nc.psum_tensor("banks_a", [P, HK], F32))
        wA = weight_set(room_f)
        wB = weight_set(room_v)
        first_in = {n: sem("s_" + n) for n in ("w1_in0", "w2_in0")}
        snet = Net("s", TILES, sem, sc, ident, A1, A2, room_a, rows_room, banks_a)
        enet = Net("e", SLOT_TILES, sem, sc, ident, EA1, EA2, room_a, rows_room, banks_a, half=HALF)
        stored = {(n, u): sem(f"a_{n}{u}") for n in ("x1_out", "z_out") for u in range(2)}
        with ExitStack() as at:
            fmh, fml = (room_f[:, i:i + 2, :].rearrange("p i n -> p (i n)").rearrange("p (k b n) -> p k b n", k=KC, b=BATCH) for i in (0, 2))
            fvh, fvl = (room_v[:, i:i + 2, :].rearrange("p i n -> p (i n)").rearrange("p (b q n) -> p b q n", b=BATCH, q=PAIRS) for i in (0, 2))
            room_b = sb("room_b", [P, 9216], F32, at)
            slot0 = room_a[:, 0:4096]
            kd = room_a[:, 4096:8192].rearrange("p (q b h k) -> p q b h k", q=PAIRS, b=BATCH, h=2)
            slot1 = room_b[:, 0:4096]
            vd = room_b[:, 4096:8192].rearrange("p (q b h k) -> p q b h k", q=PAIRS, b=BATCH, h=2)
            ctxt = room_b[:, 8192:9216].rearrange("p (k n) -> p k n", k=KC)
            with ExitStack() as a:
                SEEN_V, SEEN_WO, SEEN_S1, SEEN_S2, SEEN_B1 = PAIRS, 2 * PAIRS, 2 * PAIRS + 2, 2 * PAIRS + 10, 2 * PAIRS + 18
                seen = sb("seen", [P, SEEN_B1 + 1], F32, a)
                am = sb("am", [P, 4], F32, a)
                amr = sb("amr", [P, 4], F32, a)
                ams = sb("ams", [P, 3], F32, a)
                amsr = sb("amsr", [P, 3], F32, a)
                b1r = sb("b1r", [P, HC], F32, a)
                raw1, raw2 = (room_v[:, i:i + 2, :].rearrange("p i n -> p (i n)").bitcast(F32) for i in (0, 2))
                (in_ctx, in_wk0, in_wk1, in_wv, in_s1a, in_s1b, in_s2, in_b1, in_wq, in_wo, zeroed, kv_done, kv_out, kv_seen, w_seen,
                 amaxed, reduced, f_done, f_hi, f_lo, linked, s_max, made) = (a.enter_context(nc.semaphore(n)) for n in (
                     "in_ctx", "in_wk0", "in_wk1", "in_wv", "in_s1a", "in_s1b", "in_s2", "in_b1", "in_wq", "in_wo", "zeroed", "kv_done",
                     "kv_out", "kv_seen", "w_seen", "amaxed", "reduced", "f_done", "f_hi", "f_lo", "linked", "s_max", "made"))
                wk_v = slot0.rearrange("p (k e) -> p k e", k=KC)
                wv_v = slot1.rearrange("p (k e) -> p k e", k=KC)
                wq_v = slot0.rearrange("p (q c) -> p q c", q=PAIRS)
                wo_v = slot1.rearrange("p (q c) -> p q c", q=PAIRS)
                NM = KC * PAIRS
                NF = NM + BATCH * PAIRS
                KV = BATCH * KEYS
                LINKS_M, LINKS_V, LINKS = 5, 10, 31

                N = 4
                S = {}

                def sems(*names):
                    for n in names:
                        S[n] = a.enter_context(nc.semaphore("a_" + n))

                sems("const_in", "src_neg", "stats", "rs", "xn", "xT", "xTh", "xTl", "sim", "drop", "neg", "smask", "mx", "sub", "exp",
                     "sum", "rcp", "half_set", "prob", "pT", "pTh", "pTl", "att", "xr_bo", "x1", "stats2", "rs2", "z", "g0", "g1", "pick1",
                     "ve", "ve2", "agg", "agg2")
                for n in ("x_in", "m_in"):
                    for u in range(N):
                        S[n, u] = a.enter_context(nc.semaphore(f"a_{n}{u}"))
                for n in ("r_in", "ew_in", "sw_in", "sw_out"):
                    for u in range(2):
                        S[n, u] = a.enter_context(nc.semaphore(f"a_{n}{u}"))
                for n in ("x1_out", "z_out"):
                    for u in range(2):
                        S[n, u] = stored[n, u]
                sems("ew_max", "amw", "sws", "swh", "swl")

                xb = rows_room
                take = carve(room_a)
                sw = take([2, DM])
                swh = take([2, DM], F16)
                swl = take([2, DM], F16)
                xn = take([2, DM])
                xTh = take([2, KC, P], F16)
                xTl = take([2, KC, P], F16)
                tg = take([4, KEYS], I32)
                drop = take([2, KEYS])
                least = take([KEYS])
                xTf = take([KC, P])
                neg = take([2, KEYS])
                srcb = take([BATCH * KEYS], U8)
                srcf = take([BATCH * KEYS])
                bob = take([DM])
                gw = take([2, DM])
                junk = take([DM])
                take = carve(room_b)
                s = take([2, HEADS, KEYS])
                mx = take([2, HEADS])
                sm = take([2, HEADS])
                ri = take([2, HEADS])
                pTh = take([PAIRS, P], F16)
                pTl = take([PAIRS, P], F16)
                xr = take([2, DM])
                x1 = take([2, DM])
                z = take([2, DM])
                ew = take([2, 2, DM])
                ewm = take([2, 2])
                half = sb("half", [P, 1], F32, a)
                eps = sb("eps", [P, 1], F32, a)
                st = sb("st", [P, 2, 6], F32, a)
                mv = sb("mv", [P, 2, 2], F32, a)
                ve = sb("ve", [P, 2, 1], F32, a)
                rs = sb("rs", [P, 2, 1], F32, a)
                st2 = sb("st2", [P, 2, 6], F32, a)
                mv2 = sb("mv2", [P, 2, 2], F32, a)
                ve2 = sb("ve2", [P, 2, 1], F32, a)
                rs2 = sb("rs2", [P, 2, 1], F32, a)
                gg = sb("gg", [P, 2, 2], F32, a)
                pS = [banks_a, ps("pS1", [P, HK], a)]
                pk = [pS[n // 2][:, (n % 2) * 512:(n % 2 + 1) * 512] for n in range(4)]
                pX = ps("pX", [P, DM], a)
                pP = ps("pP", [P, HK], a)
                pO = ps("pO", [P, DM], a)

                def f_dst(n, m, v):
                    if n < NM:
                        k, q = n // PAIRS, n % PAIRS
                        return m[:, k, :, q * P:(q + 1) * P]
                    b, q = (n - NM) // PAIRS, n % PAIRS
                    return v[:, b, q, :]

                def f_src(n):
                    return pk[n % 4].rearrange("p (b n) -> p b n", b=BATCH) if n < NM else pk[n % 4]

                def count(g, u):
                    return N * g + u + 1

                def dma_count(g):
                    return 16 * g + 16

                def dma_count2(g, u):
                    return 16 * (2 * g + u // 2 + 1)

                def step(eng, g, u, d, fn):
                    g2, u2 = shift(g, u, d, N)
                    if live(g2, u2, N, SUB):
                        fn(eng, g2, u2)

                def rows(t, g, u):
                    return t[bass.ds((N * g + u) * P, P), :]

                def last_tile(g, u):
                    return isinstance(g, int) and N * g + u == SUB - 1

                def first_tile(g, u, d):
                    return isinstance(g, int) and N * g + u + d == 0

                with nc.Block() as block:
                    @block.sync
                    def _(sp):
                        sp.dma_start(ctxt, ctxT.rearrange("(k p) n -> p k n", p=P)).then_inc(in_ctx, 16)
                        wk_in = wkT.rearrange("(k p) n -> p k n", p=P)
                        for h, arrived in enumerate((in_wk0, in_wk1)):
                            c = slice(h * INNER // 2, (h + 1) * INNER // 2)
                            sp.dma_start(wk_v[:, :, c], wk_in[:, :, c]).then_inc(arrived, 16)
                        s1_in = sw1.rearrange("(p k) n -> p (k n)", p=P)
                        sp.dma_start(raw1[:, 0:4096], s1_in[:, 0:4096]).then_inc(in_s1a, 16)
                        sp.dma_start(wv_v, wvT.rearrange("(k p) n -> p k n", p=P)).then_inc(in_wv, 16)
                        sp.dma_start(raw1[:, 4096:8192], s1_in[:, 4096:8192]).then_inc(in_s1b, 16)
                        sp.wait_ge(kv_done, PAIRS)
                        sp.dma_start(wq_v, wq.rearrange("(q p) n -> p q n", p=P)).then_inc(in_wq, 16)
                        sp.dma_start(raw2, sw2.rearrange("(p k) n -> p (k n)", p=P)).then_inc(in_s2, 16)
                        with nc.allow_non_contiguous_dma("biases in columns"):
                            sp.dma_start(b1r[:, :], sb1.rearrange("(j p) -> p j", p=P)).then_inc(in_b1, 16)
                            sp.dma_start(b1e[:, :], b1.rearrange("e (j p) -> p (e j)", p=P)).then_inc(in_b1, 16)
                        sp.wait_ge(kv_done, 2 * PAIRS)
                        sp.dma_start(wo_v, woT.rearrange("(q p) n -> p q n", p=P)).then_inc(in_wo, 16)
                        for u in range(N):
                            sp.dma_start(xb[:, u, :], x[u * P:(u + 1) * P, :]).then_inc(S["x_in", u], 16)
                        sp.wait_ge(f_done, NM)
                        sp.dma_start(srcb[:, :], src.partition_broadcast(P)).then_inc(S["const_in"], 16)
                        sp.dma_start(bob[:, :], bo.partition_broadcast(P)).then_inc(S["const_in"], 16)
                        sp.dma_start(gw[:, :, :].rearrange("p e n -> p (e n)"),
                                     gate_w.rearrange("e n -> (e n)").partition_broadcast(P)).then_inc(S["const_in"], 16)

                        def load_x(e, g, u):
                            at_least(e, S["xn"], count(g, u) - 4)
                            e.dma_start(xb[:, u, :], rows(x, g, u)).then_inc(S["x_in", u], 16)

                        def load_m(e, g, u):
                            at_least(e, S["drop"], count(g, u) - 4)
                            e.dma_start(tg[:, u, :], rows(tgt, g, u)).then_inc(S["m_in", u], 16)

                        def load_r(e, g, u):
                            at_least(e, S["x1"], count(g, u) - 2)
                            e.dma_start(xr[:, u % 2, :], rows(x, g, u)).then_inc(S["r_in", u % 2], 16)

                        def load_w(e, g, u):
                            at_least(e, S["ew_max"], 2 * count(g, u) - 4)
                            e.dma_start(ew[:, u % 2, 0, :], rows(units(w1), g, u)).then_inc(S["ew_in", u % 2], 16)
                            e.dma_start(ew[:, u % 2, 1, :], rows(units(w2), g, u)).then_inc(S["ew_in", u % 2], 16)
                            wait_apart(e, S["swl"], count(g, u) - 2)
                            e.dma_start(sw[:, u % 2, :], sw_rows((sw1, sw2)[u % 2], g, u)).then_inc(S["sw_in", u % 2], 16)

                        def sw_rows(t, g, u):
                            return units(t)[bass.ds((2 * g + u // 2) * P, P), :]

                        def store_w(e, g, u):
                            wait_apart(e, S["swl"], count(g, u))
                            t = (s1_d, s2_d)[u % 2]
                            e.dma_start(sw_rows(t[0], g, u), swh[:, u % 2, :]).then_inc(S["sw_out", u % 2], 16)
                            e.dma_start(sw_rows(t[1], g, u), swl[:, u % 2, :]).then_inc(S["sw_out", u % 2], 16)

                        def store(e, g, u):
                            e.wait_ge(S["x1"], count(g, u))
                            e.dma_start(rows(x1_d, g, u), x1[:, u % 2, :]).then_inc(S["x1_out", u % 2], 16)
                            e.wait_ge(S["z"], count(g, u))
                            e.dma_start(rows(z_d, g, u), z[:, u % 2, :]).then_inc(S["z_out", u % 2], 16)

                        def body(g):
                            for u in range(N):
                                if not isinstance(g, int) or N * g + u + 6 >= N:
                                    step(sp, g, u, 6, load_x)
                                step(sp, g, u, 4, load_m)
                                if first_tile(g, u, 3):
                                    sp.wait_ge(f_done, NF)
                                step(sp, g, u, 1, load_r)
                                step(sp, g, u, -2, store)
                                step(sp, g, u, 3, load_w)
                                step(sp, g, u, 1, store_w)
                                if last_tile(g, u):
                                    load_next()
                        def load_next():
                            sp.wait_ge(S["xn"], SUB)
                            for u in range(2):
                                sp.wait_ge(S["z_out", u], 32)
                            sp.dma_start(Net.rows_buffer(rows_room)[:, 0, :, :], Net.rows(z_d, 0)).then_inc(snet.S["z_in", 0], 16)
                            sp.wait_ge(S["sim"], SUB)
                            for u in range(2):
                                sp.wait_ge(S["sw_out", u], 16 * SUB)
                            load_quarter(sp, wA, s1_d, s2_d, 0, 1, first_in["w1_in0"])
                            load_quarter(sp, wA, s1_d, s2_d, 0, 2, first_in["w2_in0"])
                        groups(sp, SUB // N, body, peel_last=2)

                    @block.tensor
                    def _(pe):
                        def t_x(e, g, u):
                            e.wait_ge(S["xn"], count(g, u))
                            at_least(e, S["xTh"], count(g, u) - 1)
                            for k in range(KC):
                                mm = e.transpose(pX[:, k * P:(k + 1) * P], xn[:, u % 2, k * P:(k + 1) * P], ident[:, :])
                            mm.then_inc(S["xT"], 1)

                        def sim(e, g, u):
                            e.wait_ge(S["xTl"], count(g, u))
                            at_least(e, S["smask"], count(g, u) - 2)
                            b = (N * g + u) // (SUB // BATCH)
                            for h in range(2):
                                n = 0
                                for k in range(KC):
                                    for xt, f in ((xTh, fmh), (xTh, fml), (xTl, fmh)):
                                        mm = e.matmul(pS[u % 2][:, h * 512:(h + 1) * 512], xt[:, u % 2, k, :],
                                                      f[:, k, bass.ds(b, 1), h * 512:(h + 1) * 512],
                                                      start=(n == 0), stop=(n == 3 * KC - 1))
                                        n += 1
                            mm.then_inc(S["sim"], 1)

                        def t_p(e, g, u):
                            e.wait_ge(S["prob"], count(g, u))
                            at_least(e, S["pTl"], count(g, u) - 1)
                            for q in range(PAIRS):
                                mm = e.transpose(pP[:, q * P:(q + 1) * P],
                                                 s[:, u % 2, 2 * q:2 * q + 2, :].rearrange("p h k -> p (h k)"), ident[:, :])
                            mm.then_inc(S["pT"], 1)

                        def attend(e, g, u):
                            e.wait_ge(S["pTl"], count(g, u))
                            at_least(e, S["x1"], count(g, u) - 1)
                            b = (N * g + u) // (SUB // BATCH)
                            n = 0
                            for q in range(PAIRS):
                                for pt, f in ((pTh, fvh), (pTh, fvl), (pTl, fvh)):
                                    mm = e.matmul(pO[:, :], pt[:, q, :], f[:, bass.ds(b, 1), q, :],
                                                  start=(n == 0), stop=(n == 3 * PAIRS - 1))
                                    n += 1
                            mm.then_inc(S["att"], 1)

                        def body(g):
                            for u in range(N):
                                step(pe, g, u, 0, t_p)
                                step(pe, g, u, 2, sim)
                                if not first_tile(g, u, 3):
                                    step(pe, g, u, 3, t_x)
                                if last_tile(g, u):
                                    pe.wait_ge(S["smask"], SUB - 1)
                                    snet.t_z(pe, 0, 0, 16)
                                step(pe, g, u, 0, attend)

                        pe.wait_ge(in_ctx, 16)
                        for n in range(2 * PAIRS):
                            w, q = (wk_v if n < PAIRS else wv_v), n % PAIRS
                            if n in (0, PAIRS // 2, PAIRS):
                                pe.wait_ge({0: in_wk0, PAIRS // 2: in_wk1, PAIRS: in_wv}[n], 16)
                            if n >= 4:
                                pe.wait_ge(kv_out, n - 3)
                            for k in range(KC):
                                mm = pe.matmul(pk[n % 4][:, 0:KV], w[:, k, q * P:(q + 1) * P], ctxt[:, k, :],
                                               start=(k == 0), stop=(k == KC - 1))
                            mm.then_inc(kv_done, 1)
                        pe.wait_ge(kv_out, 2 * PAIRS)
                        pe.wait_ge(in_wq, 16)
                        for n in range(NF):
                            if n == NM:
                                pe.wait_ge(in_wo, 16)
                            if n == NF - 2:
                                pe.wait_ge(made, 2)
                                t_x(pe, 0, 0)
                            if n >= 4:
                                pe.wait_ge(f_lo, n - 3)
                            if n < NM:
                                k, q = n // PAIRS, n % PAIRS
                                mm = pe.matmul(pk[n % 4], wq_v[:, q, k * P:(k + 1) * P],
                                               kd[:, q, :, :, :].rearrange("p b h k -> p (b h k)"), start=True, stop=True)
                            else:
                                b, q = (n - NM) // PAIRS, n % PAIRS
                                mm = pe.matmul(pk[n % 4], vd[:, q, b, :, :].rearrange("p h k -> p (h k)"),
                                               wo_v[:, q, :], start=True, stop=True)
                            mm.then_inc(f_done, 1)
                        pe.wait_ge(f_lo, NF)
                        groups(pe, SUB // N, body, peel_last=1)

                    @block.scalar
                    def _(act):
                        def hi_x(e, g, u):
                            e.wait_ge(S["xT"], count(g, u))
                            at_least(e, S["xTl"], count(g, u) - 1)
                            e.activation(xTf, pX[:, :].rearrange("p (k n) -> p k n", k=KC), ACT.Copy, scale=LN_SCALE)
                            at_least(e, S["sim"], count(g, u) - 2)
                            e.activation(xTh[:, u % 2, :, :], pX[:, :].rearrange("p (k n) -> p k n", k=KC), ACT.Copy, scale=LN_SCALE).then_inc(S["xTh"], 1)

                        def hi_p(e, g, u):
                            e.wait_ge(S["pT"], count(g, u))
                            at_least(e, S["att"], count(g, u) - 1)
                            e.activation(pTh[:, :, :], pP[:, :].rearrange("p (k n) -> p k n", k=PAIRS), ACT.Copy, scale=P_SCALE).then_inc(S["pTh"], 1)

                        def scale_w(e, g, u):
                            s_col = (SW1, SW2)[u % 2]
                            if first_tile(g, u, 0):
                                e.wait_ge(linked, LINKS)
                            e.wait_ge(S["sw_in", u % 2], dma_count2(g, u))
                            at_least(e, S["swl"], count(g, u) - 2)
                            if not isinstance(g, int) or N * g + u >= 2:
                                e.wait_ge(S["sw_out", u % 2], 2 * dma_count2(g, u) - 32)
                            e.activation(swh[:, u % 2, :], sw[:, u % 2, :], ACT.Copy, scale=sc[:, s_col:s_col + 1]).then_inc(S["swh"], 1)
                            e.wait_ge(S["swh"], count(g, u))
                            e.activation(sw[:, u % 2, :], sw[:, u % 2, :], ACT.Copy, scale=sc[:, s_col:s_col + 1]).then_inc(S["sws"], 1)

                        def exp(e, g, u):
                            e.wait_ge(S["sub"], count(g, u))
                            e.activation(s[:, u % 2, :, :], s[:, u % 2, :, :], ACT.Exp).then_inc(S["exp"], 1)

                        for n in range(2 * PAIRS):
                            q, t = n % PAIRS, (kd if n < PAIRS else vd)
                            if n == 0:
                                act.wait_ge(zeroed, 2)
                            act.wait_ge(kv_done, n + 1)
                            v = pk[n % 4][:, 0:KV].rearrange("p (b k) -> p b k", b=BATCH)
                            act.activation(t[0:64, q, :, 0, :], v[0:64], ACT.Copy)
                            act.activation(t[64:128, q, :, 1, :], v[64:128], ACT.Copy).then_inc(kv_out, 1)
                        act.wait_ge(linked, LINKS_M)
                        for n in range(NF):
                            if n == NM:
                                act.wait_ge(linked, LINKS_V)
                            if n >= NM and n % PAIRS == 0:
                                act.wait_ge(w_seen, 10 + 2 * ((n - NM) // PAIRS + 1))
                            if n == NF - 1:
                                hi_x(act, 0, 0)
                            act.wait_ge(f_done, n + 1)
                            c = SM if n < NM else SV
                            act.activation(f_dst(n, fmh, fvh), f_src(n), ACT.Copy, scale=sc[:, c:c + 1]).then_inc(f_hi, 1)

                        def body(g):
                            for u in range(N):
                                step(act, g, u, 0, hi_p)
                                if not first_tile(g, u, 2):
                                    step(act, g, u, 2, scale_w)
                                step(act, g, u, 1, exp)
                                if not first_tile(g, u, 3):
                                    step(act, g, u, 3, hi_x)
                                if first_tile(g, u, 2):
                                    step(act, g, u, 2, scale_w)
                                if last_tile(g, u):
                                    for v in range(2):
                                        act.wait_ge(S["sw_out", v], 16 * SUB)
                                    snet.hi_z(act, 0, 0)
                        groups(act, SUB // N, body, peel_last=1)

                    @block.gpsimd
                    def _(pool):
                        pool.memset(kd, 0.0).then_inc(zeroed, 1)
                        pool.memset(vd, 0.0).then_inc(zeroed, 1)
                        pool.memset(half[:, :], -0.5).then_inc(S["half_set"], 1)
                        pool.memset(eps[:, :], EPS).then_inc(S["half_set"], 1)
                        pool.memset(ident[:, :], 0.0).then_inc(made, 1)
                        pool.wait_ge(made, 1)
                        pool.affine_select(out=ident[:, :], in_=ident[:, :], compare_op=ALU.not_equal, fill=1.0,
                                           base=0, pattern=[[-1, P]], channel_multiplier=1).then_inc(made, 1)
                        pool.memset(ones[:, :], 1.0).then_inc(made, 1)
                        pool.wait_ge(made, 3)
                        pool.affine_select(out=upper[:, :], in_=ones[:, :], compare_op=ALU.is_gt, fill=0.0,
                                           base=0, pattern=[[1, P]], channel_multiplier=-1)
                        pool.iota(lane[:, :], pattern=[[1, P]], base=0, channel_multiplier=0, allow_small_or_imprecise_dtypes=True)
                        pool.iota(row_id[:, :], pattern=[[P, SUB]], base=-ROWS, channel_multiplier=1, allow_small_or_imprecise_dtypes=True)
                        pool.iota(starts[:, :], pattern=[[TOK, SLOT_TILES]], base=P, channel_multiplier=0, allow_small_or_imprecise_dtypes=True)
                        pool.wait_ge(amaxed, 2)
                        pool.partition_all_reduce(amr[:, 0:2], am[:, 0:2], P, RMAX).then_inc(reduced, 1)
                        pool.wait_ge(amaxed, 4)
                        pool.partition_all_reduce(amr[:, 2:4], am[:, 2:4], P, RMAX).then_inc(reduced, 1)
                        pool.wait_ge(s_max, 3)
                        pool.partition_all_reduce(amsr[:, :], ams[:, :], P, RMAX).then_inc(reduced, 1)
                        pool.wait_ge(S["half_set"], 2)

                        def rstd(src_sem, mv, ve, rs, ves, done):
                            def fn(e, g, u):
                                e.wait_ge(src_sem, count(g, u))
                                e.tensor_tensor(ve[:, u % 2, :], mv[:, u % 2, 1:2], eps[:, :], ALU.add).then_inc(ves, 1)
                                e.wait_ge(ves, count(g, u))
                                e.tensor_tensor(rs[:, u % 2, :], ve[:, u % 2, :], half[:, :], ALU.pow).then_inc(done, 1)
                            return fn

                        def sub(e, g, u):
                            e.wait_ge(S["mx"], count(g, u))
                            v = s[:, u % 2, :, :]
                            e.tensor_tensor(v, v, mx[:, u % 2, :].unsqueeze(2).broadcast_to([P, HEADS, KEYS]), ALU.subtract).then_inc(S["sub"], 1)

                        def norm(e, g, u):
                            e.wait_ge(S["rcp"], count(g, u))
                            v = s[:, u % 2, :, :]
                            e.tensor_tensor(v, v, ri[:, u % 2, :].unsqueeze(2).broadcast_to([P, HEADS, KEYS]), ALU.mult).then_inc(S["prob"], 1)

                        def add_bo(e, g, u):
                            e.wait_ge(S["r_in", u % 2], dma_count2(g, u))
                            e.tensor_tensor(xr[:, u % 2, :], xr[:, u % 2, :], bob[:, :], ALU.add).then_inc(S["xr_bo"], 1)

                        def lo_x(e, g, u):
                            e.wait_ge(S["xTh"], count(g, u))
                            e.tensor_tensor(xTl[:, u % 2, :, :], xTf, xTh[:, u % 2, :, :], ALU.subtract).then_inc(S["xTl"], 1)

                        def negate(e, g, u):
                            e.wait_ge(S["drop"], count(g, u))
                            at_least(e, S["smask"], count(g, u) - 2)
                            e.tensor_tensor(neg[:, u % 2, :], drop[:, u % 2, :], least, ALU.mult).then_inc(S["neg"], 1)

                        def low_w(e, g, u):
                            e.wait_ge(S["sws"], count(g, u))
                            e.tensor_tensor(swl[:, u % 2, :], sw[:, u % 2, :], swh[:, u % 2, :], ALU.subtract).then_inc(S["swl"], 1)

                        rs_1 = rstd(S["agg"], mv, ve, rs, S["ve"], S["rs"])
                        rs_2 = rstd(S["agg2"], mv2, ve2, rs2, S["ve2"], S["rs2"])

                        rs_1(pool, 0, 0)
                        pool.memset(least, -NEG).then_inc(S["half_set"], 1)
                        lo_x(pool, 0, 0)
                        pool.wait_ge(S["const_in"], 48)
                        pool.wait_ge(S["half_set"], 3)

                        def body(g):
                            for u in range(N):
                                step(pool, g, u, 2, negate)
                                if not first_tile(g, u, 4):
                                    step(pool, g, u, 4, rs_1)
                                step(pool, g, u, -1, rs_2)
                                step(pool, g, u, 1, norm)
                                if not first_tile(g, u, 3):
                                    step(pool, g, u, 3, lo_x)
                                step(pool, g, u, 0, add_bo)
                                step(pool, g, u, 2, sub)
                                step(pool, g, u, 2, low_w)
                        groups(pool, SUB // N, body, peel_last=1)

                    @block.vector
                    def _(dve):
                        def lo_p(e, g, u):
                            e.wait_ge(S["pTh"], count(g, u))
                            e.scalar_tensor_tensor(out=pTl[:, :, :], in0=pP[:, :].rearrange("p (k n) -> p k n", k=PAIRS), scalar=P_SCALE,
                                                   in1=pTh[:, :, :], op0=ALU.mult, op1=ALU.subtract).then_inc(S["pTl"], 1)

                        def stats(e, g, u):
                            e.wait_ge(S["x_in", u], dma_count(g))
                            e.bn_stats(st[:, u % 2, :], xb[:, u, :]).then_inc(S["stats"], 1)

                        def stats_done(e, g, u):
                            e.wait_ge(S["stats"], count(g, u))

                        def aggregate(e, g, u):
                            e.bn_aggr(mv[:, u % 2, :], st[:, u % 2, :]).then_inc(S["agg"], 1)

                        def stats2_done(e, g, u):
                            e.wait_ge(S["stats2"], count(g, u))

                        def aggregate2(e, g, u):
                            e.bn_aggr(mv2[:, u % 2, :], st2[:, u % 2, :]).then_inc(S["agg2"], 1)

                        def sums(e, g, u):
                            e.wait_ge(S["exp"], count(g, u))
                            e.tensor_reduce(sm[:, u % 2, :], s[:, u % 2, :, :], AX.X, ALU.add).then_inc(S["sum"], 1)
                            e.wait_ge(S["sum"], count(g, u))
                            e.reciprocal(ri[:, u % 2, :], sm[:, u % 2, :]).then_inc(S["rcp"], 1)

                        def residual(e, g, u):
                            e.wait_ge(S["att"], count(g, u))
                            e.wait_ge(S["xr_bo"], count(g, u))
                            if not isinstance(g, int) or N * g + u >= 2:
                                e.wait_ge(S["x1_out", u % 2], dma_count2(g, u) - 16)
                                e.wait_ge(S["z_out", u % 2], dma_count2(g, u) - 16)
                            e.scalar_tensor_tensor(out=x1[:, u % 2, :], in0=pO[:, :], scalar=sc[:, INV_OUT:INV_OUT + 1], in1=xr[:, u % 2, :],
                                                   op0=ALU.mult, op1=ALU.add).then_inc(S["x1"], 1)
                            e.wait_ge(S["x1"], count(g, u))
                            e.bn_stats(st2[:, u % 2, :], x1[:, u % 2, :]).then_inc(S["stats2"], 1)

                        def normal(e, g, u):
                            e.wait_ge(S["rs"], count(g, u))
                            at_least(e, S["xT"], count(g, u) - 2)
                            e.tensor_scalar(xn[:, u % 2, :], xb[:, u, :], mv[:, u % 2, 0:1], rs[:, u % 2, :], ALU.subtract, ALU.mult).then_inc(S["xn"], 1)

                        def dropped(e, g, u):
                            e.wait_ge(S["m_in", u], dma_count(g))
                            at_least(e, S["neg"], count(g, u) - 2)
                            b = (N * g + u) // (SUB // BATCH)
                            e.scalar_tensor_tensor(out=drop[:, u % 2, :], in0=tg[:, u, :], scalar=0.0, in1=srcf[:, bass.ds(b * KEYS, KEYS)],
                                                   op0=ALU.is_equal, op1=ALU.max).then_inc(S["drop"], 1)

                        def masked(e, g, u):
                            e.wait_ge(S["neg"], count(g, u))
                            e.wait_ge(S["sim"], count(g, u))
                            e.scalar_tensor_tensor(out=s[:, u % 2, :, :], in0=pS[u % 2][:, :].rearrange("p (h k) -> p h k", k=KEYS),
                                                   scalar=sc[:, INV_SIM:INV_SIM + 1],
                                                   in1=neg[:, u % 2, :].unsqueeze(1).broadcast_to([P, HEADS, KEYS]),
                                                   op0=ALU.mult, op1=ALU.add).then_inc(S["smask"], 1)
                            e.wait_ge(S["smask"], count(g, u))
                            e.tensor_reduce(mx[:, u % 2, :], s[:, u % 2, :, :], AX.X, ALU.max).then_inc(S["mx"], 1)

                        def largest_w(e, g, u):
                            e.wait_ge(S["ew_in", u % 2], 2 * dma_count2(g, u))
                            for c in range(2):
                                e.tensor_reduce(ewm[:, u % 2, c:c + 1], ew[:, u % 2, c, :], AX.X, ALU.max,
                                                apply_absolute_value=True).then_inc(S["ew_max"], 1)
                            e.wait_ge(S["ew_max"], 2 * count(g, u))
                            at_least(e, S["amw"], count(g, u) - 1)
                            e.tensor_tensor(amw[:, 0:2], amw[:, 0:2], ewm[:, u % 2, :], ALU.max).then_inc(S["amw"], 1)

                        def gate(e, g, u):
                            e.wait_ge(S["rs2"], count(g, u))
                            e.tensor_scalar(z[:, u % 2, :], x1[:, u % 2, :], mv2[:, u % 2, 0:1], rs2[:, u % 2, :], ALU.subtract, ALU.mult).then_inc(S["z"], 1)
                            e.wait_ge(S["z"], count(g, u))
                            for k in range(2):
                                if k == 1:
                                    e.wait_ge(S["g0"], count(g, u))
                                e.tensor_tensor_reduce(junk[:, :], z[:, u % 2, :], gw[:, k, :], 1.0, 0.0, ALU.mult, ALU.add, gg[:, u % 2, k:k + 1]).then_inc(S[f"g{k}"], 1)
                            e.wait_ge(S["g1"], count(g, u))
                            e.tensor_scalar(expert1[:, bass.ds(N * g + u, 1)], gg[:, u % 2, 1:2], gg[:, u % 2, 0:1], TIE,
                                            ALU.subtract, ALU.is_gt).then_inc(S["pick1"], 1)

                        def largest(dst, t, done, arrived=None):
                            if arrived is not None:
                                dve.wait_ge(arrived, 16)
                            dve.tensor_reduce(dst, t, AX.X, ALU.max, apply_absolute_value=True).then_inc(done, 1)

                        def see(c):
                            t = (raw1 if c < 8 else raw2)[:, (c % 8) * 1024:(c % 8 + 1) * 1024]
                            largest(seen[:, SEEN_S1 + c:SEEN_S1 + c + 1], t, w_seen, in_s1a if c < 4 else in_s1b if c < 8 else in_s2)

                        steps = [0]

                        def link(ins):
                            steps[0] += 1
                            ins.then_inc(linked, 1)
                            dve.wait_ge(linked, steps[0])

                        def col(c):
                            return sc[:, c:c + 1]

                        def split(n):
                            dve.wait_ge(f_hi, n + 1)
                            dve.scalar_tensor_tensor(out=f_dst(n, fml, fvl), in0=f_src(n), scalar=col(SM if n < NM else SV),
                                                     in1=f_dst(n, fmh, fvh), op0=ALU.mult, op1=ALU.subtract).then_inc(f_lo, 1)

                        def see_kv(n):
                            dve.wait_ge(kv_out, n + 1)
                            t = (kd if n < PAIRS else vd)[:, n % PAIRS, :, :, :]
                            largest(seen[:, n:n + 1], t.rearrange("p b h k -> p (b h k)"), kv_seen)

                        for n in range(2 * PAIRS - 3):
                            see_kv(n)
                            if n in (4, 5, 6, 7, 8, 9, 10, 11):
                                see(n - 4)
                            if n == 12:
                                largest(am[:, 1:2], slot0, amaxed, in_wq)
                        dve.wait_ge(kv_seen, PAIRS)
                        dve.tensor_reduce(am[:, 0:1], seen[:, 0:SEEN_V], AX.X, ALU.max).then_inc(amaxed, 1)
                        dve.wait_ge(reduced, 1)
                        link(dve.tensor_scalar(col(SM), amr[:, 0:1], amr[:, 1:2], float(DH), ALU.mult, ALU.mult))
                        scale_of(link, dve, col(SM), col(SM), col(IM))
                        assert steps[0] == LINKS_M
                        for n in range(2 * PAIRS - 3, 2 * PAIRS):
                            see_kv(n)
                        for n in range(NM):
                            split(n)
                            if n in (16, 19):
                                h = (n - 16) // 3
                                largest(seen[:, SEEN_WO + h:SEEN_WO + h + 1], slot1[:, h * 2048:(h + 1) * 2048], w_seen, in_wo)
                            if n in (22, 25):
                                see(8 + (n - 22) // 3)
                            if n == 28:
                                dve.wait_ge(kv_seen, 2 * PAIRS)
                                dve.wait_ge(w_seen, 10)
                                dve.tensor_reduce(am[:, 2:3], seen[:, SEEN_V:SEEN_WO], AX.X, ALU.max).then_inc(amaxed, 1)
                                dve.tensor_reduce(am[:, 3:4], seen[:, SEEN_WO:SEEN_S1], AX.X, ALU.max).then_inc(amaxed, 1)
                        dve.wait_ge(reduced, 2)
                        link(dve.tensor_scalar(col(SV), amr[:, 2:3], amr[:, 3:4], float(DH), ALU.mult, ALU.mult))
                        scale_of(link, dve, col(SV), col(SV), col(IV))
                        assert steps[0] == LINKS_V
                        for n in range(NM, NF):
                            i = n - NM
                            split(n)
                            if i < 3 * PAIRS and i % 4 == 1:
                                see(10 + i // 4)
                            if i == 21:
                                dve.wait_ge(in_b1, 32)
                                largest(seen[:, SEEN_B1:SEEN_B1 + 1], b1r[:, :], w_seen)
                                dve.wait_ge(w_seen, 19)
                                for c, (a0, a1) in enumerate(((SEEN_S1, SEEN_S2), (SEEN_S2, SEEN_B1), (SEEN_B1, SEEN_B1 + 1))):
                                    dve.tensor_reduce(ams[:, c:c + 1], seen[:, a0:a1], AX.X, ALU.max).then_inc(s_max, 1)
                            if i == 23:
                                stats(dve, 0, 0)
                                stats_done(dve, 0, 0)
                                aggregate(dve, 0, 0)
                            if i == 25:
                                normal(dve, 0, 0)
                        def other_scales():
                            dve.wait_ge(reduced, 3)
                            link(dve.tensor_scalar(col(INV_SIM), col(IM), SCALE / LN_SCALE, None, ALU.mult))
                            link(dve.tensor_scalar(col(INV_OUT), col(IV), 1.0 / P_SCALE, None, ALU.mult))
                            net_scales(link, dve, amsr, b1r[:, :], b1s[:, :], (SW1, IW1, SW2, IW2, SH, IH, A1, A2))
                            link(dve.memset(amw[:, :], 0.0))
                            assert steps[0] == LINKS, steps[0]

                        dve.wait_ge(S["const_in"], 48)
                        dve.tensor_scalar(srcf[:, :], srcb[:, :], 0.0, None, ALU.is_equal).then_inc(S["src_neg"], 1)
                        dve.wait_ge(S["src_neg"], 1)

                        def body(g):
                            for u in range(N):
                                step(dve, g, u, -1, residual)
                                step(dve, g, u, 0, lo_p)
                                step(dve, g, u, 2, dropped)
                                if not first_tile(g, u, 4):
                                    step(dve, g, u, 4, stats)
                                    step(dve, g, u, 4, stats_done)
                                step(dve, g, u, -1, stats2_done)
                                step(dve, g, u, 1, sums)
                                if not first_tile(g, u, 4):
                                    step(dve, g, u, 4, aggregate)
                                step(dve, g, u, -1, aggregate2)
                                if first_tile(g, u, 2):
                                    other_scales()
                                step(dve, g, u, 2, masked)
                                if not first_tile(g, u, 4):
                                    step(dve, g, u, 4, normal)
                                step(dve, g, u, -1, gate)
                                step(dve, g, u, 2, largest_w)
                                if last_tile(g, u):
                                    snet.lo_z(dve, 0, 0)
                        groups(dve, SUB // N, body, peel_last=1)

        with ExitStack() as f:
            cacc = sb("cacc", [P, 2, DM], F32, f)
            inv = sb("inv", [P, SLOT_SUBS], F32, f)
            is1 = sb("is1", [P, SLOT_TILES], F32, f)
            is0 = sb("is0", [P, SLOT_TILES], F32, f)
            order = sb("order", [P, SLOT_SUBS], F32, f)
            eh = sb("s_eh", [P, 2, 2, DM], F16, f)
            el = sb("s_el", [P, 2, 2, DM], F16, f)
            iz = sb("e_iz", [P, Net.N, Net.R], I32, f)
            w0_in = f.enter_context(nc.semaphore("w0_in"))
            pH = [ps(f"pH{n}", [P, 512], f) for n in range(2)]
            pY = [[ps(f"pY{u}{r}", [P, DM], f) for r in range(Net.R)] for u in range(Net.N)]
            for net in (snet, enet):
                net.pH, net.pY = pH, pY
            enet.S["pick_z"] = f.enter_context(nc.semaphore("e_pick_z"))
            snet.S["e_out"] = f.enter_context(nc.semaphore("s_e_out"))
            room = (sb, ps, sc, wA, wB, cacc, order, inv, is1, is0, eh, el, iz, w0_in, snet, enet, stored, first_in)
            shared_net(nc, room, x1_d, z_d, res_d, (s1_d, s2_d), (e1_d, e2_d), units, w1, w2, sb2, net_scales,
                       (ones, upper, lane, row_id, starts, amw, b1e, b1e_s, b1s, expert1),
                       ((EW1, IEW1, EW2, IEW2, EH, IEH, EA1, EA2), AME, ARE))
            experts(nc, room, z_d, res_d, out, (e1_d, e2_d), b2, (ones, b1e_s))


class Net:

    N = 2
    R = TOK // P
    HR = 4
    LAG = 2

    def __init__(self, tag, count, sem, sc, ident, a1, a2, room, rows_room, banks, half=None):
        self.tiles, self.ident, self.half = count, ident, half
        self.a1, self.a2 = sc[:, a1:a1 + 1], sc[:, a2:a2 + 1]
        N, R, HR = self.N, self.R, self.HR
        S = self.S = {n: sem(f"{tag}_{n}") for n in ("zT", "zTh", "zTl", "h", "hh", "hl", "y", "o", "ob")}
        for n in ("z_in", "r_in", "out"):
            for u in range(N):
                S[n, u] = sem(f"{tag}_{n}{u}")
        self.zb = self.rows_buffer(rows_room)
        take = carve(room)
        self.zTh = take([N, KC, TOK], F16)
        self.zTl = take([N, KC, TOK], F16)
        self.rb = take([N, R, DM])
        self.ob = take([N, R, DM])
        self.hf = take([HR, TOK])
        self.hh = take([HR, TOK], F16)
        self.hl = take([HR, TOK], F16)
        self.pZ = banks[:, :].rearrange("p (r n) -> p r n", r=R)
        self.pH = self.pY = None

    @classmethod
    def rows_buffer(cls, room):
        return room[:, :, :].rearrange("p (u r) n -> p u r n", r=cls.R)

    @staticmethod
    def rows(t, tile):
        return t[bass.ds(tile * TOK, TOK), :].rearrange("(r p) n -> p r n", p=P)

    def tile(self, g, u):
        return self.N * g + u

    def parts(self, g, u):
        return 1 if isinstance(g, int) and self.tile(g, u) == self.half else self.R

    def step(self, eng, g, u, d, fn, *more):
        g2, u2 = shift(g, u, d, self.N)
        if live(g2, u2, self.N, self.tiles):
            fn(eng, g2, u2, *more)

    def t_z(self, q, g, u, z_count):
        t = self.tile(g, u)
        q.wait_ge(self.S["z_in", u], z_count * g + z_count * self.parts(g, u) // self.R)
        at_least(q, self.S["zTl"], t)
        for r in range(self.parts(g, u)):
            for k in range(KC):
                mm = q.transpose(self.pZ[:, r, k * P:(k + 1) * P], self.zb[:, u, r, k * P:(k + 1) * P], self.ident[:, :])
        mm.then_inc(self.S["zT"], 1)

    def first(self, q, g, u, j, weights):
        w1h, w1l = weights[0:2]
        rows = P * self.parts(g, u)
        if j == 0:
            q.wait_ge(self.S["zTl"], self.tile(g, u) + 1)
        at_least(q, self.S["hh"], HC * self.tile(g, u) + j - 1)
        n = 0
        for k in range(KC):
            for w, zt in ((w1h, self.zTh), (w1h, self.zTl), (w1l, self.zTh)):
                mm = q.matmul(self.pH[j % 2][:, 0:rows], w[:, k, j * P:(j + 1) * P], zt[:, u, k, 0:rows],
                              start=(n == 0), stop=(n == 3 * KC - 1))
                n += 1
        mm.then_inc(self.S["h"], 1)

    def second(self, q, g, u, j, weights):
        w2h, w2l = weights[2:4]
        if j == 0:
            at_least(q, self.S["o"], self.tile(g, u) - 1)
        q.wait_ge(self.S["hl"], HC * self.tile(g, u) + j + 1)
        for r in range(self.parts(g, u)):
            for n, (h, w) in enumerate(((self.hh, w2h), (self.hh, w2l), (self.hl, w2h))):
                mm = q.matmul(self.pY[u][r][:, :], h[:, j % self.HR, r * P:(r + 1) * P], w[:, j, :],
                              start=(j == 0 and n == 0), stop=(j == HC - 1 and n == 2))
        mm.then_inc(self.S["y"], 1)

    def hi_z(self, q, g, u):
        q.wait_ge(self.S["zT"], self.tile(g, u) + 1)
        at_least(q, self.S["h"], HC * (self.tile(g, u) - 1))
        for r in range(self.parts(g, u)):
            v = q.activation(self.zTh[:, u, :, r * P:(r + 1) * P], self.pZ[:, r, :].rearrange("p (k n) -> p k n", k=KC), ACT.Copy,
                             scale=LN_SCALE)
        v.then_inc(self.S["zTh"], 1)

    def relu(self, q, g, u, j, bias):
        done = HC * self.tile(g, u) + j
        b = bias(u, j)
        rows = P * self.parts(g, u)
        q.wait_ge(self.S["h"], done + 1)
        at_least(q, self.S["hl"], done + 1 - self.HR)
        q.activation(self.hf[:, j % self.HR, 0:rows], self.pH[j % 2][:, 0:rows], ACT.Relu, bias=b, scale=self.a1)
        at_least(q, self.S["y"], done + 1 - self.HR)
        q.activation(self.hh[:, j % self.HR, 0:rows], self.pH[j % 2][:, 0:rows], ACT.Relu, bias=b, scale=self.a1).then_inc(self.S["hh"], 1)

    def lo_z(self, q, g, u):
        q.wait_ge(self.S["zTh"], self.tile(g, u) + 1)
        for r in range(self.parts(g, u)):
            v = q.scalar_tensor_tensor(out=self.zTl[:, u, :, r * P:(r + 1) * P], in0=self.pZ[:, r, :].rearrange("p (k n) -> p k n", k=KC),
                                       scalar=LN_SCALE, in1=self.zTh[:, u, :, r * P:(r + 1) * P], op0=ALU.mult, op1=ALU.subtract)
        v.then_inc(self.S["zTl"], 1)

    def lo_h(self, q, g, u, j):
        q.wait_ge(self.S["hh"], HC * self.tile(g, u) + j + 1)
        rows = P * self.parts(g, u)
        q.tensor_tensor(self.hl[:, j % self.HR, 0:rows], self.hf[:, j % self.HR, 0:rows], self.hh[:, j % self.HR, 0:rows], ALU.subtract).then_inc(self.S["hl"], 1)

    def result(self, q, g, u, r_count, out_count):
        q.wait_ge(self.S["y"], HC * (self.tile(g, u) + 1))
        q.wait_ge(self.S["r_in", u], r_count * g + r_count * self.parts(g, u) // self.R)
        if not isinstance(g, int) or g > 0:
            q.wait_ge(self.S["out", u], out_count * g)
        for r in range(self.parts(g, u)):
            v = q.scalar_tensor_tensor(out=self.ob[:, u, r, :], in0=self.pY[u][r][:, :], scalar=self.a2, in1=self.rb[:, u, r, :],
                                       op0=ALU.mult, op1=ALU.add)
        v.then_inc(self.S["o"], 1)


def weight_set(room):
    return tuple(room[:, i, :].rearrange("p (k n) -> p k n", n=n) for i, n in enumerate((HID, HID, DM, DM)))


QUARTERS = 4


def load_quarter(q, dst, s1_d, s2_d, n, which, done):
    for i in range(2):
        if which == 1:
            c = slice(n * HID // QUARTERS, (n + 1) * HID // QUARTERS)
            q.dma_start(dst[i][:, :, c], s1_d[i].rearrange("(k p) n -> p k n", p=P)[:, :, c]).then_inc(done, 16)
        else:
            c = slice(n * HC // QUARTERS, (n + 1) * HC // QUARTERS)
            q.dma_start(dst[2 + i][:, c, :], s2_d[i].rearrange("(j p) n -> p j n", p=P)[:, c, :]).then_inc(done, 16)


def shared_net(nc, room, x1_d, z_d, res_d, split_s, split_e, units, w1, w2, sb2, net_scales, consts, cols):
    sb, ps, sc, wA, wB, cacc, order, inv, is1, is0, eh, el, iz, w0_in, net, enet, stored, first_in = room
    ones, upper, lane, row_id, starts, amw, b1e, b1e_s, b1s, expert1 = consts
    ECOLS, AME, ARE = cols
    EW1, EW2 = ECOLS[0], ECOLS[2]
    s1_d, s2_d = split_s
    e1_d, e2_d = split_e
    Q = QUARTERS
    with ExitStack() as f:
        N, S, step = net.N, net.S, net.step

        def sem(n):
            S[n] = f.enter_context(nc.semaphore("s_" + n))

        for n in ("brow_in", "e_am", "e_red", "e_step", "ranks", "sort", "onehot", "placed", "invadd", "ordered", "eh", "el", "cacc", "rb1"):
            sem(n)
        S["w1_in0"], S["w2_in0"] = first_in["w1_in0"], first_in["w2_in0"]
        for q in range(1, Q):
            sem(f"w1_in{q}")
            sem(f"w2_in{q}")
        for u in range(N):
            sem(f"e_in{u}")
        brow = sb("s_brow", [P, DM], F32, f)
        rb1 = sb("s_rb1", [P, 2 * HC], F32, f)
        er = sb("s_er", [P, N, 2, 2, DM], F32, f)
        place = sb("s_place", [P, 2, SUB], F32, f)
        work = sb("s_work", [P, 6, SUB], F32, f)
        worki = sb("s_worki", [P, 3, SUB], I32, f)
        hot = sb("s_hot", [P, 2, P], F32, f)
        half_at = sb("s_half_at", [P, SLOT_SUBS], F32, f)
        half_sub = sb("s_half_sub", [P, 1], F32, f)[:, :]
        late = sb("s_late", [P, TILES, 2], F32, f)
        hota = sb("s_hota", [P, 2, SLOT_SUBS], F32, f)
        pI = net.pZ
        pR = pI[:, 1, 0:2 * SUB]
        pV = pI[:, 1, 0:SLOT_SUBS]
        EXP_STEPS = 18
        BF = 12
        TZ = 11

        def first_tile(g, u, d):
            return isinstance(g, int) and N * g + u + d == 0

        def last_tile(g, u):
            return isinstance(g, int) and N * g + u == TILES - 1

        def past(g, u):
            return isinstance(g, int) and N * g + u == TILES

        def rows(t, g, u):
            return net.rows(t, N * g + u)

        with nc.Block() as block:
            @block.sync
            def _(sp):
                sp.dma_start(net.zb[:, 1, :, :], rows(z_d, 0, 1)).then_inc(S["z_in", 1], 16)
                for q in range(1, Q):
                    load_quarter(sp, wA, s1_d, s2_d, q, 1, S[f"w1_in{q}"])
                    load_quarter(sp, wA, s1_d, s2_d, q, 2, S[f"w2_in{q}"])
                    if q == 1:
                        sp.dma_start(brow[:, :], sb2.partition_broadcast(P)).then_inc(S["brow_in"], 16)
                for u in range(2):
                    sp.wait_ge(stored["x1_out", u], 16 * SUB // 2)
                    sp.wait_ge(stored["z_out", u], 16 * SUB // 2)

                def load_z(q, g, u):
                    q.wait_ge(S["zT"], net.tile(g, u) - 1)
                    q.dma_start(net.zb[:, u, :, :], rows(z_d, g, u)).then_inc(S["z_in", u], 16)

                def load_r(q, g, u):
                    at_least(q, S["o"], net.tile(g, u) - 1)
                    q.dma_start(net.rb[:, u, :, :], rows(x1_d, g, u)).then_inc(S["r_in", u], 16)

                def store(q, g, u):
                    wait_apart(q, S["ob"], net.tile(g, u) + 1)
                    q.dma_start(rows(res_d, g, u), net.ob[:, u, :, :]).then_inc(S["out", u], 16)

                def load_e(q, g, u):
                    wait_apart(q, S["el"], 2 * (net.tile(g, u) - 1))
                    for i, w in enumerate((w1, w2)):
                        q.dma_start(er[:, u, i, :, :], rows(units(w), g, u)).then_inc(S[f"e_in{u}"], 16)

                def store_e(q, g, u):
                    wait_apart(q, S["el"], 2 * net.tile(g, u) + 2)
                    for i, d in enumerate((e1_d, e2_d)):
                        q.dma_start(rows(units(d[0]), g, u), eh[:, i, :, :]).then_inc(S["e_out"], 16)
                        q.dma_start(rows(units(d[1]), g, u), el[:, i, :, :]).then_inc(S["e_out"], 16)

                def body(g):
                    if isinstance(g, int) and g == TILES // N - 1:
                        load_set(nc, sp, wB, e1_d, e2_d, 0, w0_in)
                    for u in range(N):
                        if not isinstance(g, int) or g >= 0:
                            step(sp, g, u, 2, load_z)
                        step(sp, g, u, 1, load_r)
                        step(sp, g, u, 1, load_e)
                        step(sp, g, u, -1, store)
                        step(sp, g, u, 0, store_e)
                groups(sp, TILES // N, body)

            @block.gpsimd
            def _(pool):
                pool.memset(cacc[:, :, :], 0.0).then_inc(S["cacc"], 1)
                pool.memset(inv[:, :], 0.0).then_inc(S["invadd"], 1)
                pool.wait_ge(S["e_am"], 1)
                pool.partition_all_reduce(sc[:, ARE:ARE + 3], sc[:, AME:AME + 3], P, RMAX).then_inc(S["e_red"], 1)
                pool.wait_ge(S["brow_in"], 16)

                def bias(q, g, u):
                    q.wait_ge(S["o"], net.tile(g, u) + 1)
                    for r in range(net.R):
                        v = q.tensor_tensor(net.ob[:, u, r, :], net.ob[:, u, r, :], brow[:, :], ALU.add)
                    v.then_inc(S["ob"], 1)

                def body(g):
                    for u in range(N):
                        step(pool, g, u, -1, bias)
                        if last_tile(g, u):
                            gather(pool, enet, enet.zb, z_d, iz, 0, 0, enet.S["pick_z"], "z_in")
                groups(pool, TILES // N, body)

            @block.tensor
            def _(pe):
                def place_rows(q, g, u):
                    t = net.tile(g, u)
                    q.wait_ge(S["onehot"], t + 1)
                    q.wait_ge(S["invadd"], t + 1)
                    if not isinstance(g, int) or t + 2 <= TILES:
                        q.wait_ge(S["zTl"], t + 2)
                    for r in range(2):
                        mm = q.matmul(pV, hot[:, r, :], hota[:, r, :], start=(r == 0), stop=(r == 1))
                    mm.then_inc(S["placed"], 1)

                def first(q, g, u, j):
                    if isinstance(g, int) and g == 0 and u == 0 and j % (HC // Q) == 0:
                        q.wait_ge(S[f"w1_in{j * Q // HC}"], 32)
                    net.first(q, g, u, j, wA)

                def second(q, g, u, j):
                    if isinstance(g, int) and g == 0 and u == 0 and j % (HC // Q) == 0:
                        q.wait_ge(S[f"w2_in{j * Q // HC}"], 32)
                    net.second(q, g, u, j, wA)

                def t_z(q, g, u):
                    if isinstance(g, int) and g == 1 and u == 0:
                        q.wait_ge(S["sort"], 2)
                    at_least(q, S["invadd"], net.tile(g, u))
                    net.t_z(q, g, u, 16)

                def body(g):
                    for u in range(N):
                        for j in range(HC):
                            step(pe, g, u, 0, first, j)
                            if j >= net.LAG:
                                step(pe, g, u, 0, second, j - net.LAG)
                            else:
                                step(pe, g, u, -1, second, j - net.LAG + HC)
                            if j == 8:
                                if not past(g, u):
                                    step(pe, g, u, -1, place_rows)
                            if j == TZ:
                                if not first_tile(g, u, 1):
                                    step(pe, g, u, 1, t_z)
                            if j == 12 and last_tile(g, u):
                                step(pe, g, u, 0, place_rows)
                            if j == 12 and isinstance(g, int) and g == 0 and u == 0:
                                pe.wait_ge(S["zTl"], 2)
                                pe.matmul(pR[:, 0:SUB], upper[:, :], expert1[:, :], start=True, stop=True)
                                pe.matmul(pR[:, SUB:2 * SUB], ones[:, :], expert1[:, :], start=True, stop=True).then_inc(S["ranks"], 1)
                groups(pe, TILES // N, body)
                pe.wait_ge(S["invadd"], TILES + 1)
                enet.t_z(pe, 0, 0, 32)

            @block.scalar
            def _(act):
                def split_hi(q, g, u, i):
                    t = net.tile(g, u)
                    q.wait_ge(S[f"e_in{u}"], 32 * (g + 1))
                    if not isinstance(g, int) or t > 0:
                        q.wait_ge(S["e_out"], 64 * t)
                    q.activation(eh[:, i, :, :], er[:, u, i, :, :], ACT.Copy, scale=sc[:, (EW1, EW2)[i]:(EW1, EW2)[i] + 1]).then_inc(S["eh"], 1)

                def body(g):
                    for u in range(N):
                        for j in range(HC):
                            step(act, g, u, 0, net.relu, j, lambda u, j: b1s[:, j:j + 1])
                            if j == TZ:
                                if not first_tile(g, u, 1):
                                    step(act, g, u, 1, net.hi_z)
                            if j in (BF, BF + 2):
                                if isinstance(g, int) and g == 0 and u == 0 and j == BF:
                                    act.wait_ge(S["e_step"], EXP_STEPS)
                                step(act, g, u, 0, split_hi, (j - BF) // 2)
                groups(act, TILES // N, body)
                enet.hi_z(act, 0, 0)

            def linker(dve, sem):
                steps = [0]

                def link(ins):
                    steps[0] += 1
                    ins.then_inc(sem, 1)
                    dve.wait_ge(sem, steps[0])
                return link, steps

            @block.vector
            def _(dve):
                def expert_scales():
                    dve.wait_ge(S["e_red"], 1)
                    link, steps = linker(dve, S["e_step"])
                    net_scales(link, dve, sc[:, ARE:ARE + 3], b1e[:, :], b1e_s[:, :, :].rearrange("p e j -> p (e j)"), ECOLS)
                    assert steps[0] == EXP_STEPS, steps[0]

                def slots():
                    link, _ = linker(dve, S["sort"])
                    dve.wait_ge(S["ranks"], 1)
                    before, total, run, other, slot = (work[:, n, :] for n in range(5))
                    link(dve.tensor_copy(before, pR[:, 0:SUB]))
                    link(dve.tensor_copy(total, pR[:, SUB:2 * SUB]))
                    link(dve.tensor_copy(run, total))
                    d = 1
                    while d < SUB:
                        link(dve.tensor_copy(other[:, 0:d], run[:, 0:d]))
                        link(dve.tensor_tensor(other[:, d:SUB], run[:, d:SUB], run[:, 0:SUB - d], ALU.add))
                        run, other = other, run
                        d *= 2
                    count1, e0_tiles = run[:, SUB - 1:SUB], work[:, 5, 0:1]
                    link(dve.tensor_scalar(is1[:, 0:HALF], starts[:, 0:HALF], count1, float(ROWS), ALU.add, ALU.is_ge))
                    link(dve.tensor_scalar(is0[:, 0:HALF], is1[:, 0:HALF], -1.0, 1.0, ALU.mult, ALU.add))
                    link(dve.tensor_reduce(e0_tiles, is0[:, 0:HALF], AX.X, ALU.add))
                    link(dve.tensor_scalar(starts[:, HALF:HALF + 1], e0_tiles, float(TOK), None, ALU.mult))
                    link(dve.tensor_scalar(is1[:, HALF:HALF + 1], starts[:, HALF:HALF + 1], count1, float(ROWS), ALU.add, ALU.is_ge))
                    link(dve.tensor_scalar(is0[:, HALF:HALF + 1], is1[:, HALF:HALF + 1], -1.0, 1.0, ALU.mult, ALU.add))
                    link(dve.tensor_scalar(half_sub, e0_tiles, 2.0, None, ALU.mult))
                    link(dve.tensor_scalar(half_at[:, :], lane[:, 0:SLOT_SUBS], half_sub, None, ALU.is_equal))
                    link(dve.tensor_tensor(other, run, total, ALU.subtract))
                    link(dve.tensor_tensor(before, before, other, ALU.add))
                    link(dve.tensor_scalar(slot, before, -1.0, float(SLOTS - 1), ALU.mult, ALU.add))
                    link(dve.tensor_tensor(other, row_id[:, :], before, ALU.subtract))
                    link(dve.tensor_scalar(other, other, float(ROWS), None, ALU.add))
                    link(dve.tensor_tensor(slot, slot, other, ALU.subtract))
                    link(dve.tensor_tensor(slot, slot, expert1[:, :], ALU.mult))
                    link(dve.tensor_tensor(slot, slot, other, ALU.add))
                    link(dve.tensor_copy(worki[:, 0, :], slot))
                    link(dve.tensor_scalar(worki[:, 1, :], worki[:, 0, :], P - 1, None, ALU.bitwise_and))
                    link(dve.tensor_scalar(worki[:, 2, :], worki[:, 0, :], 7, None, ALU.logical_shift_right))
                    link(dve.tensor_copy(place[:, 0, :], worki[:, 1, :]))
                    link(dve.tensor_copy(place[:, 1, :], worki[:, 2, :]))

                def one_hot(q, g, u):
                    t = net.tile(g, u)
                    at_least(q, S["placed"], t)
                    for r in range(2):
                        c = bass.ds(t * 2 + r, 1)
                        q.tensor_scalar(hot[:, r, :], lane[:, :], place[:, 0, c], None, ALU.is_equal)
                        v = q.tensor_scalar(hota[:, r, :], lane[:, 0:SLOT_SUBS], place[:, 1, c], row_id[:, c], ALU.is_equal, ALU.mult)
                    v.then_inc(S["onehot"], 1)

                def add_placed(q, g, u):
                    q.wait_ge(S["placed"], net.tile(g, u) + 1)
                    q.tensor_tensor(inv[:, :], pV, inv[:, :], ALU.add).then_inc(S["invadd"], 1)

                def by_tiles():
                    dve.wait_ge(S["invadd"], TILES + 1)
                    link, steps = linker(dve, S["ordered"])

                    def pairs(v):
                        return v.rearrange("p (t r) -> p t r", r=2)

                    def each(v):
                        return v[:, 0:HALF].unsqueeze(2).broadcast_to([P, TILES, 2])

                    front = pairs(order[:, 0:2 * TILES])
                    link(dve.tensor_tensor(front, pairs(inv[:, 0:2 * TILES]), each(is0), ALU.mult))
                    link(dve.tensor_tensor(late[:, :, :], pairs(inv[:, 1:2 * TILES + 1]), each(is1), ALU.mult))
                    link(dve.tensor_tensor(front, front, late[:, :, :], ALU.add))
                    link(dve.tensor_tensor(half_at[:, :], half_at[:, :], inv[:, :], ALU.mult))
                    link(dve.tensor_reduce(order[:, 2 * HALF:2 * HALF + 1], half_at[:, :], AX.X, ALU.add))

                def split_lo(q, g, u, i):
                    t = net.tile(g, u)
                    q.wait_ge(S["eh"], 2 * t + i + 1)
                    q.scalar_tensor_tensor(out=el[:, i, :, :], in0=er[:, u, i, :, :], scalar=sc[:, (EW1, EW2)[i]:(EW1, EW2)[i] + 1],
                                           in1=eh[:, i, :, :], op0=ALU.mult, op1=ALU.subtract).then_inc(S["el"], 1)

                def idle_expert(q, g, u):
                    t = net.tile(g, u)
                    for c in range(2):
                        q.wait_ge(S["cacc"], 2 * t + c + 1)
                        e = bass.ds(t // (TILES // 2), 1)
                        v = cacc[:, e, :].rearrange("p e n -> p (e n)")
                        q.scalar_tensor_tensor(out=v, in0=er[:, u, 1, c, :], scalar=rb1[:, bass.ds(2 * t + c, 1)], in1=v,
                                               op0=ALU.mult, op1=ALU.add).then_inc(S["cacc"], 1)

                def body(g):
                    for u in range(N):
                        for j in range(HC):
                            step(dve, g, u, 0, net.lo_h, j)
                            if j == 3:
                                step(dve, g, u, -1, net.result, 16, 16)
                            if j == 4 and isinstance(g, int) and g == 0 and u == 0:
                                expert_scales()
                            if j == 3 and isinstance(g, int) and g == 0 and u == 1:
                                slots()
                            if j == 6:
                                if not past(g, u):
                                    step(dve, g, u, -1, one_hot)
                            if j == 9:
                                if not past(g, u):
                                    step(dve, g, u, -1, add_placed)
                                if last_tile(g, u):
                                    step(dve, g, u, 0, one_hot)
                            if j == TZ:
                                if not first_tile(g, u, 1):
                                    step(dve, g, u, 1, net.lo_z)
                            if j == BF + 1 and last_tile(g, u):
                                step(dve, g, u, 0, add_placed)
                                by_tiles()
                                pick_rows(dve, enet, iz, order, 0, 0, enet.S["pick_z"])
                            if j in (BF, BF + 2):
                                step(dve, g, u, 0, split_lo, (j - BF) // 2)
                            if j == BF + 1:
                                step(dve, g, u, 0, idle_expert)
                dve.tensor_copy(sc[:, AME:AME + 2], amw[:, 0:2])
                dve.tensor_scalar(rb1[:, :], b1e[:, :], 0.0, None, ALU.max).then_inc(S["rb1"], 1)
                dve.tensor_reduce(sc[:, AME + 2:AME + 3], b1e[:, :], AX.X, ALU.max, apply_absolute_value=True).then_inc(S["e_am"], 1)
                dve.wait_ge(S["rb1"], 1)
                groups(dve, TILES // N, body)
                enet.lo_z(dve, 0, 0)


def load_set(nc, q, dst, e1_d, e2_d, e, done):
    for i in range(2):
        q.dma_start(dst[i][:, :, :], e1_d[i, e].rearrange("(k p) n -> p k n", p=P)).then_inc(done, 16)
        q.dma_start(dst[2 + i][:, :, :], e2_d[i, e].rearrange("(j p) n -> p j n", p=P)).then_inc(done, 16)


def pick_rows(q, net, dst, order, g, u, done):
    n = net.parts(g, u)
    q.tensor_scalar(dst[:, u, 0:n], order[:, bass.ds(net.tile(g, u) * net.R, n)], float(ROWS), None, ALU.add).then_inc(done, 1)


def gather(q, net, dst, src, rows, g, u, picked, arrived):
    wait_apart(q, picked, net.tile(g, u) + 1)
    for r in range(net.parts(g, u)):
        q.indirect_dma_start(dst[:, u, r, :], None, src, bass.IndirectOffsetOnAxis(ap=rows[:, u, r:r + 1], axis=0),
                             bounds_check=ROWS - 1, oob_is_err=False).then_inc(net.S[arrived, u], 16)


def experts(nc, room, z_d, res_d, out, split_e, b2, consts):
    sb, ps, sc, wA, wB, cacc, order, inv, is1, is0, eh, el, iz, w0_in, snet, net, _, _ = room
    ones, b1e_s = consts
    e1_d, e2_d = split_e
    with ExitStack() as f:
        N, S, step, R = net.N, net.S, net.step, net.R
        for n in ("w1_in", "b2_in", "flags", "idle", "idle_row", "pick_r", "pick_o", "bias", "sel0", "sel", "b2s", "bias0"):
            S[n] = f.enter_context(nc.semaphore("e_" + n))
        b2r = sb("e_b2r", [P, 2, DM], F32, f)
        flags = sb("e_flags", [P, SLOT_TILES], I32, f)
        ir = sb("e_ir", [P, N, R], I32, f)
        io = sb("e_io", [P, N, R], I32, f)
        idle = sb("e_idle", [P, 2, DM], F32, f)
        sel = sb("e_sel", [P, N, DM], F32, f)
        bsel = sb("e_bsel", [P, N, HC], F32, f)

        def first_tile(g, u, d):
            return isinstance(g, int) and N * g + u + d == 0

        with nc.Block() as block:
            @block.sync
            def _(sp):
                sp.dma_start(b2r[:, :, :].rearrange("p e n -> p (e n)"), b2.rearrange("e n -> (e n)").partition_broadcast(P)).then_inc(S["b2_in"], 16)
                sp.wait_ge(snet.S["e_out"], 64 * TILES)
                load_set(nc, sp, wA, e1_d, e2_d, 1, S["w1_in"])

            @block.gpsimd
            def _(pool):
                def gather_z(q, g, u):
                    gather(q, net, net.zb, z_d, iz, g, u, S["pick_z"], "z_in")

                def gather_r(q, g, u):
                    gather(q, net, net.rb, res_d, ir, g, u, S["pick_r"], "r_in")

                def add_idle(q, g, u):
                    q.wait_ge(S["sel"], net.tile(g, u) + 1)
                    q.wait_ge(S["o"], net.tile(g, u) + 1)
                    for r in range(net.parts(g, u)):
                        v = q.tensor_tensor(net.ob[:, u, r, :], net.ob[:, u, r, :], sel[:, u, :], ALU.add)
                    v.then_inc(S["ob"], 1)

                def scatter(q, g, u):
                    wait_apart(q, S["ob"], net.tile(g, u) + 1)
                    for r in range(net.parts(g, u)):
                        q.indirect_dma_start(out, bass.IndirectOffsetOnAxis(ap=io[:, u, r:r + 1], axis=0), net.ob[:, u, r, :], None,
                                             bounds_check=ROWS - 1, oob_is_err=False).then_inc(S["out", u], 16)

                def body(g):
                    for u in range(N):
                        if not first_tile(g, u, 1):
                            step(pool, g, u, 1, gather_z)
                        step(pool, g, u, -1, add_idle)
                        step(pool, g, u, -1, scatter)
                        step(pool, g, u, 1, gather_r)
                for u in range(N):
                    pool.wait_ge(snet.S["out", u], 16 * TILES // N)
                groups(pool, TILES // N + 1, body, peel_last=2)
                pool.wait_ge(S["out", 0], 32 * (TILES // N) + 16)
                pool.wait_ge(S["out", 1], 32 * (TILES // N))

            @block.tensor
            def _(pe):
                def tile(q, g, u, weights, loaded):
                    q.wait_ge(loaded, 64)
                    for j in range(HC + net.LAG):
                        if j < HC:
                            net.first(q, g, u, j, weights)
                        else:
                            if j == HC:
                                step(q, g, u, 1, net.t_z, 32)
                        if j >= net.LAG:
                            net.second(q, g, u, j - net.LAG, weights)

                def by_expert(q, g, u):
                    e = q.value_load(flags[0:1, bass.ds(net.tile(g, u), 1)], min_val=0, max_val=1)
                    with q.If(e == 0):
                        tile(q, g, u, wB, w0_in)
                    with q.Else():
                        tile(q, g, u, wA, S["w1_in"])

                def body(g):
                    for u in range(N):
                        if isinstance(g, int) and g == 0 and u == 1:
                            pe.wait_ge(S["idle_row"], 2)
                        step(pe, g, u, 0, by_expert)

                for e in range(2):
                    pe.matmul(net.pY[1][e][:, :], ones[:, :], cacc[:, 1 - e, :], start=True, stop=True).then_inc(S["idle"], 1)
                pe.wait_ge(S["flags"], 1)
                groups(pe, TILES // N + 1, body, peel_last=2)

            @block.scalar
            def _(act):
                def body(g):
                    for u in range(N):
                        for j in range(HC):
                            if j == 0:
                                step(act, g, u, 0, lambda q, g, u: q.wait_ge(S["bias"], net.tile(g, u) + 1))
                            step(act, g, u, 0, net.relu, j, lambda u, j: bsel[:, u, j:j + 1])
                        if not first_tile(g, u, 1):
                            step(act, g, u, 1, net.hi_z)
                groups(act, TILES // N + 1, body, peel_last=2)

            @block.vector
            def _(dve):
                def pick(dst, done, free):
                    def fn(q, g, u):
                        free(q, g, u)
                        pick_rows(q, net, dst, order, g, u, done)
                    return fn

                def out_before(q, g, u):
                    if not isinstance(g, int) or g > 0:
                        q.wait_ge(S["out", u], 32 * g)

                pick_z = pick(iz, S["pick_z"], lambda q, g, u: at_least(q, S["zT"], net.tile(g, u) - 1))
                pick_r = pick(ir, S["pick_r"], lambda q, g, u: at_least(q, S["o"], net.tile(g, u) - 1))
                pick_o = pick(io, S["pick_o"], out_before)

                def pick_bias(q, g, u):
                    at_least(q, S["hh"], HC * (net.tile(g, u) - 1))
                    t = bass.ds(net.tile(g, u), 1)
                    q.tensor_scalar(bsel[:, u, :], b1e_s[:, 0, :], is0[:, t], None, ALU.mult).then_inc(S["bias0"], 1)
                    q.wait_ge(S["bias0"], net.tile(g, u) + 1)
                    q.scalar_tensor_tensor(out=bsel[:, u, :], in0=b1e_s[:, 1, :], scalar=is1[:, t], in1=bsel[:, u, :],
                                           op0=ALU.mult, op1=ALU.add).then_inc(S["bias"], 1)

                def pick_idle(q, g, u):
                    at_least(q, S["ob"], net.tile(g, u) - 1)
                    t = bass.ds(net.tile(g, u), 1)
                    q.tensor_scalar(sel[:, u, :], idle[:, 0, :], is0[:, t], None, ALU.mult).then_inc(S["sel0"], 1)
                    q.wait_ge(S["sel0"], net.tile(g, u) + 1)
                    q.scalar_tensor_tensor(out=sel[:, u, :], in0=idle[:, 1, :], scalar=is1[:, t], in1=sel[:, u, :],
                                           op0=ALU.mult, op1=ALU.add).then_inc(S["sel"], 1)

                def idle_rows():
                    dve.wait_ge(S["b2_in"], 16)
                    dve.tensor_tensor(b2r[:, 0, :], b2r[:, 0, :], b2r[:, 1, :], ALU.add).then_inc(S["b2s"], 1)
                    dve.wait_ge(S["b2s"], 1)
                    dve.wait_ge(S["idle"], 2)
                    for e in range(2):
                        dve.tensor_tensor(idle[:, e, :], net.pY[1][e][:, :], b2r[:, 0, :], ALU.add).then_inc(S["idle_row"], 1)
                    dve.wait_ge(S["idle_row"], 2)

                def body(g):
                    for u in range(N):
                        if not first_tile(g, u, 1):
                            step(dve, g, u, 1, pick_z)
                        step(dve, g, u, 0, pick_o)
                        for j in range(HC):
                            step(dve, g, u, 0, net.lo_h, j)
                            if j == 3:
                                if first_tile(g, u, -1):
                                    for v in range(N):
                                        dve.wait_ge(snet.S["out", v], 16 * TILES // N)
                                step(dve, g, u, -1, net.result, 32, 32)
                                step(dve, g, u, 1, pick_r)
                            if j == 5 and isinstance(g, int) and g == 0 and u == 0:
                                idle_rows()
                            if j == 6:
                                step(dve, g, u, 1, pick_bias)
                            if j == 8:
                                step(dve, g, u, 0, pick_idle)
                        if not first_tile(g, u, 1):
                            step(dve, g, u, 1, net.lo_z)

                dve.tensor_copy(flags[:, :], is1[:, :]).then_inc(S["flags"], 1)
                groups(dve, TILES // N + 1, body, peel_last=2)


def kernel(**inputs):
    import numpy as np
    import concourse.bacc as bacc
    from concourse.bass_utils import run_bass_kernel_spmd

    nc = bacc.Bacc("TRN2", target_bir_lowering=False, num_devices=1)
    a = {k: np.asarray(v) for k, v in inputs.items()}
    laid = {
        "x": a["x"].reshape(ROWS, DM),
        "ctxT": a["ctx_1024"].reshape(BATCH * KEYS, DM).T,
        "tgt": a["mask_Bx1xSxS2_ik0"].reshape(ROWS, KEYS),
        "src": a["mask_Bx1xS2_bk0"].reshape(BATCH * KEYS),
        "wq": a["L0_xattn_Wq"], "wkT": a["L0_xattn_Wk"].T, "wvT": a["L0_xattn_Wv"].T, "woT": a["L0_xattn_Wo"].T,
        "bo": a["L0_xattn_bo"], "gate_w": a["L0_ffn_gate_w"], "w1": a["L0_ffn_w1"], "b1": a["L0_ffn_b1"],
        "w2": a["L0_ffn_w2"], "b2": a["L0_ffn_b2"], "sw1": a["L0_ffn_sw1"], "sb1": a["L0_ffn_sb1"],
        "sw2": a["L0_ffn_sw2"], "sb2": a["L0_ffn_sb2"],
    }
    arrays, args = {}, {}
    for name, v in laid.items():
        v = np.ascontiguousarray(v)
        arrays[f"in_{name}"] = v
        args[name] = nc.dram_tensor(f"in_{name}", v.shape, mybir.dt.from_np(v.dtype), kind="ExternalInput").ap()
    out = nc.dram_tensor("out_0", (ROWS, DM), F32, kind="ExternalOutput").ap()
    xattn_ffn(nc, out=out, **args)
    r = run_bass_kernel_spmd(nc, [arrays], core_ids=[0])
    return r.results[0]["out_0"].reshape(BATCH, SEQ, DM)
```
